# Optimizing a Trainium2 kernel written in Bass

```python
import numpy as np
import jax
import jax.numpy as jnp

def _softmax(x, axis=-1):
    return jax.nn.softmax(x, axis=axis)
def _gelu(x):
    return jax.nn.gelu(x, approximate=True)
def _silu(x):
    return jax.nn.silu(x)
def _sigmoid(x):
    return jax.nn.sigmoid(x)
def _layernorm(x, axis=-1, eps=1e-5):
    m = jnp.mean(x, axis=axis, keepdims=True)
    v = jnp.var(x, axis=axis, keepdims=True)
    return (x - m) / jnp.sqrt(v + eps)
def _scatter_add(tgt, idx, src, axis=0):
    return tgt.at[idx].add(src)
def _segment_sum(src, seg, n):
    return jax.ops.segment_sum(src, seg, n)

kernel_name = 'mk_metaformer_d1_conv_nhwc128_d2052d'

def setup_inputs(seed: int = 0):
    np.random.seed(seed)
    _w = jnp.asarray
    def _rec_inputs():
        import jax
        import jax.numpy as jnp
        _gk = jax.random.key(seed)
        x = -0.0003482 + 1 * jax.random.normal(jax.random.fold_in(_gk, 1), (1, 384, 384, 128), jnp.float32)
        return x
    x = _rec_inputs()
    def _L0_conv_setup():
        import jax, jax.numpy as jnp
        import numpy as np
        EPS = 1e-05

        def layer_norm(x, a, b):
            m = jnp.mean(x, axis=-1, keepdims=True)
            v = jnp.var(x, axis=-1, keepdims=True)
            return a * (x - m) / jnp.sqrt(v + EPS) + b
        key = jax.random.key(seed)
        ks = jax.random.split(key, 16)
        b, n, d, h = (1, 384, 128, 128)
        s = 1.0 / np.sqrt(d)
        inp = {'x': jax.random.normal(ks[0], (b, n, n, d), dtype=jnp.float32), 'norm_a': jnp.ones((d,), jnp.float32), 'norm_b': jnp.zeros((d,), jnp.float32), 'Wl': jax.random.normal(ks[1], (d, h), jnp.float32) * s, 'bl': jnp.zeros((h,), jnp.float32), 'Wr': jax.random.normal(ks[2], (d, h), jnp.float32) * s, 'br': jnp.zeros((h,), jnp.float32), 'Wlg': jax.random.normal(ks[3], (d, h), jnp.float32) * s, 'blg': jnp.ones((h,), jnp.float32), 'Wrg': jax.random.normal(ks[4], (d, h), jnp.float32) * s, 'brg': jnp.ones((h,), jnp.float32), 'Wog': jax.random.normal(ks[5], (d, h), jnp.float32) * s, 'bog': jnp.ones((h,), jnp.float32), 'on_a': jnp.ones((h,), jnp.float32), 'on_b': jnp.zeros((h,), jnp.float32), 'Wo': jax.random.normal(ks[6], (h, d), jnp.float32) * s, 'bo': jnp.zeros((d,), jnp.float32)}
        return inp
    _L0_conv_all = _L0_conv_setup()
    _L0_conv_in = {k: v for k, v in _L0_conv_all.items() if k in ('norm_a', 'norm_b', 'Wl', 'bl', 'Wr', 'br', 'Wlg', 'blg', 'Wrg', 'brg', 'Wog', 'bog', 'on_a', 'on_b', 'Wo', 'bo', )}
    del _L0_conv_all

    def _L0_ffn_setup():
        import jax, jax.numpy as jnp
        import numpy as np
        B, S, D, E, H, O, K = (512, 2048, 128, 64, 512, 128, 8)
        key = jax.random.key(seed)
        k0, k1, k2, k3 = jax.random.split(key, 4)
        x = jax.random.normal(k0, (B, S, D), dtype=jnp.float32)
        gate_w = jax.random.normal(k1, (E, D), dtype=jnp.float32) * (1.0 / np.sqrt(D))
        gate_b = jnp.zeros((E,), dtype=jnp.float32)
        weight1 = jax.random.uniform(k2, (E, D + 1, H), dtype=jnp.float32, minval=-1.0, maxval=1.0) * (1.0 / np.sqrt(D + 1))
        weight2 = jax.random.uniform(k3, (E, H + 1, O), dtype=jnp.float32, minval=-1.0, maxval=1.0) * (1.0 / np.sqrt(H + 1))
        return {'x': x, 'gate_w': gate_w, 'gate_b': gate_b, 'weight1': weight1, 'weight2': weight2}
    _L0_ffn_all = _L0_ffn_setup()
    _L0_ffn_in = {k: v for k, v in _L0_ffn_all.items() if k in ('gate_w', 'gate_b', 'weight1', 'weight2', )}
    del _L0_ffn_all

    return {
        "x": x,
        "L0_conv_norm_a": _L0_conv_in["norm_a"],
        "L0_conv_norm_b": _L0_conv_in["norm_b"],
        "L0_conv_Wl": _L0_conv_in["Wl"],
        "L0_conv_bl": _L0_conv_in["bl"],
        "L0_conv_Wr": _L0_conv_in["Wr"],
        "L0_conv_br": _L0_conv_in["br"],
        "L0_conv_Wlg": _L0_conv_in["Wlg"],
        "L0_conv_blg": _L0_conv_in["blg"],
        "L0_conv_Wrg": _L0_conv_in["Wrg"],
        "L0_conv_brg": _L0_conv_in["brg"],
        "L0_conv_Wog": _L0_conv_in["Wog"],
        "L0_conv_bog": _L0_conv_in["bog"],
        "L0_conv_on_a": _L0_conv_in["on_a"],
        "L0_conv_on_b": _L0_conv_in["on_b"],
        "L0_conv_Wo": _L0_conv_in["Wo"],
        "L0_conv_bo": _L0_conv_in["bo"],
        "L0_ffn_gate_w": _L0_ffn_in["gate_w"],
        "L0_ffn_gate_b": _L0_ffn_in["gate_b"],
        "L0_ffn_weight1": _L0_ffn_in["weight1"],
        "L0_ffn_weight2": _L0_ffn_in["weight2"],
    }

def reference(x, L0_conv_norm_a, L0_conv_norm_b, L0_conv_Wl, L0_conv_bl, L0_conv_Wr, L0_conv_br, L0_conv_Wlg, L0_conv_blg, L0_conv_Wrg, L0_conv_brg, L0_conv_Wog, L0_conv_bog, L0_conv_on_a, L0_conv_on_b, L0_conv_Wo, L0_conv_bo, L0_ffn_gate_w, L0_ffn_gate_b, L0_ffn_weight1, L0_ffn_weight2):
    import jax
    import jax.numpy as jnp
    def _L0_conv_ref(x, norm_a, norm_b, Wl, bl, Wr, br, Wlg, blg, Wrg, brg, Wog, bog, on_a, on_b, Wo, bo):
        import jax, jax.numpy as jnp
        import numpy as np
        EPS = 1e-05

        def layer_norm(x, a, b):
            m = jnp.mean(x, axis=-1, keepdims=True)
            v = jnp.var(x, axis=-1, keepdims=True)
            return a * (x - m) / jnp.sqrt(v + EPS) + b
        n = x.shape[1]
        xn = layer_norm(x, norm_a, norm_b)
        left = (xn @ Wl + bl) * jax.nn.sigmoid(xn @ Wlg + blg)
        right = (xn @ Wr + br) * jax.nn.sigmoid(xn @ Wrg + brg)
        out_gate = jax.nn.sigmoid(xn @ Wog + bog)
        out = jnp.einsum('bkjd,bkid->bijd', left.astype(jnp.float32), right.astype(jnp.float32)) / n
        out = out.astype(x.dtype)
        out = layer_norm(out, on_a, on_b) * out_gate
        return out @ Wo + bo

    def _L0_ffn_ref(x, gate_w, gate_b, weight1, weight2):
        import jax, jax.numpy as jnp
        import numpy as np
        B, S, D, E, H, O, K = (512, 2048, 128, 64, 512, 128, 8)
        Bn, Sn, Dn = x.shape
        logits = jnp.einsum('bsd,ed->bse', x, gate_w) + gate_b
        probs = jax.nn.softmax(logits, axis=1)
        vals, idx = jax.lax.top_k(probs.transpose(0, 2, 1), K)
        topv = vals.transpose(0, 2, 1)
        topi = idx.transpose(0, 2, 1)
        flat_idx = topi.reshape(Bn, K * E)
        gathered = jnp.take_along_axis(x, flat_idx[:, :, None], axis=1)
        gathered = gathered.reshape(Bn, K, E, Dn)
        pooled = jnp.einsum('bked,bke->bed', gathered, topv)
        ones = jnp.ones((E, Bn, 1), dtype=x.dtype)
        h = jnp.concatenate([pooled.transpose(1, 0, 2), ones], axis=-1)
        h = jax.nn.gelu(jnp.einsum('ebd,edh->ebh', h, weight1), approximate=False)
        h = jnp.concatenate([h, ones], axis=-1)
        out = jnp.einsum('ebh,eho->ebo', h, weight2)
        out = out.transpose(1, 0, 2)
        weighted = jnp.einsum('beo,bke->bkeo', out, topv).reshape(Bn, K * E, O)
        outputs = jnp.zeros((Bn, Sn, O), dtype=x.dtype)
        outputs = outputs.at[jnp.arange(Bn)[:, None], flat_idx].add(weighted)
        return outputs

    def _gn(v, G=32, eps=1e-5):
        B_, H_, W_, C_ = v.shape
        g = v.reshape(B_, H_, W_, G, C_ // G)
        m = jnp.mean(g, axis=(1, 2, 4), keepdims=True)
        s = jnp.var(g, axis=(1, 2, 4), keepdims=True)
        return ((g - m) / jnp.sqrt(s + eps)).reshape(v.shape)

    def _ln_c(v, eps=1e-6):
        m = jnp.mean(v, axis=-1, keepdims=True)
        s = jnp.var(v, axis=-1, keepdims=True)
        return (v - m) / jnp.sqrt(s + eps)

    def _ln_t(v, eps=1e-5):
        m = jnp.mean(v, axis=-1, keepdims=True)
        s = jnp.var(v, axis=-1, keepdims=True)
        return (v - m) / jnp.sqrt(s + eps)

    def _to_tokens(v):
        B_, H_, W_, C_ = v.shape
        return v.reshape(B_, H_ * W_, C_)
    def _from_tokens(t, like):
        return t.reshape(like.shape)

    x = x + _L0_conv_ref(_ln_c(x), L0_conv_norm_a, L0_conv_norm_b, L0_conv_Wl, L0_conv_bl, L0_conv_Wr, L0_conv_br, L0_conv_Wlg, L0_conv_blg, L0_conv_Wrg, L0_conv_brg, L0_conv_Wog, L0_conv_bog, L0_conv_on_a, L0_conv_on_b, L0_conv_Wo, L0_conv_bo)
    t = _to_tokens(x)
    t = t + _L0_ffn_ref(_ln_t(t), L0_ffn_gate_w, L0_ffn_gate_b, L0_ffn_weight1, L0_ffn_weight2)
    x = _from_tokens(t, x)
    return x


_drawn_inputs = setup_inputs


def setup_inputs(seed=0):
    import zlib

    import numpy as np

    out = dict(_drawn_inputs(seed))
    spreads = {'L0_conv_norm_a': (1.0, 0.2),
     'L0_conv_norm_b': (0.0, 0.1),
     'L0_conv_bl': (0.0, 0.1),
     'L0_conv_br': (0.0, 0.1),
     'L0_conv_blg': (1.0, 0.2),
     'L0_conv_brg': (1.0, 0.58),
     'L0_conv_bog': (1.0, 0.559),
     'L0_conv_on_a': (1.0, 0.2),
     'L0_conv_on_b': (0.0, 0.1),
     'L0_conv_bo': (0.0, 0.1),
     'L0_ffn_gate_b': (0.0, 0.1)}
    factors = {'L0_ffn_gate_w': 8.0, 'L0_ffn_weight1': 8.0, 'L0_ffn_weight2': 8.0}
    for name, (base, spread) in spreads.items():
        noise = np.random.default_rng([zlib.crc32(name.encode()), seed]).standard_normal(out[name].shape)
        drawn = base * np.exp(spread * noise) if base else spread * noise
        out[name] = jnp.asarray(drawn.astype(out[name].dtype))
    for name, factor in factors.items():
        out[name] = (out[name] * factor).astype(out[name].dtype)
    return out
```

```python
from contextlib import ExitStack

import numpy as np

import concourse.bass as bass
from concourse import mybir

FP32 = mybir.dt.float32
BF16 = mybir.dt.bfloat16
U32 = mybir.dt.uint32
I32 = mybir.dt.int32
ALU = mybir.AluOpType
ACT = mybir.ActivationFunctionType
AXX = mybir.AxisListType.X

P = 128
CHUNK = 512
TILES = CHUNK // P
TOP = 8
PARTS = 3
EPS_CONV_IN = 1e-6
EPS = 1e-5


def shifted(i, b, k):
    return i + (b + k) // 2, (b + k) % 2


def in_range(i, b, k, steps):
    return not isinstance(i, int) or 0 <= 2 * i + b + k < steps


def mark(per_step, step, k):
    return per_step * (step + 2) + k


def chunk_mark(per_chunk, chunk, k):
    return per_chunk * (chunk + 4) + k


def settle(engine, tick):
    engine.sem_inc(tick, 1)


def pairs(engine, steps, body, drain=0, cuts=()):
    first, last = 2, steps // 2 - 2
    for i in range(first):
        body(i)
    edges = [first + (last - first) * n // (len(cuts) + 1) for n in range(len(cuts) + 2)]
    for n in range(len(cuts) + 1):
        if edges[n] < edges[n + 1]:
            with engine.Fori(edges[n], edges[n + 1]) as i:
                body(i)
        if n < len(cuts):
            cuts[n]()
    for i in range(last, steps // 2 + drain):
        body(i)


def build(nc, x, norm_a, norm_b, Wl, bl, Wr, br, Wlg, blg, Wrg, brg, Wog, bog, on_a, on_b, Wo, bo,
          gate_w, gate_b, weight1, weight2, out):
    GRID, DIM = x.shape[1], x.shape[3]
    EXPERTS, _, HIDDEN = weight1.shape
    TOKENS = GRID * GRID
    NT = GRID // P
    STEPS = TOKENS // (2 * CHUNK)
    HALF = TOKENS // 2
    HC = HIDDEN // P
    PICKS = TOP * EXPERTS
    GROUPS = PICKS // P
    WGROUP = 8
    WLOADS = EXPERTS // WGROUP
    KR = 2 * PARTS * PARTS

    x_tok = x.rearrange("b i j d -> (b i j) d")
    out_tok = out.rearrange("b i j d -> (b i j) d")
    left_d = nc.dram_tensor("left_d", (DIM, TOKENS), FP32, kind="Internal").ap()
    right_d = nc.dram_tensor("right_d", (DIM, TOKENS), FP32, kind="Internal").ap()
    gate_d = nc.dram_tensor("gate_d", (DIM, TOKENS), FP32, kind="Internal").ap()
    mixed_d = nc.dram_tensor("mixed_d", (DIM, TOKENS), FP32, kind="Internal").ap()
    stat_d = nc.dram_tensor("stat_d", (2 * PARTS, TOKENS), BF16, kind="Internal").ap()
    picks_d = nc.dram_tensor("picks_d", (TOP, EXPERTS), FP32, kind="Internal").ap()

    with ExitStack() as ctx:
        def sb(name, shape, dt=FP32):
            return ctx.enter_context(nc.sbuf_tensor(name, shape, dt))

        def sem(name):
            return ctx.enter_context(nc.semaphore(name))

        W1_WORDS = EXPERTS * HIDDEN
        arena = sb("arena", [P, W1_WORDS])
        used = [0]

        def carve(pattern, **dims):
            size = int(np.prod(list(dims.values())))
            view = arena[:, used[0]:used[0] + size].rearrange(f"p ({pattern}) -> p {pattern}", **dims)
            used[0] += size
            return view

        xin = carve("b t d", b=2, t=2 * TILES, d=DIM)
        xhat = carve("b t d", b=2, t=2 * TILES, d=DIM)
        xn = carve("b n", b=2, n=CHUNK)
        sig_l = carve("b n", b=2, n=CHUNK)
        sig_r = carve("b n", b=2, n=CHUNK)
        left_sb = carve("b n", b=2, n=2 * CHUNK)
        right_sb = carve("b n", b=2, n=2 * CHUNK)
        gate_sb = carve("b n", b=2, n=2 * CHUNK)
        lch = carve("b t n", b=2, t=NT, n=GRID)
        rch = carve("b t n", b=2, t=NT, n=GRID)
        mix = carve("b t n", b=2, t=NT, n=GRID)
        mixsq = carve("b t n", b=2, t=NT, n=GRID)
        wcat = carve("k d", k=5, d=DIM)
        newton = carve("t n", t=NT, n=GRID)
        sum1 = carve("t n", t=NT, n=GRID)
        sum2 = carve("t n", t=NT, n=GRID)
        rstd_map = carve("t n", t=NT, n=GRID)
        halves = used[0]
        used[0] += PARTS * NT * GRID
        split = arena[:, halves:used[0]].bitcast(BF16).rearrange("p (q t n) -> p q t n", q=2 * PARTS, t=NT)
        assert used[0] <= W1_WORDS
        w1_sb = arena[:, :].rearrange("p (e n) -> p e n", e=EXPERTS)
        w2_in_w1 = arena[:, :].rearrange("p (e c n) -> p e c n", e=EXPERTS, c=HC)

        work = sb("work", [P, 2 * WGROUP * HIDDEN])
        tail_used = [WGROUP * HIDDEN]

        def tail(size):
            tail_used[0] += size
            assert tail_used[0] <= 2 * WGROUP * HIDDEN
            return work[:, tail_used[0] - size:tail_used[0]]

        wv = work[:, :].rearrange("p (k b h n) -> p k b h n", k=4, b=2, h=2)
        ot, gt = wv[:, 0], wv[:, 1]
        xs = wv[:, 2].rearrange("p b h (c d) -> p b h c d", c=TILES)
        ys = wv[:, 3].rearrange("p b h (c d) -> p b h c d", c=TILES)
        w2_in_work = work[:, 0:WGROUP * HIDDEN].rearrange("p (e c n) -> p e c n", e=WGROUP, c=HC)
        yt = sb("yt", [P, 2, 2, CHUNK])
        expo = sb("expo", [P, CHUNK])
        statrow = sb("statrow", [P, 2, 2, CHUNK], BF16)

        CANDS = STEPS * TOP
        late = sb("late", [P, 4 * CANDS + max(CANDS, PICKS)])
        rstd_tok = late[:, 0:CANDS]
        cand = late[:, CANDS:2 * CANDS].rearrange("p (s k) -> p s k", k=TOP)
        cidx = late[:, 2 * CANDS:3 * CANDS].rearrange("p (s k) -> p s k", k=TOP)
        place = late[:, 3 * CANDS:4 * CANDS]
        base = late[:, 4 * CANDS:5 * CANDS].rearrange("p (s k) -> p s k", k=TOP)
        junk = late[:, 4 * CANDS:]
        csum = sb("csum", [P, STEPS])

        wo_sb = sb("wo_sb", [P, DIM])
        cols = sb("cols", [P, 9])
        A_COL, B_COL, BLG, BL, BRG, BR, BOG, ONA = range(8)
        ident = sb("ident", [P, P])
        gate_nat = sb("gate_nat", [EXPERTS, DIM])
        gate_t = sb("gate_t", [P, EXPERTS])
        exact = sb("exact", [2 * PARTS, 2, DIM])
        exact_lo = sb("exact_lo", [2 * PARTS, 2, DIM])
        exact_p = sb("exact_p", [2 * PARTS, PARTS, 2, DIM], BF16)
        coef = sb("coef", [P, 2, DIM], BF16)
        rowsign = sb("rowsign", [2 * PARTS, 2])

        bn = sb("bn", [P, 2, 2 * TILES, 6])
        mv = sb("mv", [P, 2, 2 * TILES, 2])
        vv = sb("vv", [P, 2, 2 * TILES])
        rs = sb("rs", [P, 2, 2 * TILES])
        nmr = sb("nmr", [P, 2, 2 * TILES])
        mhalf = sb("mhalf", [P, 2 * TILES])
        rcol = sb("rcol", [P, 2, 2, TILES])
        mx = sb("mx", [P, 2, TOP])
        ix = sb("ix", [P, 2, TOP], U32)
        negmax = sb("negmax", [P, 2, 1])
        esum = sb("esum", [P, 2, 1])

        half_off = sb("half_off", [P, 1])
        gb_col = sb("gb_col", [P, 1])
        pack = sb("pack", [P, 2 * TOP + 1])
        pack_hi = sb("pack_hi", [EXPERTS, 2 * TOP + 1])
        posu = sb("posu", [P, TOP], U32)
        posf = sb("posf", [P, TOP])
        wexp = sb("wexp", [P, STEPS])
        negm = sb("negm", [P, 1])
        both = sb("both", [EXPERTS, 2, 2 * TOP])
        best = sb("best", [EXPERTS, TOP])
        negbest = sb("negbest", [EXPERTS, 1])
        zscale = sb("zscale", [EXPERTS, 2])
        zsum = sb("zsum", [EXPERTS, 2])
        ztot = sb("ztot", [EXPERTS, 2])
        pick = sb("pick", [EXPERTS, 2, TOP])
        rowpick = sb("rowpick", [P, 2, GROUPS])
        allpick = tail(PICKS)
        earlier = tail(2 * PICKS - P)
        seen = sb("seen", [P, GROUPS])
        rowidx = sb("rowidx", [P, GROUPS], I32)
        scatidx = sb("scatidx", [P, GROUPS], I32)
        scatf = sb("scatf", [P, GROUPS])
        xg = tail(PICKS).rearrange("p (g d) -> p g d", g=GROUPS)
        yg = tail(PICKS).rearrange("p (g d) -> p g d", g=GROUPS)
        rw = sb("rw", [P, GROUPS])
        sel = sb("sel", [P, EXPERTS])
        pooled = sb("pooled", [P, EXPERTS])
        b1_nat = tail(HIDDEN)[0:EXPERTS, :]
        b2_nat = sb("b2_nat", [EXPERTS, DIM])
        b1_t = tail(HC * EXPERTS)
        b2_t = sb("b2_t", [P, EXPERTS])
        hid = tail(HC * EXPERTS)
        eo_t = sb("eo_t", [P, EXPERTS])
        eo = sb("eo", [EXPERTS, DIM])
        wt = tail(PICKS)[0:EXPERTS, :]
        wtk = expo[0:EXPERTS, :]

        ps = [ctx.enter_context(nc.psum_tensor(f"bank{n}", [P, CHUNK], FP32)) for n in range(8)]

        s_const = sem("s_const")
        s_coef = sem("s_coef")
        s_pool0 = sem("s_pool0")
        s_gtp = sem("s_gtp")
        s_setup = sem("s_setup")
        s_dve = sem("s_dve")

        s_tick_dve = sem("s_tick_dve")
        s_tick_pool = sem("s_tick_pool")

        s_xin = [sem(f"s_xin{b}") for b in range(2)]
        s_bn = sem("s_bn")
        s_ag = sem("s_ag")
        s_var = sem("s_var")
        s_rstd = sem("s_rstd")
        s_xhat = sem("s_xhat")
        s_xt = sem("s_xt")
        s_xn = sem("s_xn")
        s_proj = sem("s_proj")
        s_sig = sem("s_sig")
        s_prod = sem("s_prod")
        s_lst = [sem(f"s_lst{b}") for b in range(2)]
        s_rst = [sem(f"s_rst{b}") for b in range(2)]
        s_gst = [sem(f"s_gst{b}") for b in range(2)]

        s_ch = [sem(f"s_ch{b}") for b in range(2)]
        s_mix = sem("s_mix")
        s_ev = sem("s_ev")
        s_acc = sem("s_acc")
        s_mst = [sem(f"s_mst{b}") for b in range(2)]
        s_mom = sem("s_mom")
        s_sq = sem("s_sq")
        s_rmap = sem("s_rmap")
        s_split = sem("s_split")
        s_stst = sem("s_stst")
        s_rtp = sem("s_rtp")
        s_rtc = sem("s_rtc")

        s_oin = [sem(f"s_oin{b}") for b in range(2)]
        s_x3 = [sem(f"s_x3{b}") for b in range(2)]
        s_sin = [sem(f"s_sin{b}") for b in range(2)]
        s_rc = sem("s_rc")
        s_c3 = sem("s_c3")
        s_w3 = sem("s_w3")
        s_g3 = sem("s_g3")
        s_z3 = sem("s_z3")
        s_r3 = sem("s_r3")
        s_v3 = sem("s_v3")
        s_n3 = sem("s_n3")
        s_y3 = sem("s_y3")
        s_t3 = sem("s_t3")
        s_p3 = sem("s_p3")
        s_l3 = sem("s_l3")
        s_m3 = sem("s_m3")
        s_k3 = sem("s_k3")
        s_e3 = sem("s_e3")
        s_q3 = sem("s_q3")
        s_ost = [sem(f"s_ost{b}") for b in range(2)]

        s_w1 = sem("s_w1")
        s_w2 = [sem(f"s_w2{n}") for n in range(WLOADS)]
        s_b1 = sem("s_b1")
        s_pack = sem("s_pack")
        s_hi = sem("s_hi")
        s_nm = sem("s_nm")
        s_we = sem("s_we")
        s_pick = sem("s_pick")
        s_rows = sem("s_rows")
        s_pst = sem("s_pst")
        s_all = sem("s_all")
        s_ri = sem("s_ri")
        s_gat = sem("s_gat")
        s_gvar = sem("s_gvar")
        s_gr = sem("s_gr")
        s_yg = sem("s_yg")
        s_pool = sem("s_pool")
        s_pl = sem("s_pl")
        s_bt = sem("s_bt")
        s_h1 = sem("s_h1")
        s_pre = sem("s_pre")
        s_hid = sem("s_hid")
        s_h2 = sem("s_h2")
        s_eot = sem("s_eot")
        s_eop = sem("s_eop")
        s_eo = sem("s_eo")
        s_del = sem("s_del")
        s_new = sem("s_new")
        s_scat = sem("s_scat")

        def by_channel(t, h=None):
            return t.rearrange("c (s n) -> c s n", n=2 * CHUNK)

        left_w, right_w, gate_w_d = by_channel(left_d), by_channel(right_d), by_channel(gate_d)
        x_step = x_tok.rearrange("(s t p) d -> s p t d", t=2 * TILES, p=P)
        left_r = left_d.rearrange("c (t p j) -> c p t j", t=NT, p=P)
        right_r = right_d.rearrange("c (t p j) -> c p t j", t=NT, p=P)
        mixed_w = mixed_d.rearrange("c (t p j) -> c p t j", t=NT, p=P)
        stat_w = stat_d.rearrange("q (t p j) -> q p t j", t=NT, p=P)
        mixed_r = mixed_d.rearrange("c (h s n) -> s c h n", h=2, n=CHUNK)
        gate_r = gate_d.rearrange("c (h s n) -> s c h n", h=2, n=CHUNK)
        stat_r = stat_d.rearrange("q (h s n) -> s q h n", h=2, n=CHUNK)
        x_half = x_tok.rearrange("(h s t p) d -> h s p t d", h=2, t=TILES, p=P)
        out_half = out_tok.rearrange("(h s t p) d -> h s p t d", h=2, t=TILES, p=P)
        rstd_half = rstd_tok.rearrange("p (h t) -> p h t", h=2)
        N_CONST = 5 + 1 + 8 + 1 + 4 * PARTS - PARTS + 2 + 1

        block = ctx.enter_context(nc.Block())

        @block.sync
        def _(sp):
            for n, w in enumerate((Wlg, Wl, Wrg, Wr, Wog)):
                sp.dma_start(wcat[:, n, :], w).then_inc(s_const, 16)
            sp.dma_start(wo_sb[:, :], Wo).then_inc(s_const, 16)
            for n, v in enumerate((norm_a, norm_b, blg, bl, brg, br, bog, on_a)):
                sp.dma_start(cols[:, n:n + 1], v.rearrange("(p o) -> p o", o=1)).then_inc(s_const, 16)
            sp.dma_start(gate_nat[:, :], gate_w).then_inc(s_const, 16)
            sp.wait_ge(s_pool0, 6)
            for q in range(PARTS):
                sp.dma_start(exact[q:q + 1, 0, :], on_a.rearrange("(o d) -> o d", o=1)).then_inc(s_const, 16)
                sp.dma_start(exact[PARTS + q:PARTS + q + 1, 0, :], on_b.rearrange("(o d) -> o d", o=1)).then_inc(s_const, 16)
                sp.dma_start(exact[PARTS + q:PARTS + q + 1, 1, :], bo.rearrange("(o d) -> o d", o=1)).then_inc(s_const, 16)
            for h in range(2):
                sp.dma_start(gb_col[EXPERTS * h:EXPERTS * (h + 1), :], gate_b.rearrange("(p o) -> p o", o=1)).then_inc(s_const, 16)
            sp.dma_start(b2_nat[:, :], weight2[:, HIDDEN, :]).then_inc(s_const, 16)

            def load_x(i, b):
                sp.wait_ge(s_xhat, mark(1, 2 * i + b - 2, 1))
                sp.dma_start(xin[:, b], x_step[2 * i + b]).then_inc(s_xin[b], 16)

            def stage1(i):
                for b in range(2):
                    s = 2 * i + b
                    if in_range(i, b, 3, STEPS):
                        load_x(*shifted(i, b, 3))
                    sp.wait_ge(s_prod, mark(4, s, 3))
                    sp.dma_start(left_w[:, s, :], left_sb[:, b]).then_inc(s_lst[b], 16)
                    sp.wait_ge(s_prod, mark(4, s, 4))
                    sp.dma_start(right_w[:, s, :], right_sb[:, b]).then_inc(s_rst[b], 16)
                    sp.wait_ge(s_sig, mark(6, s, 6))
                    sp.dma_start(gate_w_d[:, s, :], gate_sb[:, b]).then_inc(s_gst[b], 16)

            load_x(0, 0)
            load_x(0, 1)
            load_x(1, 0)
            pairs(sp, STEPS, stage1)
            for b in range(2):
                sp.wait_ge(s_lst[b], 16 * (STEPS // 2))
                sp.wait_ge(s_rst[b], 16 * (STEPS // 2))

            def load_channel(i, b):
                sp.wait_ge(s_mix, mark(NT, 2 * i + b - 2, NT))
                sp.dma_start(lch[:, b], left_r[2 * i + b]).then_inc(s_ch[b], 16)
                sp.dma_start(rch[:, b], right_r[2 * i + b]).then_inc(s_ch[b], 16)

            def stage2(i):
                for b in range(2):
                    if in_range(i, b, 2, DIM):
                        load_channel(*shifted(i, b, 2))
                    sp.wait_ge(s_ev, mark(NT, 2 * i + b, NT))
                    sp.dma_start(mixed_w[2 * i + b], mix[:, b]).then_inc(s_mst[b], 16)

            load_channel(0, 0)
            load_channel(0, 1)
            pairs(sp, DIM, stage2)
            for b in range(2):
                sp.wait_ge(s_mst[b], 16 * (DIM // 2))
                sp.wait_ge(s_gst[b], 16 * (STEPS // 2))

            def load_mixed(i, b):
                s = 2 * i + b
                sp.wait_ge(s_z3, mark(2, s - 2, 2))
                sp.dma_start(ot[:, b], mixed_r[s]).then_inc(s_oin[b], 16)
                sp.dma_start(gt[:, b], gate_r[s]).then_inc(s_oin[b], 16)

            def load_parts(i, b):
                for a in range(PARTS):
                    sp.dma_start(statrow[2 * PARTS * a:2 * PARTS * (a + 1), b], stat_r[2 * i + b]).then_inc(s_sin[b], 16)

            def load_x3(i, b):
                s = 2 * i + b
                sp.wait_ge(s_ost[b], 32 * i)
                sp.wait_ge(s_y3, mark(2, s - 2, 2))
                for h in range(2):
                    sp.dma_start(xs[:, b, h], x_half[h, s]).then_inc(s_x3[b], 16)

            def stage3(i):
                for b in range(2):
                    s = 2 * i + b
                    if in_range(i, b, 1, STEPS):
                        load_x3(*shifted(i, b, 1))
                    if in_range(i, b, 2, STEPS):
                        load_mixed(*shifted(i, b, 2))
                        load_parts(*shifted(i, b, 2))
                    sp.wait_ge(s_r3, mark(2, s, 2))
                    for h in range(2):
                        sp.dma_start(out_half[h, s], xs[:, b, h]).then_inc(s_ost[b], 16)

            load_mixed(0, 0)
            load_mixed(0, 1)
            load_x3(0, 0)
            for half in range(2):
                sp.wait_ge(s_split, half + 1)
                for q in range(PARTS * half, PARTS * (half + 1)):
                    sp.dma_start(stat_w[q], split[:, q]).then_inc(s_stst, 16)
            sp.wait_ge(s_stst, 16 * 2 * PARTS)
            load_parts(0, 0)
            load_parts(0, 1)
            pairs(sp, STEPS, stage3)

            w2_view = weight2[:, 0:HIDDEN, :].rearrange("e (c p) n -> e p c n", p=P)

            def load_w2(n):
                for e in range(n * WGROUP, (n + 1) * WGROUP):
                    dst = w2_in_work[:, e] if n < 1 else w2_in_w1[:, e - WGROUP]
                    sp.dma_start(dst, w2_view[e]).then_inc(s_w2[n], 16)

            for b in range(2):
                sp.wait_ge(s_ost[b], 32 * (STEPS // 2))
            sp.wait_ge(s_t3, mark(2, STEPS - 1, 2))
            sp.dma_start(b1_nat, weight1[:, DIM, :]).then_inc(s_b1, 16)
            load_w2(0)
            sp.wait_ge(s_pack, 1)
            sp.dma_start(pack_hi[:, :], pack[EXPERTS:2 * EXPERTS, :]).then_inc(s_hi, 16)
            sp.wait_ge(s_pick, 1)
            for hh in range(2):
                for kind in range(2):
                    sp.dma_start(rowpick[EXPERTS * hh:EXPERTS * (hh + 1), kind, :],
                                 pick[:, kind, hh:TOP:2],
                                 allow_slow_non_contiguous=True).then_inc(s_rows, 16)
            sp.dma_start(picks_d.rearrange("k e -> e k"), pick[:, 0, :],
                         allow_slow_non_contiguous=True).then_inc(s_pst, 16)
            sp.wait_ge(s_pst, 16)
            sp.dma_start(allpick[:, :], picks_d.rearrange("(o k) e -> o (k e)", o=1).broadcast_to([P, PICKS])).then_inc(s_all, 16)
            for n in range(1, WLOADS):
                sp.wait_ge(s_h1, n)
                load_w2(n)

        @block.gpsimd
        def _(pool):
            made = [0]

            def alone(instruction):
                made[0] += 1
                instruction.then_inc(s_pool0, 1)
                pool.wait_ge(s_pool0, made[0])

            alone(nc.gpsimd.memset(ident[:, :], 0.0))
            alone(nc.gpsimd.memset(sel[:, :], 0.0))
            alone(nc.gpsimd.memset(mhalf[:, :], -0.5))
            alone(nc.gpsimd.memset(half_off[0:EXPERTS, :], 0.0))
            alone(nc.gpsimd.memset(half_off[EXPERTS:P, :], float(HALF)))
            alone(nc.gpsimd.memset(exact[:, 1, :], 0.0))
            alone(nc.gpsimd.memset(rowsign[:, :], 1.0))
            alone(nc.gpsimd.memset(statrow[:, :, :, :], 0.0))
            alone(nc.gpsimd.memset(coef[:, :, :], 0.0))
            alone(nc.gpsimd.affine_select(out=ident[:, :], in_=ident[:, :], compare_op=ALU.not_equal, fill=1.0,
                                          base=0, pattern=[[-1, P]], channel_multiplier=1))
            for shift in (0, EXPERTS):
                alone(nc.gpsimd.affine_select(out=sel[:, :], in_=sel[:, :], compare_op=ALU.not_equal, fill=1.0,
                                              base=-shift, pattern=[[-1, EXPERTS]], channel_multiplier=1))
            alone(nc.gpsimd.affine_select(out=rowsign[:, 0:1], in_=rowsign[:, 0:1], compare_op=ALU.is_ge, fill=-1.0,
                                          base=-PARTS, pattern=[[0, 1]], channel_multiplier=1))
            alone(nc.gpsimd.iota(place[:, :], pattern=[[1, STEPS * TOP]], base=0, channel_multiplier=0,
                                 allow_small_or_imprecise_dtypes=True))
            alone(nc.gpsimd.iota(base[:, :, :], pattern=[[CHUNK, STEPS], [0, TOP]], base=0, channel_multiplier=0,
                                 allow_small_or_imprecise_dtypes=True))

            pool.wait_ge(s_setup, 2)
            for a in range(PARTS):
                pool.dma_start(coef[2 * PARTS * a:2 * PARTS * (a + 1), :, :], exact_p[:, a]).then_inc(s_coef, 16)

            def stage1(i):
                for b in range(2):
                    pool.wait_ge(s_var, mark(1, 2 * i + b, 1))
                    nc.gpsimd.tensor_tensor(rs[:, b], vv[:, b], mhalf[:, 0:2 * TILES], ALU.pow).then_inc(s_rstd, 1)

            pairs(pool, STEPS, stage1)

            def columns(i, b):
                s = 2 * i + b
                pool.wait_ge(s_r3, mark(2, s - 2, 2))
                nc.gpsimd.tensor_copy(rcol[:, b], rstd_half[:, :, bass.ds(s * TILES, TILES)]).then_inc(s_rc, 1)

            def gate(i, b):
                for h in range(2):
                    pool.wait_ge(s_w3, mark(2, 2 * i + b, h + 1))
                    nc.gpsimd.tensor_tensor(ot[:, b, h], ot[:, b, h], gt[:, b, h], ALU.mult).then_inc(s_g3, 1)

            def negate_max(i, b):
                pool.wait_ge(s_e3, mark(1, 2 * i + b - 2, 1))
                pool.wait_ge(s_m3, mark(2, 2 * i + b, 1))
                settle(pool, s_tick_pool)
                nc.gpsimd.tensor_scalar(negmax[:, b], mx[:, b, 0:1], -1.0, 0.0, ALU.mult, ALU.add).then_inc(s_k3, 1)

            def keep(i, b):
                s = 2 * i + b
                pool.wait_ge(s_m3, mark(2, s, 2))
                nc.gpsimd.tensor_copy(cand[:, bass.ds(s, 1), :], mx[:, b:b + 1, :])
                nc.gpsimd.tensor_copy(cidx[:, bass.ds(s, 1), :], ix[:, b:b + 1, :]).then_inc(s_q3, 1)

            def keep_sum(i, b):
                s = 2 * i + b
                pool.wait_ge(s_e3, mark(1, s, 1))
                nc.gpsimd.tensor_copy(csum[:, bass.ds(s, 1)], esum[:, b]).then_inc(s_q3, 1)

            def scales(i, b):
                s = 2 * i + b
                pool.wait_ge(s_v3, mark(1, s, 1))
                pool.wait_ge(s_y3, mark(2, s - 2, 2))
                nc.gpsimd.tensor_tensor(rs[:, b], vv[:, b], mhalf[:, 0:2 * TILES], ALU.pow).then_inc(s_n3, 1)
                pool.wait_ge(s_n3, mark(3, s, 1))
                nc.gpsimd.tensor_tensor(nmr[:, b], mv[:, b, :, 0], rs[:, b], ALU.mult).then_inc(s_n3, 1)
                pool.wait_ge(s_n3, mark(3, s, 2))
                settle(pool, s_tick_pool)
                nc.gpsimd.tensor_scalar(nmr[:, b], nmr[:, b], -1.0, 0.0, ALU.mult, ALU.add).then_inc(s_n3, 1)

            def stage3(i):
                for b in range(2):
                    if in_range(i, b, 1, STEPS):
                        columns(*shifted(i, b, 1))
                        gate(*shifted(i, b, 1))
                    if in_range(i, b, -3, STEPS):
                        negate_max(*shifted(i, b, -3))
                        keep(*shifted(i, b, -3))
                    if in_range(i, b, 0, STEPS):
                        scales(i, b)
                    if in_range(i, b, -3, STEPS):
                        keep_sum(*shifted(i, b, -3))

            pool.wait_ge(s_rtc, NT * NT)
            columns(0, 0)
            gate(0, 0)
            pairs(pool, STEPS, stage3, drain=2)

            for b in range(2):
                pool.wait_ge(s_ost[b], 32 * (STEPS // 2))
            pool.wait_ge(s_t3, mark(2, STEPS - 1, 2))
            alone(nc.gpsimd.memset(earlier, 1.0))
            alone(nc.gpsimd.affine_select(out=earlier, in_=earlier, compare_op=ALU.is_gt, fill=0.0,
                                          base=PICKS - P, pattern=[[-1, 2 * PICKS - P]], channel_multiplier=1))
            pool.wait_ge(s_ri, 1)
            for g in range(GROUPS):
                pool.indirect_dma_start(xg[:, g, :], None, out_tok, bass.IndirectOffsetOnAxis(rowidx[:, g:g + 1], 0)).then_inc(s_gat, 16)
            pool.wait_ge(s_gvar, 1)
            nc.gpsimd.tensor_tensor(rs[:, 0, 0:GROUPS], vv[:, 0, 0:GROUPS], mhalf[:, 0:GROUPS], ALU.pow).then_inc(s_gr, 1)
            pool.wait_ge(s_new, GROUPS)
            for g in range(GROUPS):
                pool.indirect_dma_start(out_tok, bass.IndirectOffsetOnAxis(scatidx[:, g:g + 1], 0), yg[:, g, :], None,
                                        bounds_check=TOKENS - 1, oob_is_err=False).then_inc(s_scat, 16)
            pool.wait_ge(s_scat, 16 * GROUPS)

        @block.scalar
        def _(act):
            act.sem_inc(s_xn, 2 * 2)
            act.sem_inc(s_sig, 2 * 6)
            act.sem_inc(s_ev, 2 * NT)
            act.sem_inc(s_y3, 2 * 2)
            act.sem_inc(s_p3, 2 * 2)
            act.sem_inc(s_e3, 2)
            act.wait_ge(s_const, 16 * N_CONST)

            def scaled(i, b, c):
                n = 2 * (2 * i + b) + c
                act.wait_ge(s_xt, chunk_mark(1, n, 1))
                act.wait_ge(s_proj, chunk_mark(5, n - 2, 5))
                nc.scalar.activation(xn[:, c], ps[c][:, :], ACT.Identity, bias=cols[:, B_COL:B_COL + 1],
                                     scale=cols[:, A_COL:A_COL + 1]).then_inc(s_xn, 1)

            def stage1(i):
                for b in range(2):
                    for c in range(2):
                        s, n = 2 * i + b, 2 * (2 * i + b) + c
                        if c == 0:
                            scaled(i, b, 1)
                        elif in_range(i, b, 1, STEPS):
                            scaled(*shifted(i, b, 1), 0)
                        act.wait_ge(s_proj, chunk_mark(5, n, 1))
                        act.wait_ge(s_prod, chunk_mark(2, n - 2, 1))
                        nc.scalar.activation(sig_l[:, c], ps[2][:, :], ACT.Sigmoid, bias=cols[:, BLG:BLG + 1]).then_inc(s_sig, 1)
                        act.wait_ge(s_proj, chunk_mark(5, n, 3))
                        act.wait_ge(s_prod, chunk_mark(2, n - 2, 2))
                        nc.scalar.activation(sig_r[:, c], ps[4][:, :], ACT.Sigmoid, bias=cols[:, BRG:BRG + 1]).then_inc(s_sig, 1)
                        act.wait_ge(s_proj, chunk_mark(5, n, 5))
                        act.wait_ge(s_gst[b], 16 * i)
                        nc.scalar.activation(gate_sb[:, b, CHUNK * c:CHUNK * (c + 1)], ps[6][:, :], ACT.Sigmoid,
                                             bias=cols[:, BOG:BOG + 1]).then_inc(s_sig, 1)

            scaled(0, 0, 0)
            pairs(act, STEPS, stage1)

            def stage2(i):
                for b in range(2):
                    d = 2 * i + b
                    act.wait_ge(s_mst[b], 16 * i)
                    act.wait_ge(s_acc, mark(1, d - 2, 1))
                    for t in range(NT):
                        act.wait_ge(s_mix, mark(NT, d, t + 1))
                        nc.scalar.activation(mix[:, b, t], ps[NT * b + t][:, 0:GRID], ACT.Copy, scale=1.0 / GRID)
                        nc.scalar.activation(mixsq[:, b, t], ps[NT * b + t][:, 0:GRID], ACT.Square,
                                             scale=1.0 / GRID).then_inc(s_ev, 1)

            pairs(act, DIM, stage2)

            for t in range(NT):
                act.wait_ge(s_mom, t + 1)
                nc.scalar.activation(rstd_map[:, t], sum2[:, t], ACT.Sqrt).then_inc(s_sq, 1)
            rstd_grid = rstd_tok.rearrange("p (i c) -> p i c", c=NT)
            for t in range(NT):
                for c in range(NT):
                    n = t * NT + c
                    act.wait_ge(s_rtp, n + 1)
                    nc.scalar.copy(rstd_grid[:, t * P:(t + 1) * P, c], ps[n % 2][:, 0:P]).then_inc(s_rtc, 1)

            act.wait_ge(s_mix, mark(NT, DIM - 1, NT))
            act.wait_ge(s_acc, mark(1, DIM - 1, 1))
            act.wait_ge(s_stst, 16 * 2 * PARTS)
            act.wait_ge(s_rtp, NT * NT)
            for b in range(2):
                act.wait_ge(s_mst[b], 16 * (DIM // 2))
                act.wait_ge(s_gst[b], 16 * (STEPS // 2))
                act.wait_ge(s_lst[b], 16 * (STEPS // 2))
                act.wait_ge(s_rst[b], 16 * (STEPS // 2))
            for n in range(WLOADS):
                e = slice(n * WGROUP, (n + 1) * WGROUP)
                act.dma_start(w1_sb[:, e, :], weight1[e, 0:DIM, :].rearrange("e p n -> p e n")).then_inc(s_w1, 16)

            def exponentials(i, b):
                s = 2 * i + b
                act.wait_ge(s_m3, mark(2, s, 2))
                act.wait_ge(s_k3, mark(1, s, 1))
                act.wait_ge(s_q3, mark(2, s - 2, 2))
                nc.scalar.activation(expo[:, :], ps[6 + b][:, :], ACT.Exp, bias=negmax[:, b],
                                     accum_out=esum[:, b]).then_inc(s_e3, 1)

            def copy_transposed(i, b):
                s = 2 * i + b
                act.wait_ge(s_l3, mark(2, s - 2, 2))
                for h in range(2):
                    act.wait_ge(s_t3, mark(2, s, h + 1))
                    nc.scalar.copy(yt[:, b, h], ps[4 + h][:, :]).then_inc(s_p3, 1)

            def normalise(i, b):
                s = 2 * i + b
                act.wait_ge(s_n3, mark(3, s, 3))
                act.wait_ge(s_t3, mark(2, s - 2, 2))
                for h in range(2):
                    for c in range(TILES):
                        k = TILES * h + c
                        last = nc.scalar.activation(ys[:, b, h, c], xs[:, b, h, c], ACT.Identity,
                                                    bias=nmr[:, b, k:k + 1], scale=rs[:, b, k:k + 1])
                    last.then_inc(s_y3, 1)

            def stage3(i):
                for b in range(2):
                    if in_range(i, b, -2, STEPS):
                        copy_transposed(*shifted(i, b, -2))
                    if in_range(i, b, -3, STEPS):
                        exponentials(*shifted(i, b, -3))
                    if in_range(i, b, 0, STEPS):
                        normalise(i, b)

            pairs(act, STEPS, stage3, drain=2)

            act.wait_ge(s_nm, 1)
            nc.scalar.activation(wexp[:, :], cand[:, :, 0], ACT.Exp, bias=negm[:, :]).then_inc(s_we, 1)
            act.wait_ge(s_nm, 2)
            nc.scalar.activation(zscale[:, :], both[:, 0, 0:2 * TOP:TOP], ACT.Exp, bias=negbest[:, :]).then_inc(s_we, 1)
            nc.scalar.activation(pick[:, 1, :], best[:, :], ACT.Exp, bias=negbest[:, :]).then_inc(s_we, 1)
            act.wait_ge(s_pre, 1)
            nc.scalar.activation(hid[:, :], b1_t[:, :], ACT.Gelu).then_inc(s_hid, 1)

        @block.vector
        def _(dve):
            chain = [0]

            def link(instruction):
                chain[0] += 1
                instruction.then_inc(s_dve, 1)
                dve.wait_ge(s_dve, chain[0])

            for s_, n in ((s_bn, 1), (s_ag, 1), (s_var, 1), (s_xhat, 1), (s_prod, 4), (s_acc, 1),
                          (s_w3, 2), (s_r3, 2), (s_v3, 1), (s_m3, 2)):
                dve.sem_inc(s_, 2 * n)
            for s_, n in ((s_rstd, 1), (s_rc, 1), (s_g3, 2), (s_n3, 3), (s_k3, 1), (s_q3, 2)):
                dve.sem_inc(s_, 2 * n)

            dve.wait_ge(s_const, 16 * N_CONST)
            dve.wait_ge(s_pool0, 15)
            for q in range(2):
                link(nc.vector.tensor_scalar(exact[:, q, :], exact[:, q, :], rowsign[:, q:q + 1], None, ALU.mult))
            link(nc.vector.tensor_copy(exact_p[:, 0], exact[:, :, :]))
            link(nc.vector.tensor_tensor(exact_lo[:, :, :], exact[:, :, :], exact_p[:, 0], ALU.subtract))
            link(nc.vector.tensor_copy(exact_p[:, 1], exact_lo[:, :, :]))
            link(nc.vector.tensor_tensor(exact_lo[:, :, :], exact_lo[:, :, :], exact_p[:, 1], ALU.subtract))
            nc.vector.tensor_copy(exact_p[:, 2], exact_lo[:, :, :]).then_inc(s_setup, 1)
            dve.wait_ge(s_gtp, 1)
            nc.vector.tensor_copy(gate_t[:, :], ps[7][:, 0:EXPERTS]).then_inc(s_setup, 1)
            nc.vector.memset(sum1[:, :, :], 0.0)
            nc.vector.memset(sum2[:, :, :], 0.0)

            def statistics(i, b):
                s = 2 * i + b
                dve.wait_ge(s_xin[b], 16 * (i + 1))
                for t in range(2 * TILES):
                    last = nc.vector.bn_stats(bn[:, b, t], xin[:, b, t])
                last.then_inc(s_bn, 1)
                dve.wait_ge(s_bn, mark(1, s, 1))
                settle(dve, s_tick_dve)
                for t in range(2 * TILES):
                    last = nc.vector.bn_aggr(mv[:, b, t], bn[:, b, t])
                last.then_inc(s_ag, 1)
                dve.wait_ge(s_ag, mark(1, s, 1))
                nc.vector.tensor_scalar(vv[:, b], mv[:, b, :, 1], 1.0 + EPS, EPS_CONV_IN * EPS,
                                        ALU.mult, ALU.add).then_inc(s_var, 1)

            def centre(i, b):
                dve.wait_ge(s_rstd, mark(1, 2 * i + b, 1))
                dve.wait_ge(s_xt, mark(2, 2 * i + b - 2, 2))
                for t in range(2 * TILES):
                    last = nc.vector.tensor_scalar(xhat[:, b, t], xin[:, b, t], mv[:, b, t, 0:1],
                                                   rs[:, b, t:t + 1], ALU.subtract, ALU.mult)
                last.then_inc(s_xhat, 1)

            def product(i, b, c, side):
                n = 2 * (2 * i + b) + c
                stored, bank, col, sig, dst = ((s_lst, 3, BL, sig_l, left_sb), (s_rst, 5, BR, sig_r, right_sb))[side]
                dve.wait_ge(stored[b], 16 * i)
                dve.wait_ge(s_sig, chunk_mark(3, n, side + 1))
                dve.wait_ge(s_proj, chunk_mark(5, n, 2 * side + 2))
                nc.vector.scalar_tensor_tensor(out=dst[:, b, CHUNK * c:CHUNK * (c + 1)], in0=ps[bank][:, :],
                                               scalar=cols[:, col:col + 1], in1=sig[:, c], op0=ALU.add,
                                               op1=ALU.mult).then_inc(s_prod, 1)

            def stage1(i):
                for b in range(2):
                    if in_range(i, b, 1, STEPS):
                        centre(*shifted(i, b, 1))
                    product(i, b, 0, 0)
                    product(i, b, 0, 1)
                    if in_range(i, b, 2, STEPS):
                        statistics(*shifted(i, b, 2))
                    product(i, b, 1, 0)
                    product(i, b, 1, 1)

            statistics(0, 0)
            centre(0, 0)
            statistics(0, 1)
            pairs(dve, STEPS, stage1)

            def stage2(i):
                for b in range(2):
                    d = 2 * i + b
                    dve.wait_ge(s_ev, mark(NT, d, NT))
                    dve.wait_ge(s_acc, mark(1, d - 1, 1))
                    nc.vector.tensor_tensor(sum1[:, :, :], sum1[:, :, :], mix[:, b], ALU.add)
                    nc.vector.tensor_tensor(sum2[:, :, :], sum2[:, :, :], mixsq[:, b], ALU.add).then_inc(s_acc, 1)

            pairs(dve, DIM, stage2)

            dve.wait_ge(s_acc, mark(1, DIM - 1, 1))
            link(nc.vector.tensor_scalar(sum1[:, :, :], sum1[:, :, :], 1.0 / DIM, None, ALU.mult))
            link(nc.vector.tensor_tensor(newton, sum1, sum1, ALU.mult))
            link(nc.vector.scalar_tensor_tensor(out=sum2[:, :, :], in0=sum2[:, :, :], scalar=1.0 / DIM,
                                                in1=newton, op0=ALU.mult, op1=ALU.subtract))
            for t in range(NT):
                nc.vector.tensor_scalar(sum2[:, t], sum2[:, t], 0.0, EPS, ALU.max, ALU.add).then_inc(s_mom, 1)

            def split3(value, first):
                link(nc.vector.tensor_copy(split[:, first], value))
                link(nc.vector.tensor_tensor(value, value, split[:, first], ALU.subtract))
                link(nc.vector.tensor_copy(split[:, first + 1], value))
                link(nc.vector.tensor_tensor(value, value, split[:, first + 1], ALU.subtract))
                link(nc.vector.tensor_copy(split[:, first + 2], value))

            split3(sum1, 0)
            nc.vector.engine_nop().then_inc(s_split, 1)
            dve.wait_ge(s_sq, NT)
            link(nc.vector.reciprocal(rstd_map, rstd_map))
            link(nc.vector.tensor_tensor(newton, rstd_map, rstd_map, ALU.mult))
            link(nc.vector.tensor_tensor(newton, newton, sum2, ALU.mult))
            link(nc.vector.tensor_scalar(newton, newton, -0.5, 1.5, ALU.mult, ALU.add))
            nc.vector.tensor_tensor(rstd_map, rstd_map, newton, ALU.mult).then_inc(s_rmap, 1)
            dve.wait_ge(s_rmap, 1)
            link(nc.vector.tensor_tensor(sum2, sum2, rstd_map, ALU.mult))
            split3(sum2, PARTS)
            nc.vector.engine_nop().then_inc(s_split, 1)

            def weighted(i, b):
                for h in range(2):
                    dve.wait_ge(s_oin[b], 32 * (i + 1))
                    dve.wait_ge(s_c3, mark(2, 2 * i + b, h + 1))
                    nc.vector.scalar_tensor_tensor(out=ot[:, b, h], in0=ot[:, b, h], scalar=cols[:, ONA:ONA + 1],
                                                   in1=ps[h][:, :], op0=ALU.mult, op1=ALU.add).then_inc(s_w3, 1)

            def residual(i, b):
                s = 2 * i + b
                dve.wait_ge(s_rc, mark(1, s, 1))
                dve.wait_ge(s_x3[b], 32 * (i + 1))
                for h in range(2):
                    dve.wait_ge(s_z3, mark(2, s, h + 1))
                    for c in range(TILES):
                        last = nc.vector.scalar_tensor_tensor(out=xs[:, b, h, c], in0=ps[2 + h][:, c * P:(c + 1) * P],
                                                              scalar=rcol[:, b, h, c:c + 1], in1=xs[:, b, h, c],
                                                              op0=ALU.mult, op1=ALU.add)
                    last.then_inc(s_r3, 1)

            def statistics3(i, b):
                s = 2 * i + b
                for h in range(2):
                    dve.wait_ge(s_r3, mark(2, s, h + 1))
                    for c in range(TILES):
                        last = nc.vector.bn_stats(bn[:, b, TILES * h + c], xs[:, b, h, c])
                last.then_inc(s_bn, 1)

            def aggregate3(i, b):
                s = 2 * i + b
                dve.wait_ge(s_bn, mark(1, STEPS + s, 1))
                dve.wait_ge(s_n3, mark(3, s - 2, 3))
                settle(dve, s_tick_dve)
                for t in range(2 * TILES):
                    last = nc.vector.bn_aggr(mv[:, b, t], bn[:, b, t])
                last.then_inc(s_ag, 1)
                dve.wait_ge(s_ag, mark(1, STEPS + s, 1))
                nc.vector.tensor_scalar(vv[:, b], mv[:, b, :, 1], 1.0, EPS, ALU.mult, ALU.add).then_inc(s_v3, 1)

            def best_values(i, b):
                s = 2 * i + b
                dve.wait_ge(s_l3, mark(2, s, 2))
                dve.wait_ge(s_q3, mark(2, s - 2, 1))
                dve.wait_ge(s_k3, mark(1, s - 2, 1))
                settle(dve, s_tick_dve)
                nc.vector.max(mx[:, b], ps[6 + b][:, :]).then_inc(s_m3, 1)

            def best_places(i, b):
                s = 2 * i + b
                dve.wait_ge(s_m3, mark(2, s, 1))
                settle(dve, s_tick_dve)
                nc.vector.max_index(ix[:, b], mx[:, b], ps[6 + b][:, :]).then_inc(s_m3, 1)

            def stage3(i):
                for b in range(2):
                    if in_range(i, b, 1, STEPS):
                        weighted(*shifted(i, b, 1))
                    if in_range(i, b, 0, STEPS):
                        residual(i, b)
                    if in_range(i, b, -3, STEPS):
                        best_values(*shifted(i, b, -3))
                    if in_range(i, b, 0, STEPS):
                        statistics3(i, b)
                    if in_range(i, b, -3, STEPS):
                        best_places(*shifted(i, b, -3))
                    if in_range(i, b, 0, STEPS):
                        aggregate3(i, b)

            weighted(0, 0)
            pairs(dve, STEPS, stage3, drain=2)

            dve.wait_ge(s_q3, mark(2, STEPS - 1, 2))
            flat = "p s k -> p (s k)"
            link(nc.vector.scalar_tensor_tensor(out=cidx[:, :, :], in0=cidx[:, :, :], scalar=half_off[:, :],
                                                in1=base[:, :, :], op0=ALU.add, op1=ALU.add))
            link(nc.vector.tensor_scalar(cand[:, :, :], cand[:, :, :], gb_col[:, :], None, ALU.add))
            link(nc.vector.max(pack[:, 0:TOP], cand[:, :, :].rearrange(flat)))
            nc.vector.tensor_scalar(negm[:, :], pack[:, 0:1], -1.0, None, ALU.mult).then_inc(s_nm, 1)
            link(nc.vector.max_index(posu[:, :], pack[:, 0:TOP], cand[:, :, :].rearrange(flat)))
            link(nc.vector.tensor_copy(posf[:, :], posu[:, :]))
            for k in range(TOP):
                link(nc.vector.scalar_tensor_tensor(out=junk[:, 0:STEPS * TOP], in0=place[:, :], scalar=posf[:, k:k + 1],
                                                      in1=cidx[:, :, :].rearrange(flat), op0=ALU.is_equal, op1=ALU.mult,
                                                      accum_out=pack[:, TOP + k:TOP + k + 1]))
            dve.wait_ge(s_we, 1)
            nc.vector.scalar_tensor_tensor(out=junk[:, 0:STEPS], in0=wexp[:, :], scalar=1.0, in1=csum[:, :],
                                           op0=ALU.mult, op1=ALU.mult,
                                           accum_out=pack[:, 2 * TOP:2 * TOP + 1]).then_inc(s_pack, 1)
            dve.wait_ge(s_pack, 1)
            nc.vector.tensor_copy(both[:, :, 0:TOP], pack[0:EXPERTS, 0:2 * TOP].rearrange("p (q k) -> p q k", q=2))
            nc.vector.tensor_copy(zsum[:, 0:1], pack[0:EXPERTS, 2 * TOP:2 * TOP + 1])
            dve.wait_ge(s_hi, 16)
            nc.vector.tensor_copy(both[:, :, TOP:2 * TOP], pack_hi[:, 0:2 * TOP].rearrange("p (q k) -> p q k", q=2))
            link(nc.vector.tensor_copy(zsum[:, 1:2], pack_hi[:, 2 * TOP:2 * TOP + 1]))
            link(nc.vector.max(best[:, :], both[:, 0, :]))
            nc.vector.tensor_scalar(negbest[:, :], best[:, 0:1], -1.0, None, ALU.mult).then_inc(s_nm, 1)
            link(nc.vector.max_index(posu[0:EXPERTS, :], best[:, :], both[:, 0, :]))
            link(nc.vector.tensor_copy(posf[0:EXPERTS, :], posu[0:EXPERTS, :]))
            for k in range(TOP):
                link(nc.vector.scalar_tensor_tensor(out=junk[0:EXPERTS, 0:2 * TOP], in0=place[0:EXPERTS, 0:2 * TOP],
                                                      scalar=posf[0:EXPERTS, k:k + 1], in1=both[:, 1, :],
                                                      op0=ALU.is_equal, op1=ALU.mult, accum_out=pick[:, 0, k:k + 1]))
            dve.wait_ge(s_we, 3)
            link(nc.vector.scalar_tensor_tensor(out=ztot[:, :], in0=zscale[:, :], scalar=1.0, in1=zsum[:, :],
                                                op0=ALU.mult, op1=ALU.mult, accum_out=negbest[:, :]))
            link(nc.vector.reciprocal(ztot[:, 0:1], negbest[:, :]))
            nc.vector.tensor_scalar(pick[:, 1, :], pick[:, 1, :], ztot[:, 0:1], None, ALU.mult).then_inc(s_pick, 1)
            dve.wait_ge(s_rows, 64)
            nc.vector.tensor_copy(rowidx[:, :], rowpick[:, 0, :]).then_inc(s_ri, 1)
            dve.wait_ge(s_all, 16)
            dve.wait_ge(s_pool0, 17)
            for g in range(GROUPS):
                at = PICKS - P - g * P
                link(nc.vector.scalar_tensor_tensor(out=junk[:, 0:PICKS], in0=allpick[:, :], scalar=rowpick[:, 0, g:g + 1],
                                                      in1=earlier[:, at:at + PICKS], op0=ALU.is_equal, op1=ALU.mult,
                                                      accum_out=seen[:, g:g + 1]))
            link(nc.vector.scalar_tensor_tensor(out=scatf[:, :], in0=seen[:, :], scalar=float(TOKENS),
                                                in1=rowpick[:, 0, :], op0=ALU.mult, op1=ALU.add))
            nc.vector.tensor_copy(scatidx[:, :], scatf[:, :])
            dve.wait_ge(s_pick, 1)
            for k in range(TOP):
                dst = wt if k == 0 else wtk
                link(nc.vector.tensor_scalar(dst[:, :], allpick[0:EXPERTS, :], pick[:, 0, k:k + 1], pick[:, 1, k:k + 1],
                                             ALU.is_equal, ALU.mult))
                if k:
                    link(nc.vector.tensor_tensor(wt[:, :], wt[:, :], wtk[:, :], ALU.add))
            dve.wait_ge(s_gat, 16 * GROUPS)
            for g in range(GROUPS):
                last = nc.vector.bn_stats(bn[:, 0, g], xg[:, g])
            link(last)
            for g in range(GROUPS):
                last = nc.vector.bn_aggr(mv[:, 0, g], bn[:, 0, g])
            link(last)
            nc.vector.tensor_scalar(vv[:, 0, 0:GROUPS], mv[:, 0, 0:GROUPS, 1], 1.0, EPS, ALU.mult, ALU.add).then_inc(s_gvar, 1)
            dve.wait_ge(s_gr, 1)
            link(nc.vector.tensor_tensor(rw[:, :], rs[:, 0, 0:GROUPS], rowpick[:, 1, :], ALU.mult))
            for g in range(GROUPS):
                last = nc.vector.tensor_scalar(yg[:, g], xg[:, g], mv[:, 0, g, 0:1], rw[:, g:g + 1], ALU.subtract, ALU.mult)
            last.then_inc(s_yg, 1)
            dve.wait_ge(s_pool, 1)
            nc.vector.tensor_copy(pooled[:, :], ps[0][:, 0:EXPERTS]).then_inc(s_pl, 1)
            dve.wait_ge(s_bt, 1)
            nc.vector.tensor_copy(b2_t[:, :], ps[1][:, HC * EXPERTS:(HC + 1) * EXPERTS])
            link(nc.vector.tensor_copy(b1_t[:, :], ps[1][:, 0:HC * EXPERTS]))
            dve.wait_ge(s_h1, WLOADS)
            nc.vector.tensor_tensor(b1_t[:, :], b1_t[:, :], ps[2][:, 0:HC * EXPERTS], ALU.add).then_inc(s_pre, 1)
            dve.wait_ge(s_h2, 1)
            nc.vector.tensor_tensor(eo_t[:, :], b2_t[:, :], ps[3][:, 0:EXPERTS], ALU.add).then_inc(s_eot, 1)
            dve.wait_ge(s_eop, 1)
            nc.vector.tensor_copy(eo[:, :], ps[4][0:EXPERTS, 0:DIM]).then_inc(s_eo, 1)
            dve.wait_ge(s_del, 1)
            for g in range(GROUPS):
                nc.vector.tensor_tensor(yg[:, g], xg[:, g], ps[5][:, g * DIM:(g + 1) * DIM], ALU.add).then_inc(s_new, 1)

        @block.tensor
        def _(pe):
            for s_, n in ((s_xt, 2), (s_proj, 10), (s_mix, NT), (s_c3, 2), (s_z3, 2), (s_t3, 2), (s_l3, 2)):
                pe.sem_inc(s_, 2 * n)
            pe.wait_ge(s_const, 16 * N_CONST)
            pe.wait_ge(s_pool0, 15)
            nc.tensor.transpose(ps[7][:, 0:EXPERTS], gate_nat[:, :], ident[0:EXPERTS, 0:EXPERTS]).then_inc(s_gtp, 1)

            def transposes(i, b, c):
                s, n = 2 * i + b, 2 * (2 * i + b) + c
                pe.wait_ge(s_xhat, mark(1, s, 1))
                pe.wait_ge(s_xn, chunk_mark(1, n - 2, 1))
                for t in range(TILES):
                    last = nc.tensor.transpose(ps[c][:, t * P:(t + 1) * P], xhat[:, b, TILES * c + t], ident[:, :])
                last.then_inc(s_xt, 1)

            def projections(i, b, c):
                n = 2 * (2 * i + b) + c
                pe.wait_ge(s_xn, chunk_mark(1, n, 1))
                free = ((s_sig, 3, 1), (s_prod, 2, 1), (s_sig, 3, 2), (s_prod, 2, 2), (s_sig, 3, 3))
                for k, (reader, per, at) in enumerate(free):
                    pe.wait_ge(reader, chunk_mark(per, n - 1, at))
                    nc.tensor.matmul(ps[2 + k][:, :], wcat[:, k], xn[:, c], start=True, stop=True).then_inc(s_proj, 1)

            def stage1(i):
                for b in range(2):
                    transposes(i, b, 1)
                    projections(i, b, 0)
                    if in_range(i, b, 1, STEPS):
                        transposes(*shifted(i, b, 1), 0)
                    projections(i, b, 1)

            transposes(0, 0, 0)
            pairs(pe, STEPS, stage1)

            pe.wait_ge(s_xn, mark(2, STEPS - 1, 2))
            pe.wait_ge(s_sig, mark(6, STEPS - 1, 6))
            pe.wait_ge(s_prod, mark(4, STEPS - 1, 4))

            def stage2(i):
                for b in range(2):
                    d = 2 * i + b
                    pe.wait_ge(s_ch[b], 32 * (i + 1))
                    for t in range(NT):
                        pe.wait_ge(s_ev, mark(NT, d - 2, t + 1))
                        for k in range(NT):
                            last = nc.tensor.matmul(ps[NT * b + t][:, 0:GRID], rch[:, b, k, t * P:(t + 1) * P],
                                                    lch[:, b, k], start=(k == 0), stop=(k == NT - 1))
                        last.then_inc(s_mix, 1)

            pairs(pe, DIM, stage2)

            pe.wait_ge(s_ev, mark(NT, DIM - 1, NT))
            pe.wait_ge(s_rmap, 1)
            for t in range(NT):
                for c in range(NT):
                    n = t * NT + c
                    if n >= 2:
                        pe.wait_ge(s_rtc, n - 1)
                    nc.tensor.transpose(ps[n % 2][:, 0:P], rstd_map[:, t, c * P:(c + 1) * P], ident[:, :]).then_inc(s_rtp, 1)

            def outer(i, b):
                s = 2 * i + b
                pe.wait_ge(s_sin[b], 16 * PARTS * (i + 1))
                for h in range(2):
                    pe.wait_ge(s_w3, mark(2, s - 1, h + 1))
                    nc.tensor.matmul(ps[h][:, :], coef[:, 0, :], statrow[:, b, h, :], start=True, stop=True).then_inc(s_c3, 1)

            def project(i, b):
                s = 2 * i + b
                for h in range(2):
                    pe.wait_ge(s_g3, mark(2, s, h + 1))
                    pe.wait_ge(s_r3, mark(2, s - 1, h + 1))
                    for c in range(TILES):
                        tok = slice(c * P, (c + 1) * P)
                        nc.tensor.matmul(ps[2 + h][:, tok], ot[:, b, h, tok], wo_sb[:, :], start=True, stop=False)
                        last = nc.tensor.matmul(ps[2 + h][:, tok], statrow[:, b, h, tok], coef[:, 1, :], start=False, stop=True)
                    last.then_inc(s_z3, 1)

            def transposes3(i, b):
                s = 2 * i + b
                for h in range(2):
                    pe.wait_ge(s_y3, mark(2, s, h + 1))
                    pe.wait_ge(s_p3, mark(2, s - 1, h + 1))
                    for c in range(TILES):
                        last = nc.tensor.transpose(ps[4 + h][:, c * P:(c + 1) * P], ys[:, b, h, c], ident[:, :])
                    last.then_inc(s_t3, 1)

            def logits(i, b):
                s = 2 * i + b
                pe.wait_ge(s_e3, mark(1, s - 2, 1))
                for h in range(2):
                    pe.wait_ge(s_p3, mark(2, s, h + 1))
                    nc.tensor.matmul(ps[6 + b][EXPERTS * h:EXPERTS * (h + 1), :], gate_t[:, :], yt[:, b, h],
                                     start=True, stop=True).then_inc(s_l3, 1)

            def stage3(i):
                for b in range(2):
                    if in_range(i, b, 1, STEPS):
                        outer(*shifted(i, b, 1))
                    if in_range(i, b, 0, STEPS):
                        project(i, b)
                    if in_range(i, b, -2, STEPS):
                        transposes3(*shifted(i, b, -2))
                        logits(*shifted(i, b, -2))

            pe.wait_ge(s_rtc, NT * NT)
            pe.wait_ge(s_coef, 16 * PARTS)
            pe.wait_ge(s_setup, 2)
            outer(0, 0)
            pairs(pe, STEPS, stage3, drain=1)

            pe.wait_ge(s_r3, mark(2, STEPS - 1, 2))
            pe.wait_ge(s_p3, mark(2, STEPS - 1, 2))
            pe.wait_ge(s_b1, 16)
            for c in range(HC):
                nc.tensor.transpose(ps[1][:, c * EXPERTS:(c + 1) * EXPERTS], b1_nat[:, c * P:(c + 1) * P],
                                    ident[0:EXPERTS, 0:EXPERTS])
            nc.tensor.transpose(ps[1][:, HC * EXPERTS:(HC + 1) * EXPERTS], b2_nat[:, :],
                                ident[0:EXPERTS, 0:EXPERTS]).then_inc(s_bt, 1)
            pe.wait_ge(s_yg, 1)
            for g in range(GROUPS):
                last = nc.tensor.matmul(ps[0][:, 0:EXPERTS], yg[:, g], sel[:, :], start=(g == 0), stop=(g == GROUPS - 1))
            last.then_inc(s_pool, 1)
            pe.wait_ge(s_pl, 1)
            pe.wait_ge(s_w1, 16 * WLOADS)
            for n in range(WLOADS):
                for e in range(n * WGROUP, (n + 1) * WGROUP):
                    for c in range(HC):
                        at = c * EXPERTS + e
                        last = nc.tensor.matmul(ps[2][:, at:at + 1], w1_sb[:, e, c * P:(c + 1) * P], pooled[:, e:e + 1],
                                                start=True, stop=True)
                last.then_inc(s_h1, 1)
            pe.wait_ge(s_hid, 1)
            for e in range(EXPERTS):
                if e % WGROUP == 0:
                    pe.wait_ge(s_w2[e // WGROUP], 16 * WGROUP)
                w2 = w2_in_work[:, e] if e < WGROUP else w2_in_w1[:, e - WGROUP]
                for c in range(HC):
                    at = c * EXPERTS + e
                    last = nc.tensor.matmul(ps[3][:, e:e + 1], w2[:, c], hid[:, at:at + 1], start=(c == 0), stop=(c == HC - 1))
            last.then_inc(s_h2, 1)
            pe.wait_ge(s_eot, 1)
            nc.tensor.transpose(ps[4][0:EXPERTS, 0:DIM], eo_t[:, :], ident[:, :]).then_inc(s_eop, 1)
            pe.wait_ge(s_eo, 1)
            for g in range(GROUPS):
                last = nc.tensor.matmul(ps[5][:, g * DIM:(g + 1) * DIM], wt[:, g * P:(g + 1) * P], eo[:, :], start=True, stop=True)
            last.then_inc(s_del, 1)


_INS = ["x", "L0_conv_norm_a", "L0_conv_norm_b", "L0_conv_Wl", "L0_conv_bl", "L0_conv_Wr", "L0_conv_br",
        "L0_conv_Wlg", "L0_conv_blg", "L0_conv_Wrg", "L0_conv_brg", "L0_conv_Wog", "L0_conv_bog",
        "L0_conv_on_a", "L0_conv_on_b", "L0_conv_Wo", "L0_conv_bo", "L0_ffn_gate_w", "L0_ffn_gate_b",
        "L0_ffn_weight1", "L0_ffn_weight2"]


def kernel(**inputs):
    import concourse.bacc as bacc
    from concourse.bass_utils import run_bass_kernel_spmd

    nc = bacc.Bacc("TRN2", target_bir_lowering=False, num_devices=1)
    arrays, args = {}, []
    for name in _INS:
        a = np.ascontiguousarray(inputs[name])
        arrays[f"in_{name}_dram"] = a
        args.append(nc.dram_tensor(f"in_{name}_dram", a.shape, mybir.dt.from_np(a.dtype), kind="ExternalInput").ap())
    result = nc.dram_tensor("out_0_dram", arrays["in_x_dram"].shape, FP32, kind="ExternalOutput").ap()
    build(nc, *args, result)
    r = run_bass_kernel_spmd(nc, [arrays], core_ids=[0])
    return r.results[0]["out_0_dram"]
```

```python
from contextlib import ExitStack

import numpy as np

import concourse.bass as bass
from concourse import mybir

FP32 = mybir.dt.float32
BF16 = mybir.dt.bfloat16
U32 = mybir.dt.uint32
I32 = mybir.dt.int32
ALU = mybir.AluOpType
ACT = mybir.ActivationFunctionType
AXX = mybir.AxisListType.X

P = 128
CHUNK = 512
TILES = CHUNK // P
TOP = 8
PARTS = 3
EPS_CONV_IN = 1e-6
EPS = 1e-5


def shifted(i, b, k):
    return i + (b + k) // 2, (b + k) % 2


def in_range(i, b, k, steps):
    return not isinstance(i, int) or 0 <= 2 * i + b + k < steps


def mark(per_step, step, k):
    return per_step * (step + 2) + k


def chunk_mark(per_chunk, chunk, k):
    return per_chunk * (chunk + 4) + k


def settle(engine, tick):
    engine.sem_inc(tick, 1)


def pairs(engine, steps, body, drain=0, cuts=()):
    first, last = 2, steps // 2 - 2
    for i in range(first):
        body(i)
    edges = [first + (last - first) * n // (len(cuts) + 1) for n in range(len(cuts) + 2)]
    for n in range(len(cuts) + 1):
        if edges[n] < edges[n + 1]:
            with engine.Fori(edges[n], edges[n + 1]) as i:
                body(i)
        if n < len(cuts):
            cuts[n]()
    for i in range(last, steps // 2 + drain):
        body(i)


def build(nc, x, norm_a, norm_b, Wl, bl, Wr, br, Wlg, blg, Wrg, brg, Wog, bog, on_a, on_b, Wo, bo,
          gate_w, gate_b, weight1, weight2, out):
    GRID, DIM = x.shape[1], x.shape[3]
    EXPERTS, _, HIDDEN = weight1.shape
    TOKENS = GRID * GRID
    NT = GRID // P
    STEPS = TOKENS // (2 * CHUNK)
    HC = HIDDEN // P
    PICKS = TOP * EXPERTS
    GROUPS = PICKS // P
    BAND = 32
    BANDS = P // BAND
    SIDE = EXPERTS // BANDS
    WGROUP = 2 * BANDS
    WLOADS = EXPERTS // WGROUP
    KR = 2 * PARTS * PARTS

    x_tok = x.rearrange("b i j d -> (b i j) d")
    out_tok = out.rearrange("b i j d -> (b i j) d")
    left_d = nc.dram_tensor("left_d", (DIM, TOKENS), FP32, kind="Internal").ap()
    right_d = nc.dram_tensor("right_d", (DIM, TOKENS), FP32, kind="Internal").ap()
    gate_d = nc.dram_tensor("gate_d", (DIM, TOKENS), FP32, kind="Internal").ap()
    mixed_d = nc.dram_tensor("mixed_d", (DIM, TOKENS), FP32, kind="Internal").ap()
    stat_d = nc.dram_tensor("stat_d", (2 * PARTS, TOKENS), BF16, kind="Internal").ap()
    picks_d = nc.dram_tensor("picks_d", (TOP, EXPERTS), FP32, kind="Internal").ap()

    with ExitStack() as ctx:
        def sb(name, shape, dt=FP32):
            return ctx.enter_context(nc.sbuf_tensor(name, shape, dt))

        def sem(name):
            return ctx.enter_context(nc.semaphore(name))

        W1_WORDS = EXPERTS * HIDDEN
        arena = sb("arena", [P, W1_WORDS])
        used = [0]

        def carve(pattern, **dims):
            size = int(np.prod(list(dims.values())))
            view = arena[:, used[0]:used[0] + size].rearrange(f"p ({pattern}) -> p {pattern}", **dims)
            used[0] += size
            return view

        xin = carve("b t d", b=2, t=2 * TILES, d=DIM)
        xhat = carve("b t d", b=2, t=2 * TILES, d=DIM)
        xn = carve("b n", b=2, n=CHUNK)
        sig_l = carve("b n", b=2, n=CHUNK)
        sig_r = carve("b n", b=2, n=CHUNK)
        left_sb = carve("b n", b=2, n=2 * CHUNK)
        right_sb = carve("b n", b=2, n=2 * CHUNK)
        gate_sb = carve("b n", b=2, n=2 * CHUNK)
        lch = carve("b t n", b=2, t=NT, n=GRID)
        rch = carve("b t n", b=2, t=NT, n=GRID)
        mix = carve("b t n", b=2, t=NT, n=GRID)
        mixsq = carve("b t n", b=2, t=NT, n=GRID)
        wcat = carve("k d", k=5, d=DIM)
        newton = carve("t n", t=NT, n=GRID)
        sum1 = carve("t n", t=NT, n=GRID)
        sum2 = carve("t n", t=NT, n=GRID)
        rstd_map = carve("t n", t=NT, n=GRID)
        halves = used[0]
        used[0] += PARTS * NT * GRID
        split = arena[:, halves:used[0]].bitcast(BF16).rearrange("p (q t n) -> p q t n", q=2 * PARTS, t=NT)
        assert used[0] <= W1_WORDS
        w1_sb = arena[:, :].rearrange("p (j g n) -> p j g n", j=SIDE, g=BANDS)
        w2_in_w1 = arena[:, :].rearrange("p (j g c n) -> p j g c n", j=SIDE, g=BANDS, c=HC)
        late_arena = arena[:, W1_WORDS - 8 * CHUNK:].rearrange("p (k b h n) -> p k b h n", k=2, b=2, h=2)
        gated = late_arena[:, 0]
        summed = late_arena[:, 1].rearrange("p b h (c d) -> p b h c d", c=TILES)

        work = sb("work", [P, 2 * WGROUP * HIDDEN])
        tail_used = [WGROUP * HIDDEN]

        def tail(size):
            tail_used[0] += size
            assert tail_used[0] <= 2 * WGROUP * HIDDEN
            return work[:, tail_used[0] - size:tail_used[0]]

        wv = work[:, :].rearrange("p (k b h n) -> p k b h n", k=4, b=2, h=2)
        ot, gt = wv[:, 0], wv[:, 1]
        xs = wv[:, 2].rearrange("p b h (c d) -> p b h c d", c=TILES)
        ys = wv[:, 3].rearrange("p b h (c d) -> p b h c d", c=TILES)
        w2_in_work = work[:, 0:WGROUP * HIDDEN].rearrange("p (j g c n) -> p j g c n", j=2, g=BANDS, c=HC)
        yt = sb("yt", [P, 2, 2, CHUNK])
        expo = sb("expo", [P, CHUNK])
        statrow = sb("statrow", [P, 2, 2, CHUNK], BF16)

        CANDS = STEPS * TOP
        WINDOWS = SIDE * BAND
        late = sb("late", [P, max(4 * CANDS, 2 * BANDS * WINDOWS) + max(CANDS, PICKS)])
        rstd_tok = late[:, 0:CANDS]
        cand = late[:, CANDS:2 * CANDS].rearrange("p (s k) -> p s k", k=TOP)
        cidx = late[:, 2 * CANDS:3 * CANDS].rearrange("p (s k) -> p s k", k=TOP)
        place = late[:, 3 * CANDS:4 * CANDS]
        base = late[:, 4 * CANDS:5 * CANDS].rearrange("p (s k) -> p s k", k=TOP)
        junk = late[:, max(4 * CANDS, 2 * BANDS * WINDOWS):]
        csum = sb("csum", [P, STEPS])

        wo_sb = sb("wo_sb", [P, DIM])
        cols = sb("cols", [P, 9])
        A_COL, B_COL, BLG, BL, BRG, BR, BOG, ONA = range(8)
        ident = sb("ident", [P, P])
        gate_nat = sb("gate_nat", [EXPERTS, DIM])
        gate_t = sb("gate_t", [P, EXPERTS])
        exact = sb("exact", [2 * PARTS, 2, DIM])
        exact_lo = sb("exact_lo", [2 * PARTS, 2, DIM])
        exact_p = sb("exact_p", [2 * PARTS, PARTS, 2, DIM], BF16)
        coef = sb("coef", [P, 2, DIM], BF16)
        rowsign = sb("rowsign", [2 * PARTS, 2])

        bn = sb("bn", [P, 2, 2 * TILES, 6])
        mv = sb("mv", [P, 2, 2 * TILES, 2])
        vv = sb("vv", [P, 2, 2 * TILES])
        rs = sb("rs", [P, 2, 2 * TILES])
        nmr = sb("nmr", [P, 2, 2 * TILES])
        mhalf = sb("mhalf", [P, 2 * TILES])
        rcol = sb("rcol", [P, 2, 2 * TILES])
        mx = sb("mx", [P, 2, TOP])
        ix = sb("ix", [P, 2, TOP], U32)
        negmax = sb("negmax", [P, 2, 1])
        esum = sb("esum", [P, 2, 1])

        half_off = sb("half_off", [P, 1])
        gb_col = sb("gb_col", [P, 1])
        pack = sb("pack", [P, 2 * TOP + 1])
        pack_hi = sb("pack_hi", [EXPERTS, 2 * TOP + 1])
        posu = sb("posu", [P, TOP], U32)
        posf = sb("posf", [P, TOP])
        wexp = sb("wexp", [P, STEPS])
        negm = sb("negm", [P, 1])
        both = sb("both", [EXPERTS, 2, 2 * TOP])
        best = sb("best", [EXPERTS, TOP])
        rank = sb("rank", [EXPERTS, 2 * TOP])
        rows = tail(2 * PICKS)
        scratch = rows[0:EXPERTS, :].rearrange("p (q j k) -> p q j k", q=4, k=2 * TOP)
        ahead, same, sooner = (scratch[:, q, 0:2 * TOP] for q in range(3))
        chosen = scratch[:, 3, 0:TOP]
        negbest = sb("negbest", [EXPERTS, 1])
        zscale = sb("zscale", [EXPERTS, 2])
        zsum = sb("zsum", [EXPERTS, 2])
        ztot = sb("ztot", [EXPERTS, 2])
        pick = sb("pick", [EXPERTS, 2, TOP])
        rowpick = sb("rowpick", [P, 2, GROUPS])
        allpick = tail(PICKS)
        earlier = tail(2 * PICKS - P)
        seen = sb("seen", [P, GROUPS])
        rowidx = sb("rowidx", [P, GROUPS], I32)
        scatidx = sb("scatidx", [P, GROUPS], I32)
        scatf = sb("scatf", [P, GROUPS])
        xg = rows[:, 0:PICKS].rearrange("p (g d) -> p g d", g=GROUPS)
        yg = rows[:, PICKS:2 * PICKS].rearrange("p (g d) -> p g d", g=GROUPS)
        rw = sb("rw", [P, GROUPS])
        sel = sb("sel", [P, EXPERTS])
        def windows(words):
            return words.rearrange("p (g w) -> p g w", g=BANDS)

        def diagonal(w):
            return w[:, :, 0:(SIDE - 1) * (BAND + 1) + 1:BAND + 1]

        win1 = windows(yt[:, :, :, :].rearrange("p b h n -> p (b h n)"))
        win2_words = (arena[:, W1_WORDS - 2 * BANDS * WINDOWS:], late[:, 0:2 * BANDS * WINDOWS])
        win2 = [windows(win2_words[c // 2][:, c % 2 * BANDS * WINDOWS:(c % 2 + 1) * BANDS * WINDOWS]) for c in range(HC)]
        pick_row = sb("pick_row", [P, 2, TOP])
        b1_row = tail(HIDDEN)
        b2_row = sb("b2_row", [P, DIM])
        hid = tail(HIDDEN)
        eo = sb("eo", [P, DIM])
        wt = tail(PICKS)
        wtk = expo[:, :]

        ps = [ctx.enter_context(nc.psum_tensor(f"bank{n}", [P, CHUNK], FP32)) for n in range(8)]

        HT_BANK = (3, 4, 6, 7)

        s_const = sem("s_const")
        s_coef = sem("s_coef")
        s_pool0 = sem("s_pool0")
        s_gtp = sem("s_gtp")
        s_setup = sem("s_setup")
        s_dve = sem("s_dve")

        s_tick_dve = sem("s_tick_dve")
        s_tick_sp = sem("s_tick_sp")
        s_tick_pool = sem("s_tick_pool")

        s_xin = [sem(f"s_xin{b}") for b in range(2)]
        s_bn = sem("s_bn")
        s_ag = sem("s_ag")
        s_var = sem("s_var")
        s_rstd = sem("s_rstd")
        s_xhat = sem("s_xhat")
        s_xt = sem("s_xt")
        s_xn = sem("s_xn")
        s_proj = sem("s_proj")
        s_sig = sem("s_sig")
        s_prod = sem("s_prod")
        s_lst = [sem(f"s_lst{b}") for b in range(2)]
        s_rst = [sem(f"s_rst{b}") for b in range(2)]
        s_gst = [sem(f"s_gst{b}") for b in range(2)]

        s_ch = [sem(f"s_ch{b}") for b in range(2)]
        s_mix = sem("s_mix")
        s_ev = sem("s_ev")
        s_acc = sem("s_acc")
        s_mst = [sem(f"s_mst{b}") for b in range(2)]
        s_mom = sem("s_mom")
        s_sq = sem("s_sq")
        s_rmap = sem("s_rmap")
        s_split = sem("s_split")
        s_stst = sem("s_stst")
        s_rtp = sem("s_rtp")
        s_rtc = sem("s_rtc")

        s_oin = [sem(f"s_oin{b}") for b in range(2)]
        s_x3 = [sem(f"s_x3{b}") for b in range(2)]
        s_sin = [sem(f"s_sin{b}") for b in range(2)]
        s_rc = sem("s_rc")
        s_c3 = sem("s_c3")
        s_w3 = sem("s_w3")
        s_g3 = sem("s_g3")
        s_z3 = sem("s_z3")
        s_r3 = sem("s_r3")
        s_v3 = sem("s_v3")
        s_n3 = sem("s_n3")
        s_y3 = sem("s_y3")
        s_t3 = sem("s_t3")
        s_p3 = sem("s_p3")
        s_l3 = sem("s_l3")
        s_m3 = sem("s_m3")
        s_k3 = sem("s_k3")
        s_e3 = sem("s_e3")
        s_q3 = sem("s_q3")
        s_ost = [sem(f"s_ost{b}") for b in range(2)]

        s_w1 = sem("s_w1")
        s_w2 = [sem(f"s_w2{n}") for n in range(WLOADS)]
        s_b1 = sem("s_b1")
        s_pack = sem("s_pack")
        s_hi = sem("s_hi")
        s_nm = sem("s_nm")
        s_we = sem("s_we")
        s_pick = sem("s_pick")
        s_rows = sem("s_rows")
        s_pst = sem("s_pst")
        s_all = sem("s_all")
        s_ri = sem("s_ri")
        s_gat = sem("s_gat")
        s_gvar = sem("s_gvar")
        s_gr = sem("s_gr")
        s_yg = sem("s_yg")
        s_pool = sem("s_pool")
        s_pl = sem("s_pl")
        s_h1 = sem("s_h1")
        s_pre = sem("s_pre")
        s_hid = sem("s_hid")
        s_ht = sem("s_ht")
        s_win = sem("s_win")
        s_clear = sem("s_clear")
        s_prow = sem("s_prow")
        s_h2 = sem("s_h2")
        s_eo = sem("s_eo")
        s_del = sem("s_del")
        s_new = sem("s_new")
        s_scat = sem("s_scat")

        def by_channel(t, h=None):
            return t.rearrange("c (s n) -> c s n", n=2 * CHUNK)

        left_w, right_w, gate_w_d = by_channel(left_d), by_channel(right_d), by_channel(gate_d)
        x_step = x_tok.rearrange("(s t p) d -> s p t d", t=2 * TILES, p=P)
        left_r = left_d.rearrange("c (t p j) -> c p t j", t=NT, p=P)
        right_r = right_d.rearrange("c (t p j) -> c p t j", t=NT, p=P)
        mixed_w = mixed_d.rearrange("c (t p j) -> c p t j", t=NT, p=P)
        stat_w = stat_d.rearrange("q (t p j) -> q p t j", t=NT, p=P)
        mixed_r = mixed_d.rearrange("c (s h n) -> s c h n", h=2, n=CHUNK)
        gate_r = gate_d.rearrange("c (s h n) -> s c h n", h=2, n=CHUNK)
        stat_r = stat_d.rearrange("(o q) (s n) -> s o q n", o=1, n=2 * CHUNK)
        out_step = out_tok.rearrange("(s t p) d -> s p t d", t=2 * TILES, p=P)
        N_CONST = 5 + 1 + 8 + 1 + 3 * PARTS + 2 + BANDS
        N_POOL0 = 17

        block = ctx.enter_context(nc.Block())

        @block.sync
        def _(sp):
            for n, w in enumerate((Wlg, Wl, Wrg, Wr, Wog)):
                sp.dma_start(wcat[:, n, :], w).then_inc(s_const, 16)
            sp.dma_start(wo_sb[:, :], Wo).then_inc(s_const, 16)
            for n, v in enumerate((norm_a, norm_b, blg, bl, brg, br, bog, on_a)):
                sp.dma_start(cols[:, n:n + 1], v.rearrange("(p o) -> p o", o=1)).then_inc(s_const, 16)
            sp.dma_start(gate_nat[:, :], gate_w).then_inc(s_const, 16)
            sp.wait_ge(s_pool0, 6)
            for q in range(PARTS):
                sp.dma_start(exact[q:q + 1, 0, :], on_a.rearrange("(o d) -> o d", o=1)).then_inc(s_const, 16)
                sp.dma_start(exact[PARTS + q:PARTS + q + 1, 0, :], on_b.rearrange("(o d) -> o d", o=1)).then_inc(s_const, 16)
                sp.dma_start(exact[PARTS + q:PARTS + q + 1, 1, :], bo.rearrange("(o d) -> o d", o=1)).then_inc(s_const, 16)
            for h in range(2):
                sp.dma_start(gb_col[EXPERTS * h:EXPERTS * (h + 1), :], gate_b.rearrange("(p o) -> p o", o=1)).then_inc(s_const, 16)
            sp.wait_ge(s_pool0, N_POOL0)
            for g in range(BANDS):
                sp.dma_start(b2_row[BAND * g:BAND * g + SIDE, :], weight2[SIDE * g:SIDE * (g + 1), HIDDEN, :]).then_inc(s_const, 16)

            def load_x(i, b):
                sp.wait_ge(s_xhat, mark(1, 2 * i + b - 2, 1))
                sp.dma_start(xin[:, b], x_step[2 * i + b]).then_inc(s_xin[b], 16)

            def stage1(i):
                for b in range(2):
                    s = 2 * i + b
                    if in_range(i, b, 3, STEPS):
                        load_x(*shifted(i, b, 3))
                    sp.wait_ge(s_prod, mark(4, s, 3))
                    sp.dma_start(left_w[:, s, :], left_sb[:, b]).then_inc(s_lst[b], 16)
                    sp.wait_ge(s_prod, mark(4, s, 4))
                    sp.dma_start(right_w[:, s, :], right_sb[:, b]).then_inc(s_rst[b], 16)
                    sp.wait_ge(s_sig, mark(6, s, 6))
                    sp.dma_start(gate_w_d[:, s, :], gate_sb[:, b]).then_inc(s_gst[b], 16)

            load_x(0, 0)
            load_x(0, 1)
            load_x(1, 0)
            pairs(sp, STEPS, stage1)
            for b in range(2):
                sp.wait_ge(s_lst[b], 16 * (STEPS // 2))
                sp.wait_ge(s_rst[b], 16 * (STEPS // 2))

            def load_channel(i, b):
                sp.wait_ge(s_mix, mark(NT, 2 * i + b - 2, NT))
                sp.dma_start(lch[:, b], left_r[2 * i + b]).then_inc(s_ch[b], 16)
                sp.dma_start(rch[:, b], right_r[2 * i + b]).then_inc(s_ch[b], 16)

            def stage2(i):
                for b in range(2):
                    if in_range(i, b, 2, DIM):
                        load_channel(*shifted(i, b, 2))
                    sp.wait_ge(s_ev, mark(NT, 2 * i + b, NT))
                    sp.dma_start(mixed_w[2 * i + b], mix[:, b]).then_inc(s_mst[b], 16)

            load_channel(0, 0)
            load_channel(0, 1)
            pairs(sp, DIM, stage2)
            for b in range(2):
                sp.wait_ge(s_mst[b], 16 * (DIM // 2))
                sp.wait_ge(s_gst[b], 16 * (STEPS // 2))

            def load_mixed(i, b):
                s = 2 * i + b
                sp.wait_ge(s_g3, mark(2, s - 2, 2))
                sp.dma_start(ot[:, b], mixed_r[s]).then_inc(s_oin[b], 16)
                sp.dma_start(gt[:, b], gate_r[s]).then_inc(s_oin[b], 16)

            def load_parts(i, b):
                s = 2 * i + b
                sp.wait_ge(s_z3, mark(2, s - 2, 2))
                settle(sp, s_tick_sp)
                sp.dma_start(statrow[0:KR, b], stat_r[s].broadcast_to([PARTS, 2 * PARTS, 2 * CHUNK])).then_inc(s_sin[b], 16)

            def load_x3(i, b):
                sp.dma_start(wv[:, 2, b].rearrange("p h (c d) -> p (h c) d", c=TILES), x_step[2 * i + b]).then_inc(s_x3[b], 16)

            def stage3(i):
                for b in range(2):
                    s = 2 * i + b
                    if in_range(i, b, 2, STEPS):
                        load_mixed(*shifted(i, b, 2))
                        load_parts(*shifted(i, b, 2))
                    sp.wait_ge(s_r3, mark(2, s, 2))
                    settle(sp, s_tick_sp)
                    sp.dma_start(out_step[s], late_arena[:, 1, b].rearrange("p h (c d) -> p (h c) d", c=TILES)).then_inc(s_ost[b], 16)
                    if in_range(i, b, 2, STEPS):
                        load_x3(*shifted(i, b, 2))

            load_mixed(0, 0)
            load_mixed(0, 1)
            load_x3(0, 0)
            load_x3(0, 1)
            for half in range(2):
                sp.wait_ge(s_split, half + 1)
                for q in range(PARTS * half, PARTS * (half + 1)):
                    sp.dma_start(stat_w[q], split[:, q]).then_inc(s_stst, 16)
            sp.wait_ge(s_stst, 16 * 2 * PARTS)
            load_parts(0, 0)
            load_parts(0, 1)
            pairs(sp, STEPS, stage3)

            w2_view = weight2[:, 0:HIDDEN, :].rearrange("(g j) (p c) n -> j p g (c n)", g=BANDS, c=HC)

            def load_w2(n):
                for j in range(2):
                    dst = w2_in_work[:, j] if n < 1 else w2_in_w1[:, 2 * n - 2 + j]
                    sp.dma_start(dst.rearrange("p g c n -> p g (c n)"), w2_view[2 * n + j]).then_inc(s_w2[n], 16)

            for b in range(2):
                sp.wait_ge(s_ost[b], 16 * (STEPS // 2))
            sp.wait_ge(s_t3, mark(2, STEPS - 1, 2))
            sp.wait_ge(s_clear, 1)
            for g in range(BANDS):
                sp.dma_start(b1_row[BAND * g:BAND * g + SIDE, :], weight1[SIDE * g:SIDE * (g + 1), DIM, :]).then_inc(s_b1, 16)
            load_w2(0)
            sp.wait_ge(s_pack, 1)
            sp.dma_start(pack_hi[:, :], pack[EXPERTS:2 * EXPERTS, :]).then_inc(s_hi, 16)
            sp.wait_ge(s_pick, 1)
            for hh in range(2):
                for kind in range(2):
                    sp.dma_start(rowpick[EXPERTS * hh:EXPERTS * (hh + 1), kind, :],
                                 pick[:, kind, hh:TOP:2],
                                 allow_slow_non_contiguous=True).then_inc(s_rows, 16)
            sp.dma_start(picks_d.rearrange("k e -> e k"), pick[:, 0, :],
                         allow_slow_non_contiguous=True).then_inc(s_pst, 16)
            sp.wait_ge(s_pst, 16)
            sp.dma_start(allpick[:, :], picks_d.rearrange("(o k) e -> o (k e)", o=1).broadcast_to([P, PICKS])).then_inc(s_all, 16)
            for g in range(BANDS):
                sp.dma_start(pick_row[BAND * g:BAND * g + SIDE, :, :], pick[SIDE * g:SIDE * (g + 1), :, :]).then_inc(s_prow, 16)
            for n in range(1, WLOADS):
                sp.wait_ge(s_h1, n + 1)
                load_w2(n)

        @block.gpsimd
        def _(pool):
            made = [0]

            def alone(instruction):
                made[0] += 1
                instruction.then_inc(s_pool0, 1)
                pool.wait_ge(s_pool0, made[0])

            alone(nc.gpsimd.memset(ident[:, :], 0.0))
            alone(nc.gpsimd.memset(sel[:, :], 0.0))
            alone(nc.gpsimd.memset(mhalf[:, :], -0.5))
            alone(nc.gpsimd.memset(half_off[0:EXPERTS, :], 0.0))
            alone(nc.gpsimd.memset(half_off[EXPERTS:P, :], float(CHUNK)))
            alone(nc.gpsimd.memset(exact[:, 1, :], 0.0))
            alone(nc.gpsimd.memset(rowsign[:, :], 1.0))
            alone(nc.gpsimd.memset(b2_row[:, :], 0.0))
            alone(nc.gpsimd.memset(pick_row[:, :, :], -1.0))
            alone(nc.gpsimd.memset(statrow[:, :, :, :], 0.0))
            alone(nc.gpsimd.memset(coef[:, :, :], 0.0))
            alone(nc.gpsimd.affine_select(out=ident[:, :], in_=ident[:, :], compare_op=ALU.not_equal, fill=1.0,
                                          base=0, pattern=[[-1, P]], channel_multiplier=1))
            for shift in (0, EXPERTS):
                alone(nc.gpsimd.affine_select(out=sel[:, :], in_=sel[:, :], compare_op=ALU.not_equal, fill=1.0,
                                              base=-shift, pattern=[[-1, EXPERTS]], channel_multiplier=1))
            alone(nc.gpsimd.affine_select(out=rowsign[:, 0:1], in_=rowsign[:, 0:1], compare_op=ALU.is_ge, fill=-1.0,
                                          base=-PARTS, pattern=[[0, 1]], channel_multiplier=1))
            alone(nc.gpsimd.iota(place[:, :], pattern=[[1, STEPS * TOP]], base=0, channel_multiplier=0,
                                 allow_small_or_imprecise_dtypes=True))
            alone(nc.gpsimd.iota(base[:, :, :], pattern=[[2 * CHUNK, STEPS], [0, TOP]], base=0, channel_multiplier=0,
                                 allow_small_or_imprecise_dtypes=True))

            pool.wait_ge(s_setup, 2)
            for a in range(PARTS):
                pool.dma_start(coef[2 * PARTS * a:2 * PARTS * (a + 1), :, :], exact_p[:, a]).then_inc(s_coef, 16)

            def stage1(i):
                for b in range(2):
                    pool.wait_ge(s_var, mark(1, 2 * i + b, 1))
                    nc.gpsimd.tensor_tensor(rs[:, b], vv[:, b], mhalf[:, 0:2 * TILES], ALU.pow).then_inc(s_rstd, 1)

            pairs(pool, STEPS, stage1)

            def columns(i, b):
                s = 2 * i + b
                pool.wait_ge(s_r3, mark(2, s - 2, 2))
                nc.gpsimd.tensor_copy(rcol[:, b], rstd_tok[:, bass.ds(s * 2 * TILES, 2 * TILES)]).then_inc(s_rc, 1)

            def gate(i, b):
                for h in range(2):
                    pool.wait_ge(s_w3, mark(2, 2 * i + b, h + 1))
                    nc.gpsimd.tensor_tensor(gated[:, b, h], gated[:, b, h], gt[:, b, h], ALU.mult).then_inc(s_g3, 1)

            def negate_max(i, b):
                pool.wait_ge(s_e3, mark(1, 2 * i + b - 2, 1))
                pool.wait_ge(s_m3, mark(2, 2 * i + b, 1))
                settle(pool, s_tick_pool)
                nc.gpsimd.tensor_scalar(negmax[:, b], mx[:, b, 0:1], -1.0, 0.0, ALU.mult, ALU.add).then_inc(s_k3, 1)

            def keep(i, b):
                s = 2 * i + b
                pool.wait_ge(s_m3, mark(2, s, 2))
                nc.gpsimd.tensor_copy(cand[:, bass.ds(s, 1), :], mx[:, b:b + 1, :])
                nc.gpsimd.tensor_copy(cidx[:, bass.ds(s, 1), :], ix[:, b:b + 1, :]).then_inc(s_q3, 1)

            def keep_sum(i, b):
                s = 2 * i + b
                pool.wait_ge(s_e3, mark(1, s, 1))
                nc.gpsimd.tensor_copy(csum[:, bass.ds(s, 1)], esum[:, b]).then_inc(s_q3, 1)

            def scales(i, b):
                s = 2 * i + b
                pool.wait_ge(s_v3, mark(1, s, 1))
                pool.wait_ge(s_y3, mark(2, s - 2, 2))
                nc.gpsimd.tensor_tensor(rs[:, b], vv[:, b], mhalf[:, 0:2 * TILES], ALU.pow).then_inc(s_n3, 1)
                pool.wait_ge(s_n3, mark(3, s, 1))
                nc.gpsimd.tensor_tensor(nmr[:, b], mv[:, b, :, 0], rs[:, b], ALU.mult).then_inc(s_n3, 1)
                pool.wait_ge(s_n3, mark(3, s, 2))
                settle(pool, s_tick_pool)
                nc.gpsimd.tensor_scalar(nmr[:, b], nmr[:, b], -1.0, 0.0, ALU.mult, ALU.add).then_inc(s_n3, 1)

            def stage3(i):
                for b in range(2):
                    if in_range(i, b, 1, STEPS):
                        columns(*shifted(i, b, 1))
                        gate(*shifted(i, b, 1))
                    if in_range(i, b, -3, STEPS):
                        negate_max(*shifted(i, b, -3))
                        keep(*shifted(i, b, -3))
                    if in_range(i, b, 0, STEPS):
                        scales(i, b)
                    if in_range(i, b, -3, STEPS):
                        keep_sum(*shifted(i, b, -3))

            pool.wait_ge(s_rtc, NT * NT)
            columns(0, 0)
            gate(0, 0)
            pairs(pool, STEPS, stage3, drain=2)

            for b in range(2):
                pool.wait_ge(s_ost[b], 16 * (STEPS // 2))
            pool.wait_ge(s_t3, mark(2, STEPS - 1, 2))
            nc.gpsimd.memset(b1_row, 0.0).then_inc(s_clear, 1)
            alone(nc.gpsimd.memset(earlier, 1.0))
            alone(nc.gpsimd.affine_select(out=earlier, in_=earlier, compare_op=ALU.is_gt, fill=0.0,
                                          base=PICKS - P, pattern=[[-1, 2 * PICKS - P]], channel_multiplier=1))
            pool.wait_ge(s_l3, mark(2, STEPS - 1, 2))
            nc.gpsimd.memset(yt[:, :, :, :], 0.0).then_inc(s_clear, 1)
            pool.wait_ge(s_ri, 1)
            for g in range(GROUPS):
                pool.indirect_dma_start(xg[:, g, :], None, out_tok, bass.IndirectOffsetOnAxis(rowidx[:, g:g + 1], 0)).then_inc(s_gat, 16)
            nc.gpsimd.memset(win2_words[1], 0.0).then_inc(s_clear, 1)
            pool.wait_ge(s_gvar, 1)
            nc.gpsimd.tensor_tensor(rs[:, 0, 0:GROUPS], vv[:, 0, 0:GROUPS], mhalf[:, 0:GROUPS], ALU.pow).then_inc(s_gr, 1)
            pool.wait_ge(s_h1, 1)
            nc.gpsimd.memset(win2_words[0], 0.0).then_inc(s_clear, 1)
            pool.wait_ge(s_new, GROUPS)
            for g in range(GROUPS):
                pool.indirect_dma_start(out_tok, bass.IndirectOffsetOnAxis(scatidx[:, g:g + 1], 0), yg[:, g, :], None,
                                        bounds_check=TOKENS - 1, oob_is_err=False).then_inc(s_scat, 16)
            pool.wait_ge(s_scat, 16 * GROUPS)

        @block.scalar
        def _(act):
            act.sem_inc(s_xn, 2 * 2)
            act.sem_inc(s_sig, 2 * 6)
            act.sem_inc(s_ev, 2 * NT)
            act.sem_inc(s_y3, 2 * 2)
            act.sem_inc(s_p3, 2 * 2)
            act.sem_inc(s_e3, 2)
            act.wait_ge(s_const, 16 * N_CONST)

            def scaled(i, b, c):
                n = 2 * (2 * i + b) + c
                act.wait_ge(s_xt, chunk_mark(1, n, 1))
                act.wait_ge(s_proj, chunk_mark(5, n - 2, 5))
                nc.scalar.activation(xn[:, c], ps[c][:, :], ACT.Identity, bias=cols[:, B_COL:B_COL + 1],
                                     scale=cols[:, A_COL:A_COL + 1]).then_inc(s_xn, 1)

            def stage1(i):
                for b in range(2):
                    for c in range(2):
                        s, n = 2 * i + b, 2 * (2 * i + b) + c
                        if c == 0:
                            scaled(i, b, 1)
                        elif in_range(i, b, 1, STEPS):
                            scaled(*shifted(i, b, 1), 0)
                        act.wait_ge(s_proj, chunk_mark(5, n, 1))
                        act.wait_ge(s_prod, chunk_mark(2, n - 2, 1))
                        nc.scalar.activation(sig_l[:, c], ps[2][:, :], ACT.Sigmoid, bias=cols[:, BLG:BLG + 1]).then_inc(s_sig, 1)
                        act.wait_ge(s_proj, chunk_mark(5, n, 3))
                        act.wait_ge(s_prod, chunk_mark(2, n - 2, 2))
                        nc.scalar.activation(sig_r[:, c], ps[4][:, :], ACT.Sigmoid, bias=cols[:, BRG:BRG + 1]).then_inc(s_sig, 1)
                        act.wait_ge(s_proj, chunk_mark(5, n, 5))
                        act.wait_ge(s_gst[b], 16 * i)
                        nc.scalar.activation(gate_sb[:, b, CHUNK * c:CHUNK * (c + 1)], ps[6][:, :], ACT.Sigmoid,
                                             bias=cols[:, BOG:BOG + 1]).then_inc(s_sig, 1)

            scaled(0, 0, 0)
            pairs(act, STEPS, stage1)

            def stage2(i):
                for b in range(2):
                    d = 2 * i + b
                    act.wait_ge(s_mst[b], 16 * i)
                    act.wait_ge(s_acc, mark(1, d - 2, 1))
                    for t in range(NT):
                        act.wait_ge(s_mix, mark(NT, d, t + 1))
                        nc.scalar.activation(mix[:, b, t], ps[NT * b + t][:, 0:GRID], ACT.Copy, scale=1.0 / GRID)
                        nc.scalar.activation(mixsq[:, b, t], ps[NT * b + t][:, 0:GRID], ACT.Square,
                                             scale=1.0 / GRID).then_inc(s_ev, 1)

            pairs(act, DIM, stage2)

            for t in range(NT):
                act.wait_ge(s_mom, t + 1)
                nc.scalar.activation(rstd_map[:, t], sum2[:, t], ACT.Sqrt).then_inc(s_sq, 1)
            rstd_grid = rstd_tok.rearrange("p (i c) -> p i c", c=NT)
            for t in range(NT):
                for c in range(NT):
                    n = t * NT + c
                    act.wait_ge(s_rtp, n + 1)
                    nc.scalar.copy(rstd_grid[:, t * P:(t + 1) * P, c], ps[n % 2][:, 0:P]).then_inc(s_rtc, 1)

            act.wait_ge(s_mix, mark(NT, DIM - 1, NT))
            act.wait_ge(s_acc, mark(1, DIM - 1, 1))
            act.wait_ge(s_stst, 16 * 2 * PARTS)
            act.wait_ge(s_rtp, NT * NT)
            for b in range(2):
                act.wait_ge(s_mst[b], 16 * (DIM // 2))
                act.wait_ge(s_gst[b], 16 * (STEPS // 2))
                act.wait_ge(s_lst[b], 16 * (STEPS // 2))
                act.wait_ge(s_rst[b], 16 * (STEPS // 2))

            w1_view = weight1[:, 0:DIM, :].rearrange("(g j) p n -> j p g n", g=BANDS)

            def load_w1(n):
                for j in range(2 * n, 2 * n + 2):
                    act.dma_start(w1_sb[:, j], w1_view[j]).then_inc(s_w1, 16)

            def exponentials(i, b):
                s = 2 * i + b
                act.wait_ge(s_m3, mark(2, s, 2))
                act.wait_ge(s_k3, mark(1, s, 1))
                act.wait_ge(s_q3, mark(2, s - 2, 2))
                nc.scalar.activation(expo[:, :], ps[6 + b][:, :], ACT.Exp, bias=negmax[:, b],
                                     accum_out=esum[:, b]).then_inc(s_e3, 1)

            def copy_transposed(i, b):
                s = 2 * i + b
                act.wait_ge(s_l3, mark(2, s - 2, 2))
                for h in range(2):
                    act.wait_ge(s_t3, mark(2, s, h + 1))
                    nc.scalar.copy(yt[:, b, h], ps[4 + h][:, :]).then_inc(s_p3, 1)

            def normalise(i, b):
                s = 2 * i + b
                act.wait_ge(s_n3, mark(3, s, 3))
                act.wait_ge(s_t3, mark(2, s - 2, 2))
                for h in range(2):
                    for c in range(TILES):
                        k = TILES * h + c
                        last = nc.scalar.activation(ys[:, b, h, c], summed[:, b, h, c], ACT.Identity,
                                                    bias=nmr[:, b, k:k + 1], scale=rs[:, b, k:k + 1])
                    last.then_inc(s_y3, 1)

            def stage3(i):
                for b in range(2):
                    if in_range(i, b, -2, STEPS):
                        copy_transposed(*shifted(i, b, -2))
                    if in_range(i, b, -3, STEPS):
                        exponentials(*shifted(i, b, -3))
                    if in_range(i, b, 0, STEPS):
                        normalise(i, b)

            cuts = [lambda n=n: load_w1(n) for n in range(WLOADS - 1)]
            pairs(act, STEPS, stage3, drain=2, cuts=cuts)

            act.wait_ge(s_z3, mark(2, STEPS - 1, 2))
            for b in range(2):
                act.wait_ge(s_ost[b], 16 * (STEPS // 2))
            load_w1(WLOADS - 1)
            act.wait_ge(s_nm, 1)
            nc.scalar.activation(wexp[:, :], cand[:, :, 0], ACT.Exp, bias=negm[:, :]).then_inc(s_we, 1)
            act.wait_ge(s_nm, 2)
            nc.scalar.activation(zscale[:, :], both[:, 0, 0:2 * TOP:TOP], ACT.Exp, bias=negbest[:, :]).then_inc(s_we, 1)
            nc.scalar.activation(pick[:, 1, :], best[:, :], ACT.Exp, bias=negbest[:, :]).then_inc(s_we, 1)
            act.wait_ge(s_pre, 1)
            nc.scalar.activation(hid, hid, ACT.Gelu).then_inc(s_hid, 1)

        @block.vector
        def _(dve):
            chain = [0]

            def link(instruction):
                chain[0] += 1
                instruction.then_inc(s_dve, 1)
                dve.wait_ge(s_dve, chain[0])

            for s_, n in ((s_bn, 1), (s_ag, 1), (s_var, 1), (s_xhat, 1), (s_prod, 4), (s_acc, 1),
                          (s_w3, 2), (s_r3, 2), (s_v3, 1), (s_m3, 2)):
                dve.sem_inc(s_, 2 * n)
            for s_, n in ((s_rstd, 1), (s_rc, 1), (s_g3, 2), (s_n3, 3), (s_k3, 1), (s_q3, 2)):
                dve.sem_inc(s_, 2 * n)

            dve.wait_ge(s_const, 16 * N_CONST)
            dve.wait_ge(s_pool0, N_POOL0)
            for q in range(2):
                link(nc.vector.tensor_scalar(exact[:, q, :], exact[:, q, :], rowsign[:, q:q + 1], None, ALU.mult))
            link(nc.vector.tensor_copy(exact_p[:, 0], exact[:, :, :]))
            link(nc.vector.tensor_tensor(exact_lo[:, :, :], exact[:, :, :], exact_p[:, 0], ALU.subtract))
            link(nc.vector.tensor_copy(exact_p[:, 1], exact_lo[:, :, :]))
            link(nc.vector.tensor_tensor(exact_lo[:, :, :], exact_lo[:, :, :], exact_p[:, 1], ALU.subtract))
            nc.vector.tensor_copy(exact_p[:, 2], exact_lo[:, :, :]).then_inc(s_setup, 1)
            dve.wait_ge(s_gtp, 1)
            nc.vector.tensor_copy(gate_t[:, :], ps[7][:, 0:EXPERTS]).then_inc(s_setup, 1)
            nc.vector.memset(sum1[:, :, :], 0.0)
            nc.vector.memset(sum2[:, :, :], 0.0)

            def statistics(i, b):
                s = 2 * i + b
                dve.wait_ge(s_xin[b], 16 * (i + 1))
                for t in range(2 * TILES):
                    last = nc.vector.bn_stats(bn[:, b, t], xin[:, b, t])
                last.then_inc(s_bn, 1)
                dve.wait_ge(s_bn, mark(1, s, 1))
                settle(dve, s_tick_dve)
                for t in range(2 * TILES):
                    last = nc.vector.bn_aggr(mv[:, b, t], bn[:, b, t])
                last.then_inc(s_ag, 1)
                dve.wait_ge(s_ag, mark(1, s, 1))
                nc.vector.tensor_scalar(vv[:, b], mv[:, b, :, 1], 1.0 + EPS, EPS_CONV_IN * EPS,
                                        ALU.mult, ALU.add).then_inc(s_var, 1)

            def centre(i, b):
                dve.wait_ge(s_rstd, mark(1, 2 * i + b, 1))
                dve.wait_ge(s_xt, mark(2, 2 * i + b - 2, 2))
                for t in range(2 * TILES):
                    last = nc.vector.tensor_scalar(xhat[:, b, t], xin[:, b, t], mv[:, b, t, 0:1],
                                                   rs[:, b, t:t + 1], ALU.subtract, ALU.mult)
                last.then_inc(s_xhat, 1)

            def product(i, b, c, side):
                n = 2 * (2 * i + b) + c
                stored, bank, col, sig, dst = ((s_lst, 3, BL, sig_l, left_sb), (s_rst, 5, BR, sig_r, right_sb))[side]
                dve.wait_ge(stored[b], 16 * i)
                dve.wait_ge(s_sig, chunk_mark(3, n, side + 1))
                dve.wait_ge(s_proj, chunk_mark(5, n, 2 * side + 2))
                nc.vector.scalar_tensor_tensor(out=dst[:, b, CHUNK * c:CHUNK * (c + 1)], in0=ps[bank][:, :],
                                               scalar=cols[:, col:col + 1], in1=sig[:, c], op0=ALU.add,
                                               op1=ALU.mult).then_inc(s_prod, 1)

            def stage1(i):
                for b in range(2):
                    if in_range(i, b, 1, STEPS):
                        centre(*shifted(i, b, 1))
                    product(i, b, 0, 0)
                    product(i, b, 0, 1)
                    if in_range(i, b, 2, STEPS):
                        statistics(*shifted(i, b, 2))
                    product(i, b, 1, 0)
                    product(i, b, 1, 1)

            statistics(0, 0)
            centre(0, 0)
            statistics(0, 1)
            pairs(dve, STEPS, stage1)

            def stage2(i):
                for b in range(2):
                    d = 2 * i + b
                    dve.wait_ge(s_ev, mark(NT, d, NT))
                    dve.wait_ge(s_acc, mark(1, d - 1, 1))
                    nc.vector.tensor_tensor(sum1[:, :, :], sum1[:, :, :], mix[:, b], ALU.add)
                    nc.vector.tensor_tensor(sum2[:, :, :], sum2[:, :, :], mixsq[:, b], ALU.add).then_inc(s_acc, 1)

            pairs(dve, DIM, stage2)

            dve.wait_ge(s_acc, mark(1, DIM - 1, 1))
            link(nc.vector.tensor_scalar(sum1[:, :, :], sum1[:, :, :], 1.0 / DIM, None, ALU.mult))
            link(nc.vector.tensor_tensor(newton, sum1, sum1, ALU.mult))
            link(nc.vector.scalar_tensor_tensor(out=sum2[:, :, :], in0=sum2[:, :, :], scalar=1.0 / DIM,
                                                in1=newton, op0=ALU.mult, op1=ALU.subtract))
            for t in range(NT):
                nc.vector.tensor_scalar(sum2[:, t], sum2[:, t], 0.0, EPS, ALU.max, ALU.add).then_inc(s_mom, 1)

            def split3(value, first):
                link(nc.vector.tensor_copy(split[:, first], value))
                link(nc.vector.tensor_tensor(value, value, split[:, first], ALU.subtract))
                link(nc.vector.tensor_copy(split[:, first + 1], value))
                link(nc.vector.tensor_tensor(value, value, split[:, first + 1], ALU.subtract))
                link(nc.vector.tensor_copy(split[:, first + 2], value))

            split3(sum1, 0)
            nc.vector.engine_nop().then_inc(s_split, 1)
            dve.wait_ge(s_sq, NT)
            link(nc.vector.reciprocal(rstd_map, rstd_map))
            link(nc.vector.tensor_tensor(newton, rstd_map, rstd_map, ALU.mult))
            link(nc.vector.tensor_tensor(newton, newton, sum2, ALU.mult))
            link(nc.vector.tensor_scalar(newton, newton, -0.5, 1.5, ALU.mult, ALU.add))
            nc.vector.tensor_tensor(rstd_map, rstd_map, newton, ALU.mult).then_inc(s_rmap, 1)
            dve.wait_ge(s_rmap, 1)
            link(nc.vector.tensor_tensor(sum2, sum2, rstd_map, ALU.mult))
            split3(sum2, PARTS)
            nc.vector.engine_nop().then_inc(s_split, 1)

            def weighted(i, b):
                for h in range(2):
                    dve.wait_ge(s_oin[b], 32 * (i + 1))
                    dve.wait_ge(s_c3, mark(2, 2 * i + b, h + 1))
                    dve.wait_ge(s_z3, mark(2, 2 * i + b - 2, h + 1))
                    nc.vector.scalar_tensor_tensor(out=gated[:, b, h], in0=ot[:, b, h], scalar=cols[:, ONA:ONA + 1],
                                                   in1=ps[h][:, :], op0=ALU.mult, op1=ALU.add).then_inc(s_w3, 1)

            def residual(i, b):
                s = 2 * i + b
                dve.wait_ge(s_rc, mark(1, s, 1))
                dve.wait_ge(s_x3[b], 16 * (i + 1))
                dve.wait_ge(s_ost[b], 16 * i)
                dve.wait_ge(s_y3, mark(2, s - 2, 2))
                for h in range(2):
                    dve.wait_ge(s_z3, mark(2, s, h + 1))
                    for c in range(TILES):
                        last = nc.vector.scalar_tensor_tensor(out=summed[:, b, h, c], in0=ps[2 + h][:, c * P:(c + 1) * P],
                                                              scalar=rcol[:, b, TILES * h + c:TILES * h + c + 1], in1=xs[:, b, h, c],
                                                              op0=ALU.mult, op1=ALU.add)
                    last.then_inc(s_r3, 1)

            def statistics3(i, b):
                s = 2 * i + b
                for h in range(2):
                    dve.wait_ge(s_r3, mark(2, s, h + 1))
                    for c in range(TILES):
                        last = nc.vector.bn_stats(bn[:, b, TILES * h + c], summed[:, b, h, c])
                last.then_inc(s_bn, 1)

            def aggregate3(i, b):
                s = 2 * i + b
                dve.wait_ge(s_bn, mark(1, STEPS + s, 1))
                dve.wait_ge(s_n3, mark(3, s - 2, 3))
                settle(dve, s_tick_dve)
                for t in range(2 * TILES):
                    last = nc.vector.bn_aggr(mv[:, b, t], bn[:, b, t])
                last.then_inc(s_ag, 1)
                dve.wait_ge(s_ag, mark(1, STEPS + s, 1))
                nc.vector.tensor_scalar(vv[:, b], mv[:, b, :, 1], 1.0, EPS, ALU.mult, ALU.add).then_inc(s_v3, 1)

            def best_values(i, b):
                s = 2 * i + b
                dve.wait_ge(s_l3, mark(2, s, 2))
                dve.wait_ge(s_q3, mark(2, s - 2, 1))
                dve.wait_ge(s_k3, mark(1, s - 2, 1))
                settle(dve, s_tick_dve)
                nc.vector.max(mx[:, b], ps[6 + b][:, :]).then_inc(s_m3, 1)

            def best_places(i, b):
                s = 2 * i + b
                dve.wait_ge(s_m3, mark(2, s, 1))
                settle(dve, s_tick_dve)
                nc.vector.max_index(ix[:, b], mx[:, b], ps[6 + b][:, :]).then_inc(s_m3, 1)

            def stage3(i):
                for b in range(2):
                    if in_range(i, b, 1, STEPS):
                        weighted(*shifted(i, b, 1))
                    if in_range(i, b, 0, STEPS):
                        residual(i, b)
                    if in_range(i, b, -3, STEPS):
                        best_values(*shifted(i, b, -3))
                    if in_range(i, b, 0, STEPS):
                        statistics3(i, b)
                    if in_range(i, b, -3, STEPS):
                        best_places(*shifted(i, b, -3))
                    if in_range(i, b, 0, STEPS):
                        aggregate3(i, b)

            weighted(0, 0)
            pairs(dve, STEPS, stage3, drain=2)

            dve.wait_ge(s_q3, mark(2, STEPS - 1, 2))
            flat = "p s k -> p (s k)"
            link(nc.vector.scalar_tensor_tensor(out=cidx[:, :, :], in0=cidx[:, :, :], scalar=half_off[:, :],
                                                in1=base[:, :, :], op0=ALU.add, op1=ALU.add))
            link(nc.vector.tensor_scalar(cand[:, :, :], cand[:, :, :], gb_col[:, :], None, ALU.add))
            link(nc.vector.max(pack[:, 0:TOP], cand[:, :, :].rearrange(flat)))
            nc.vector.tensor_scalar(negm[:, :], pack[:, 0:1], -1.0, None, ALU.mult).then_inc(s_nm, 1)
            link(nc.vector.max_index(posu[:, :], pack[:, 0:TOP], cand[:, :, :].rearrange(flat)))
            link(nc.vector.tensor_copy(posf[:, :], posu[:, :]))
            for k in range(TOP):
                link(nc.vector.scalar_tensor_tensor(out=junk[:, 0:STEPS * TOP], in0=place[:, :], scalar=posf[:, k:k + 1],
                                                      in1=cidx[:, :, :].rearrange(flat), op0=ALU.is_equal, op1=ALU.mult,
                                                      accum_out=pack[:, TOP + k:TOP + k + 1]))
            dve.wait_ge(s_we, 1)
            nc.vector.scalar_tensor_tensor(out=junk[:, 0:STEPS], in0=wexp[:, :], scalar=1.0, in1=csum[:, :],
                                           op0=ALU.mult, op1=ALU.mult,
                                           accum_out=pack[:, 2 * TOP:2 * TOP + 1]).then_inc(s_pack, 1)
            dve.wait_ge(s_pack, 1)
            nc.vector.tensor_copy(both[:, :, 0:TOP], pack[0:EXPERTS, 0:2 * TOP].rearrange("p (q k) -> p q k", q=2))
            nc.vector.tensor_copy(zsum[:, 0:1], pack[0:EXPERTS, 2 * TOP:2 * TOP + 1])
            dve.wait_ge(s_hi, 16)
            nc.vector.tensor_copy(both[:, :, TOP:2 * TOP], pack_hi[:, 0:2 * TOP].rearrange("p (q k) -> p q k", q=2))
            link(nc.vector.tensor_copy(zsum[:, 1:2], pack_hi[:, 2 * TOP:2 * TOP + 1]))
            def each(v):
                return v.rearrange("p (o k) -> p o k", o=1)

            def of(v):
                return v.rearrange("p (k o) -> p k o", o=1)

            square, eight = [EXPERTS, 2 * TOP, 2 * TOP], [EXPERTS, TOP, 2 * TOP]
            for q, (dst, op) in enumerate(((ahead, ALU.is_gt), (same, ALU.is_equal), (sooner, ALU.is_lt))):
                v = both[:, q // 2]
                last = nc.vector.tensor_tensor(dst, each(v).broadcast_to(square), of(v).broadcast_to(square), op)
            link(last)
            link(nc.vector.tensor_tensor(same, same, sooner, ALU.mult))
            link(nc.vector.tensor_tensor(ahead, ahead, same, ALU.add))
            link(nc.vector.tensor_reduce(rank[:, :], ahead, AXX, ALU.add))
            link(nc.vector.tensor_tensor(chosen, each(rank[:, :]).broadcast_to(eight),
                                         of(place[0:EXPERTS, 0:TOP]).broadcast_to(eight), ALU.is_equal))
            nc.vector.tensor_tensor(same[:, 0:TOP], chosen, each(both[:, 0]).broadcast_to(eight), ALU.mult)
            link(nc.vector.tensor_tensor(sooner[:, 0:TOP], chosen, each(both[:, 1]).broadcast_to(eight), ALU.mult))
            nc.vector.tensor_reduce(best[:, :], same[:, 0:TOP], AXX, ALU.add)
            link(nc.vector.tensor_reduce(pick[:, 0, :], sooner[:, 0:TOP], AXX, ALU.add))
            nc.vector.tensor_scalar(negbest[:, :], best[:, 0:1], -1.0, None, ALU.mult).then_inc(s_nm, 1)
            dve.wait_ge(s_we, 3)
            link(nc.vector.scalar_tensor_tensor(out=ztot[:, :], in0=zscale[:, :], scalar=1.0, in1=zsum[:, :],
                                                op0=ALU.mult, op1=ALU.mult, accum_out=negbest[:, :]))
            link(nc.vector.reciprocal(ztot[:, 0:1], negbest[:, :]))
            nc.vector.tensor_scalar(pick[:, 1, :], pick[:, 1, :], ztot[:, 0:1], None, ALU.mult).then_inc(s_pick, 1)
            dve.wait_ge(s_rows, 64)
            nc.vector.tensor_copy(rowidx[:, :], rowpick[:, 0, :]).then_inc(s_ri, 1)
            dve.wait_ge(s_gat, 16 * GROUPS)
            for g in range(GROUPS):
                last = nc.vector.bn_stats(bn[:, 0, g], xg[:, g])
            link(last)
            for g in range(GROUPS):
                last = nc.vector.bn_aggr(mv[:, 0, g], bn[:, 0, g])
            link(last)
            nc.vector.tensor_scalar(vv[:, 0, 0:GROUPS], mv[:, 0, 0:GROUPS, 1], 1.0, EPS, ALU.mult, ALU.add).then_inc(s_gvar, 1)
            dve.wait_ge(s_gr, 1)
            link(nc.vector.tensor_tensor(rw[:, :], rs[:, 0, 0:GROUPS], rowpick[:, 1, :], ALU.mult))
            for g in range(GROUPS):
                last = nc.vector.tensor_scalar(yg[:, g], xg[:, g], mv[:, 0, g, 0:1], rw[:, g:g + 1], ALU.subtract, ALU.mult)
            last.then_inc(s_yg, 1)
            dve.wait_ge(s_pool, 1)
            dve.wait_ge(s_clear, 2)
            nc.vector.tensor_copy(diagonal(win1), ps[0][:, 0:EXPERTS].rearrange("p (g j) -> p g j", g=BANDS)).then_inc(s_pl, 1)
            dve.wait_ge(s_all, 16)
            dve.wait_ge(s_pool0, N_POOL0 + 2)
            for g in range(GROUPS):
                at = PICKS - P - g * P
                link(nc.vector.scalar_tensor_tensor(out=junk[:, 0:PICKS], in0=allpick[:, :], scalar=rowpick[:, 0, g:g + 1],
                                                      in1=earlier[:, at:at + PICKS], op0=ALU.is_equal, op1=ALU.mult,
                                                      accum_out=seen[:, g:g + 1]))
            link(nc.vector.scalar_tensor_tensor(out=scatf[:, :], in0=seen[:, :], scalar=float(TOKENS),
                                                in1=rowpick[:, 0, :], op0=ALU.mult, op1=ALU.add))
            nc.vector.tensor_copy(scatidx[:, :], scatf[:, :])
            dve.wait_ge(s_prow, 16 * BANDS)
            for k in range(TOP):
                dst = wt if k == 0 else wtk
                link(nc.vector.tensor_scalar(dst[:, :], allpick[:, :], pick_row[:, 0, k:k + 1], pick_row[:, 1, k:k + 1],
                                             ALU.is_equal, ALU.mult))
                if k:
                    link(nc.vector.tensor_tensor(wt[:, :], wt[:, :], wtk[:, :], ALU.add))
            dve.wait_ge(s_b1, 16 * BANDS)
            dve.wait_ge(s_h1, WLOADS)
            nc.vector.tensor_tensor(hid, b1_row, ps[2][:, :], ALU.add).then_inc(s_pre, 1)
            dve.wait_ge(s_clear, 4)
            for c in range(HC):
                dve.wait_ge(s_ht, c + 1)
                nc.vector.tensor_copy(diagonal(win2[c]), ps[HT_BANK[c]][:, 0:P].rearrange(
                    "p (g w) -> p g w", g=BANDS)[:, :, 0:SIDE]).then_inc(s_win, 1)
            dve.wait_ge(s_h2, 1)
            nc.vector.tensor_tensor(eo[:, :], b2_row[:, :], ps[1][:, 0:DIM], ALU.add).then_inc(s_eo, 1)
            dve.wait_ge(s_del, 1)
            for g in range(GROUPS):
                nc.vector.tensor_tensor(yg[:, g], xg[:, g], ps[5][:, g * DIM:(g + 1) * DIM], ALU.add).then_inc(s_new, 1)

        @block.tensor
        def _(pe):
            for s_, n in ((s_xt, 2), (s_proj, 10), (s_mix, NT), (s_c3, 2), (s_z3, 2), (s_t3, 2), (s_l3, 2)):
                pe.sem_inc(s_, 2 * n)
            pe.wait_ge(s_const, 16 * N_CONST)
            pe.wait_ge(s_pool0, N_POOL0)
            nc.tensor.transpose(ps[7][:, 0:EXPERTS], gate_nat[:, :], ident[0:EXPERTS, 0:EXPERTS]).then_inc(s_gtp, 1)

            def transposes(i, b, c):
                s, n = 2 * i + b, 2 * (2 * i + b) + c
                pe.wait_ge(s_xhat, mark(1, s, 1))
                pe.wait_ge(s_xn, chunk_mark(1, n - 2, 1))
                for t in range(TILES):
                    last = nc.tensor.transpose(ps[c][:, t * P:(t + 1) * P], xhat[:, b, TILES * c + t], ident[:, :])
                last.then_inc(s_xt, 1)

            def projections(i, b, c):
                n = 2 * (2 * i + b) + c
                pe.wait_ge(s_xn, chunk_mark(1, n, 1))
                free = ((s_sig, 3, 1), (s_prod, 2, 1), (s_sig, 3, 2), (s_prod, 2, 2), (s_sig, 3, 3))
                for k, (reader, per, at) in enumerate(free):
                    pe.wait_ge(reader, chunk_mark(per, n - 1, at))
                    nc.tensor.matmul(ps[2 + k][:, :], wcat[:, k], xn[:, c], start=True, stop=True).then_inc(s_proj, 1)

            def stage1(i):
                for b in range(2):
                    transposes(i, b, 1)
                    projections(i, b, 0)
                    if in_range(i, b, 1, STEPS):
                        transposes(*shifted(i, b, 1), 0)
                    projections(i, b, 1)

            transposes(0, 0, 0)
            pairs(pe, STEPS, stage1)

            pe.wait_ge(s_xn, mark(2, STEPS - 1, 2))
            pe.wait_ge(s_sig, mark(6, STEPS - 1, 6))
            pe.wait_ge(s_prod, mark(4, STEPS - 1, 4))

            def stage2(i):
                for b in range(2):
                    d = 2 * i + b
                    pe.wait_ge(s_ch[b], 32 * (i + 1))
                    for t in range(NT):
                        pe.wait_ge(s_ev, mark(NT, d - 2, t + 1))
                        for k in range(NT):
                            last = nc.tensor.matmul(ps[NT * b + t][:, 0:GRID], rch[:, b, k, t * P:(t + 1) * P],
                                                    lch[:, b, k], start=(k == 0), stop=(k == NT - 1))
                        last.then_inc(s_mix, 1)

            pairs(pe, DIM, stage2)

            pe.wait_ge(s_ev, mark(NT, DIM - 1, NT))
            pe.wait_ge(s_rmap, 1)
            for t in range(NT):
                for c in range(NT):
                    n = t * NT + c
                    if n >= 2:
                        pe.wait_ge(s_rtc, n - 1)
                    nc.tensor.transpose(ps[n % 2][:, 0:P], rstd_map[:, t, c * P:(c + 1) * P], ident[:, :]).then_inc(s_rtp, 1)

            def outer(i, b):
                s = 2 * i + b
                pe.wait_ge(s_sin[b], 16 * (i + 1))
                for h in range(2):
                    pe.wait_ge(s_w3, mark(2, s - 1, h + 1))
                    nc.tensor.matmul(ps[h][:, :], coef[:, 0, :], statrow[:, b, h, :], start=True, stop=True).then_inc(s_c3, 1)

            def project(i, b):
                s = 2 * i + b
                for h in range(2):
                    pe.wait_ge(s_g3, mark(2, s, h + 1))
                    pe.wait_ge(s_r3, mark(2, s - 1, h + 1))
                    for c in range(TILES):
                        tok = slice(c * P, (c + 1) * P)
                        nc.tensor.matmul(ps[2 + h][:, tok], gated[:, b, h, tok], wo_sb[:, :], start=True, stop=False)
                        last = nc.tensor.matmul(ps[2 + h][:, tok], statrow[:, b, h, tok], coef[:, 1, :], start=False, stop=True)
                    last.then_inc(s_z3, 1)

            def transposes3(i, b):
                s = 2 * i + b
                for h in range(2):
                    pe.wait_ge(s_y3, mark(2, s, h + 1))
                    pe.wait_ge(s_p3, mark(2, s - 1, h + 1))
                    for c in range(TILES):
                        last = nc.tensor.transpose(ps[4 + h][:, c * P:(c + 1) * P], ys[:, b, h, c], ident[:, :])
                    last.then_inc(s_t3, 1)

            def logits(i, b):
                s = 2 * i + b
                pe.wait_ge(s_e3, mark(1, s - 2, 1))
                for h in range(2):
                    pe.wait_ge(s_p3, mark(2, s, h + 1))
                    nc.tensor.matmul(ps[6 + b][EXPERTS * h:EXPERTS * (h + 1), :], gate_t[:, :], yt[:, b, h],
                                     start=True, stop=True).then_inc(s_l3, 1)

            def stage3(i):
                for b in range(2):
                    if in_range(i, b, 1, STEPS):
                        outer(*shifted(i, b, 1))
                    if in_range(i, b, 0, STEPS):
                        project(i, b)
                    if in_range(i, b, -3, STEPS):
                        logits(*shifted(i, b, -3))
                    if in_range(i, b, -2, STEPS):
                        transposes3(*shifted(i, b, -2))

            pe.wait_ge(s_rtc, NT * NT)
            pe.wait_ge(s_coef, 16 * PARTS)
            pe.wait_ge(s_setup, 2)
            outer(0, 0)
            pairs(pe, STEPS, stage3, drain=2)

            pe.wait_ge(s_r3, mark(2, STEPS - 1, 2))
            pe.wait_ge(s_p3, mark(2, STEPS - 1, 2))
            pe.wait_ge(s_e3, mark(1, STEPS - 1, 1))
            pe.wait_ge(s_yg, 1)
            for g in range(GROUPS):
                last = nc.tensor.matmul(ps[0][:, 0:EXPERTS], yg[:, g], sel[:, :], start=(g == 0), stop=(g == GROUPS - 1))
            last.then_inc(s_pool, 1)
            pe.wait_ge(s_pl, 1)
            pe.wait_ge(s_w1, 16 * SIDE)
            order = (WLOADS - 1,) + tuple(range(WLOADS - 1))
            for n in order:
                for j in (2 * n, 2 * n + 1):
                    for g in range(BANDS):
                        last = nc.tensor.matmul(ps[2][BAND * g:BAND * (g + 1), :], win1[:, g, BAND * j:BAND * (j + 1)],
                                                w1_sb[:, j, g], start=(j == 2 * order[0]), stop=(j == 2 * order[-1] + 1))
                last.then_inc(s_h1, 1)
            pe.wait_ge(s_hid, 1)
            for c in range(HC):
                nc.tensor.transpose(ps[HT_BANK[c]][:, 0:P], hid[:, c::HC], ident[:, :]).then_inc(s_ht, 1)
            pe.wait_ge(s_win, HC)
            for n in range(WLOADS):
                pe.wait_ge(s_w2[n], 32)
                for j in (2 * n, 2 * n + 1):
                    w2 = w2_in_work[:, j] if n == 0 else w2_in_w1[:, j - 2]
                    for c in range(HC):
                        for g in range(BANDS):
                            last = nc.tensor.matmul(ps[1][BAND * g:BAND * (g + 1), 0:DIM], win2[c][:, g, BAND * j:BAND * (j + 1)],
                                                    w2[:, g, c], start=(j == 0 and c == 0), stop=(j == SIDE - 1 and c == HC - 1))
            last.then_inc(s_h2, 1)
            pe.wait_ge(s_eo, 1)
            for g in range(GROUPS):
                last = nc.tensor.matmul(ps[5][:, g * DIM:(g + 1) * DIM], wt[:, g * P:(g + 1) * P], eo[:, :], start=True, stop=True)
            last.then_inc(s_del, 1)


_INS = ["x", "L0_conv_norm_a", "L0_conv_norm_b", "L0_conv_Wl", "L0_conv_bl", "L0_conv_Wr", "L0_conv_br",
        "L0_conv_Wlg", "L0_conv_blg", "L0_conv_Wrg", "L0_conv_brg", "L0_conv_Wog", "L0_conv_bog",
        "L0_conv_on_a", "L0_conv_on_b", "L0_conv_Wo", "L0_conv_bo", "L0_ffn_gate_w", "L0_ffn_gate_b",
        "L0_ffn_weight1", "L0_ffn_weight2"]


def kernel(**inputs):
    import concourse.bacc as bacc
    from concourse.bass_utils import run_bass_kernel_spmd

    nc = bacc.Bacc("TRN2", target_bir_lowering=False, num_devices=1)
    arrays, args = {}, []
    for name in _INS:
        a = np.ascontiguousarray(inputs[name])
        arrays[f"in_{name}_dram"] = a
        args.append(nc.dram_tensor(f"in_{name}_dram", a.shape, mybir.dt.from_np(a.dtype), kind="ExternalInput").ap())
    result = nc.dram_tensor("out_0_dram", arrays["in_x_dram"].shape, FP32, kind="ExternalOutput").ap()
    build(nc, *args, result)
    r = run_bass_kernel_spmd(nc, [arrays], core_ids=[0])
    return r.results[0]["out_0_dram"]
```

```python
from contextlib import ExitStack

import numpy as np

import concourse.bass as bass
from concourse import mybir

FP32 = mybir.dt.float32
BF16 = mybir.dt.bfloat16
F32R = mybir.dt.float32r
U32 = mybir.dt.uint32
I32 = mybir.dt.int32
ALU = mybir.AluOpType
ACT = mybir.ActivationFunctionType
AXX = mybir.AxisListType.X

P = 128
CHUNK = 512
TILES = CHUNK // P
CENTRED = 5
TOP = 8
PARTS = 3
EPS_CONV_IN = 1e-6
EPS = 1e-5


def shifted(i, b, k):
    return i + (b + k) // 2, (b + k) % 2


def in_range(i, b, k, steps):
    return not isinstance(i, int) or 0 <= 2 * i + b + k < steps


def mark(per_step, step, k):
    return per_step * (step + 2) + k


def chunk_mark(per_chunk, chunk, k):
    return per_chunk * (chunk + 4) + k


def settle(engine, tick):
    engine.sem_inc(tick, 1)


def pairs(engine, steps, body, drain=0, cuts=(), lead=2):
    first, last = lead, steps // 2 - 2
    for i in range(first):
        body(i)
    edges = [first + (last - first) * n // (len(cuts) + 1) for n in range(len(cuts) + 2)]
    for n in range(len(cuts) + 1):
        if edges[n] < edges[n + 1]:
            with engine.Fori(edges[n], edges[n + 1]) as i:
                body(i)
        if n < len(cuts):
            cuts[n]()
    for i in range(last, steps // 2 + drain):
        body(i)


def build(nc, x, norm_a, norm_b, Wl, bl, Wr, br, Wlg, blg, Wrg, brg, Wog, bog, on_a, on_b, Wo, bo,
          gate_w, gate_b, weight1, weight2, out):
    GRID, DIM = x.shape[1], x.shape[3]
    EXPERTS, _, HIDDEN = weight1.shape
    TOKENS = GRID * GRID
    NT = GRID // P
    STEPS = TOKENS // (2 * CHUNK)
    HC = HIDDEN // P
    PICKS = TOP * EXPERTS
    GROUPS = PICKS // P
    BAND = 32
    BANDS = P // BAND
    SIDE = EXPERTS // BANDS
    WGROUP = 2 * BANDS
    WLOADS = EXPERTS // WGROUP
    KR = 2 * PARTS * PARTS

    x_tok = x.rearrange("b i j d -> (b i j) d")
    out_tok = out.rearrange("b i j d -> (b i j) d")
    left_d = nc.dram_tensor("left_d", (DIM, TOKENS), FP32, kind="Internal").ap()
    right_d = nc.dram_tensor("right_d", (DIM, TOKENS), FP32, kind="Internal").ap()
    gate_d = nc.dram_tensor("gate_d", (DIM, TOKENS), FP32, kind="Internal").ap()
    mixed_d = nc.dram_tensor("mixed_d", (DIM, TOKENS), FP32, kind="Internal").ap()
    stat_d = nc.dram_tensor("stat_d", (2 * PARTS, TOKENS), BF16, kind="Internal").ap()
    picks_d = nc.dram_tensor("picks_d", (TOP, EXPERTS), FP32, kind="Internal").ap()

    with ExitStack() as ctx:
        def sb(name, shape, dt=FP32):
            return ctx.enter_context(nc.sbuf_tensor(name, shape, dt))

        def sem(name):
            return ctx.enter_context(nc.semaphore(name))

        W1_WORDS = EXPERTS * HIDDEN
        arena = sb("arena", [P, W1_WORDS])
        used = [0]

        def carve(pattern, **dims):
            size = int(np.prod(list(dims.values())))
            view = arena[:, used[0]:used[0] + size].rearrange(f"p ({pattern}) -> p {pattern}", **dims)
            used[0] += size
            return view

        xin = carve("b t d", b=2, t=2 * TILES, d=DIM)
        xhat = carve("b t d", b=2, t=2 * TILES, d=DIM)
        sig_l = carve("b n", b=2, n=CHUNK)
        sig_r = carve("b n", b=2, n=CHUNK)
        left_sb = carve("b n", b=2, n=2 * CHUNK)
        right_sb = carve("b n", b=2, n=2 * CHUNK)
        gate_sb = carve("b n", b=2, n=2 * CHUNK)
        lch = carve("b t n", b=2, t=NT, n=GRID)
        rch = carve("b t n", b=2, t=NT, n=GRID)
        mix = carve("b t n", b=2, t=NT, n=GRID)
        mixsq = carve("b t n", b=2, t=NT, n=GRID)
        wcat = carve("k d", k=5, d=DIM)
        newton = carve("t n", t=NT, n=GRID)
        sum1 = carve("t n", t=NT, n=GRID)
        sum2 = carve("t n", t=NT, n=GRID)
        rstd_map = carve("t n", t=NT, n=GRID)
        halves = used[0]
        used[0] += PARTS * NT * GRID
        split = arena[:, halves:used[0]].bitcast(BF16).rearrange("p (q t n) -> p q t n", q=2 * PARTS, t=NT)
        assert used[0] <= W1_WORDS
        w1_sb = arena[:, :].rearrange("p (j g n) -> p j g n", j=SIDE, g=BANDS)
        w2_in_w1 = arena[:, :].rearrange("p (j g c n) -> p j g c n", j=SIDE, g=BANDS, c=HC)
        late_arena = arena[:, W1_WORDS - 8 * CHUNK:].rearrange("p (k b h n) -> p k b h n", k=2, b=2, h=2)
        gated = late_arena[:, 0]
        summed = late_arena[:, 1].rearrange("p b h (c d) -> p b h c d", c=TILES)

        with ExitStack() as stage1_ctx:
            def early(name, shape, dt=FP32):
                return stage1_ctx.enter_context(nc.sbuf_tensor(name, shape, dt))

            xn = early("xn", [P, 2, 2, CHUNK])
            x_parts = early("x_parts", [P, 2, 2, 2, CHUNK], F32R)
            w_parts = early("w_parts", [P, 2, 5, DIM], F32R)
        HI, LO = range(2)
        with ExitStack() as stage2_ctx:
            lr_parts = [stage2_ctx.enter_context(nc.sbuf_tensor(f"{name}_parts", [P, 2, 2, NT, GRID], F32R))
                        for name in ("left", "right")]
        LEFT, RIGHT = range(2)

        work = sb("work", [P, 2 * WGROUP * HIDDEN])
        tail_used = [WGROUP * HIDDEN]

        def tail(size):
            tail_used[0] += size
            assert tail_used[0] <= 2 * WGROUP * HIDDEN
            return work[:, tail_used[0] - size:tail_used[0]]

        wv = work[:, :].rearrange("p (k b h n) -> p k b h n", k=4, b=2, h=2)
        ot, gt = wv[:, 0], wv[:, 1]
        xs = wv[:, 2].rearrange("p b h (c d) -> p b h c d", c=TILES)
        ys = wv[:, 3].rearrange("p b h (c d) -> p b h c d", c=TILES)
        w2_in_work = work[:, 0:WGROUP * HIDDEN].rearrange("p (j g c n) -> p j g c n", j=2, g=BANDS, c=HC)
        yt = sb("yt", [P, 2, 2, CHUNK])
        expo = sb("expo", [P, CHUNK])
        statrow = sb("statrow", [P, 2, 2, CHUNK], BF16)

        CANDS = STEPS * TOP
        WINDOWS = SIDE * BAND
        late = sb("late", [P, max(4 * CANDS, 2 * BANDS * WINDOWS) + max(CANDS, PICKS)])
        rstd_tok = late[:, 0:CANDS]
        cand = late[:, CANDS:2 * CANDS].rearrange("p (s k) -> p s k", k=TOP)
        cidx = late[:, 2 * CANDS:3 * CANDS].rearrange("p (s k) -> p s k", k=TOP)
        place = late[:, 3 * CANDS:4 * CANDS]
        base = late[:, 4 * CANDS:5 * CANDS].rearrange("p (s k) -> p s k", k=TOP)
        junk = late[:, max(4 * CANDS, 2 * BANDS * WINDOWS):]
        csum = sb("csum", [P, STEPS])

        wo_sb = sb("wo_sb", [P, DIM])
        cols = sb("cols", [P, 9])
        A_COL, B_COL, BLG, BL, BRG, BR, BOG, ONA = range(8)
        ident = sb("ident", [P, P])
        gate_nat = sb("gate_nat", [EXPERTS, DIM])
        gate_t = sb("gate_t", [P, EXPERTS])
        exact = sb("exact", [2 * PARTS, 2, DIM])
        exact_lo = sb("exact_lo", [2 * PARTS, 2, DIM])
        exact_p = sb("exact_p", [2 * PARTS, PARTS, 2, DIM], BF16)
        coef = sb("coef", [P, 2, DIM], BF16)
        rowsign = sb("rowsign", [2 * PARTS, 2])

        bn = sb("bn", [P, 2, 2 * TILES, 6])
        mv = sb("mv", [P, 2, 2 * TILES, 2])
        vv = sb("vv", [P, 2, 2 * TILES])
        rs = sb("rs", [P, 2, 2 * TILES])
        minus = sb("minus", [P, 2, 2 * TILES])
        nmr = sb("nmr", [P, 2, 2 * TILES])
        mhalf = sb("mhalf", [P, 2 * TILES])
        rcol = sb("rcol", [P, 2, 2 * TILES])
        mx = sb("mx", [P, 2, TOP])
        ix = sb("ix", [P, 2, TOP], U32)
        negmax = sb("negmax", [P, 2, 1])
        esum = sb("esum", [P, 2, 1])

        half_off = sb("half_off", [P, 1])
        gb_col = sb("gb_col", [P, 1])
        pack = sb("pack", [P, 2 * TOP + 1])
        pack_hi = sb("pack_hi", [EXPERTS, 2 * TOP + 1])
        posu = sb("posu", [P, TOP], U32)
        posf = sb("posf", [P, TOP])
        wexp = sb("wexp", [P, STEPS])
        negm = sb("negm", [P, 1])
        both = sb("both", [EXPERTS, 2, 2 * TOP])
        best = sb("best", [EXPERTS, TOP])
        rank = sb("rank", [EXPERTS, 2 * TOP])
        rows = tail(2 * PICKS)
        scratch = rows[0:EXPERTS, :].rearrange("p (q j k) -> p q j k", q=4, k=2 * TOP)
        ahead, same, sooner = (scratch[:, q, 0:2 * TOP] for q in range(3))
        chosen = scratch[:, 3, 0:TOP]
        negbest = sb("negbest", [EXPERTS, 1])
        zscale = sb("zscale", [EXPERTS, 2])
        zsum = sb("zsum", [EXPERTS, 2])
        ztot = sb("ztot", [EXPERTS, 2])
        pick = sb("pick", [EXPERTS, 2, TOP])
        rowpick = sb("rowpick", [P, 2, GROUPS])
        allpick = tail(PICKS)
        earlier = tail(2 * PICKS - P)
        seen = sb("seen", [P, GROUPS])
        rowidx = sb("rowidx", [P, GROUPS], I32)
        scatidx = sb("scatidx", [P, GROUPS], I32)
        scatf = sb("scatf", [P, GROUPS])
        xg = rows[:, 0:PICKS].rearrange("p (g d) -> p g d", g=GROUPS)
        yg = rows[:, PICKS:2 * PICKS].rearrange("p (g d) -> p g d", g=GROUPS)
        rw = sb("rw", [P, GROUPS])
        sel = sb("sel", [P, EXPERTS])
        def windows(words):
            return words.rearrange("p (g w) -> p g w", g=BANDS)

        def diagonal(w):
            return w[:, :, 0:(SIDE - 1) * (BAND + 1) + 1:BAND + 1]

        win1 = windows(yt[:, :, :, :].rearrange("p b h n -> p (b h n)"))
        win2_words = (arena[:, W1_WORDS - 2 * BANDS * WINDOWS:], late[:, 0:2 * BANDS * WINDOWS])
        win2 = [windows(win2_words[c // 2][:, c % 2 * BANDS * WINDOWS:(c % 2 + 1) * BANDS * WINDOWS]) for c in range(HC)]
        pick_row = sb("pick_row", [P, 2, TOP])
        b1_row = tail(HIDDEN)
        b2_row = sb("b2_row", [P, DIM])
        hid = tail(HIDDEN)
        eo = sb("eo", [P, DIM])
        wt = tail(PICKS)
        wtk = expo[:, :]

        ps = [ctx.enter_context(nc.psum_tensor(f"bank{n}", [P, CHUNK], FP32)) for n in range(8)]

        HT_BANK = (3, 4, 6, 7)

        s_const = sem("s_const")
        s_const2 = sem("s_const2")
        s_coef = sem("s_coef")
        s_pool0 = sem("s_pool0")
        s_gtp = sem("s_gtp")
        s_setup = sem("s_setup")
        s_dve = sem("s_dve")

        s_tick_dve = sem("s_tick_dve")
        s_tick_sp = sem("s_tick_sp")
        s_tick_pool = sem("s_tick_pool")

        s_xin = [sem(f"s_xin{b}") for b in range(2)]
        s_bn = sem("s_bn")
        s_ag = sem("s_ag")
        s_var = sem("s_var")
        s_rstd = sem("s_rstd")
        s_xhat = sem("s_xhat")
        s_xhp = sem("s_xhp")
        s_xt = sem("s_xt")
        s_xn = sem("s_xn")
        s_lo = sem("s_lo")
        s_proj = sem("s_proj")
        s_sig = sem("s_sig")
        s_prod = sem("s_prod")
        s_lst = [sem(f"s_lst{b}") for b in range(2)]
        s_rst = [sem(f"s_rst{b}") for b in range(2)]
        s_gst = [sem(f"s_gst{b}") for b in range(2)]

        s_left = [sem(f"s_left{b}") for b in range(2)]
        s_right = [sem(f"s_right{b}") for b in range(2)]
        s_hi2 = sem("s_hi2")
        s_lo2 = [sem("s_lo2_left"), sem("s_lo2_right")]
        s_mix = sem("s_mix")
        s_ev = sem("s_ev")
        s_acc = sem("s_acc")
        s_mst = [sem(f"s_mst{b}") for b in range(2)]
        s_mom = sem("s_mom")
        s_sq = sem("s_sq")
        s_rmap = sem("s_rmap")
        s_split = sem("s_split")
        s_stst = sem("s_stst")
        s_rtp = sem("s_rtp")
        s_rtc = sem("s_rtc")

        s_oin = [sem(f"s_oin{b}") for b in range(2)]
        s_x3 = [sem(f"s_x3{b}") for b in range(2)]
        s_sin = [sem(f"s_sin{b}") for b in range(2)]
        s_rc = sem("s_rc")
        s_c3 = sem("s_c3")
        s_w3 = sem("s_w3")
        s_g3 = sem("s_g3")
        s_z3 = sem("s_z3")
        s_r3 = sem("s_r3")
        s_zr = sem("s_zr")
        s_ra = sem("s_ra")
        s_v3 = sem("s_v3")
        s_n3 = sem("s_n3")
        s_y3 = sem("s_y3")
        s_t3 = sem("s_t3")
        s_p3 = sem("s_p3")
        s_l3 = sem("s_l3")
        s_m3 = sem("s_m3")
        s_k3 = sem("s_k3")
        s_e3 = sem("s_e3")
        s_q3 = sem("s_q3")
        s_qs = sem("s_qs")
        s_ost = [sem(f"s_ost{b}") for b in range(2)]

        s_w1 = sem("s_w1")
        s_w2 = [sem(f"s_w2{n}") for n in range(WLOADS)]
        s_b1 = sem("s_b1")
        s_pack = sem("s_pack")
        s_hi = sem("s_hi")
        s_nm = sem("s_nm")
        s_we = sem("s_we")
        s_pick = sem("s_pick")
        s_rows = sem("s_rows")
        s_pst = sem("s_pst")
        s_all = sem("s_all")
        s_ri = sem("s_ri")
        s_gat = sem("s_gat")
        s_gvar = sem("s_gvar")
        s_gr = sem("s_gr")
        s_yg = sem("s_yg")
        s_pool = sem("s_pool")
        s_pl = sem("s_pl")
        s_h1 = sem("s_h1")
        s_pre = sem("s_pre")
        s_hid = sem("s_hid")
        s_ht = sem("s_ht")
        s_win = sem("s_win")
        s_clear = sem("s_clear")
        s_prow = sem("s_prow")
        s_h2 = sem("s_h2")
        s_eo = sem("s_eo")
        s_del = sem("s_del")
        s_new = sem("s_new")
        s_scat = sem("s_scat")

        def by_channel(t, h=None):
            return t.rearrange("c (s n) -> c s n", n=2 * CHUNK)

        left_w, right_w, gate_w_d = by_channel(left_d), by_channel(right_d), by_channel(gate_d)
        x_step = x_tok.rearrange("(s t p) d -> s p t d", t=2 * TILES, p=P)
        left_r = left_d.rearrange("c (t p j) -> c p t j", t=NT, p=P)
        right_r = right_d.rearrange("c (t p j) -> c p t j", t=NT, p=P)
        mixed_w = mixed_d.rearrange("c (t p j) -> c p t j", t=NT, p=P)
        stat_w = stat_d.rearrange("q (t p j) -> q p t j", t=NT, p=P)
        mixed_r = mixed_d.rearrange("c (s h n) -> s c h n", h=2, n=CHUNK)
        gate_r = gate_d.rearrange("c (s h n) -> s c h n", h=2, n=CHUNK)
        stat_r = stat_d.rearrange("(o q) (s n) -> s o q n", o=1, n=2 * CHUNK)
        out_step = out_tok.rearrange("(s t p) d -> s p t d", t=2 * TILES, p=P)
        N_CONST = 5 + 1 + 8 + 1
        N_CONST2 = 3 * PARTS + 2 + BANDS
        N_POOL0 = 17

        block = ctx.enter_context(nc.Block())

        @block.sync
        def _(sp):
            def load_x(i, b):
                sp.wait_ge(s_xhat, mark(1, 2 * i + b - 2, 1))
                sp.wait_ge(s_xhp, mark(1, 2 * i + b - 2, 1))
                sp.dma_start(xin[:, b], x_step[2 * i + b]).then_inc(s_xin[b], 16)

            load_x(0, 0)
            load_x(0, 1)

            for n, w in enumerate((Wlg, Wl, Wrg, Wr, Wog)):
                sp.dma_start(wcat[:, n, :], w).then_inc(s_const, 16)
            sp.dma_start(wo_sb[:, :], Wo).then_inc(s_const, 16)
            for n, v in enumerate((norm_a, norm_b, blg, bl, brg, br, bog, on_a)):
                sp.dma_start(cols[:, n:n + 1], v.rearrange("(p o) -> p o", o=1)).then_inc(s_const, 16)
            sp.dma_start(gate_nat[:, :], gate_w).then_inc(s_const, 16)
            load_x(1, 0)
            load_x(1, 1)
            sp.wait_ge(s_pool0, 6)
            for q in range(PARTS):
                sp.dma_start(exact[q:q + 1, 0, :], on_a.rearrange("(o d) -> o d", o=1)).then_inc(s_const2, 16)
                sp.dma_start(exact[PARTS + q:PARTS + q + 1, 0, :], on_b.rearrange("(o d) -> o d", o=1)).then_inc(s_const2, 16)
                sp.dma_start(exact[PARTS + q:PARTS + q + 1, 1, :], bo.rearrange("(o d) -> o d", o=1)).then_inc(s_const2, 16)
            for h in range(2):
                sp.dma_start(gb_col[EXPERTS * h:EXPERTS * (h + 1), :], gate_b.rearrange("(p o) -> p o", o=1)).then_inc(s_const2, 16)
            sp.wait_ge(s_pool0, N_POOL0)
            for g in range(BANDS):
                sp.dma_start(b2_row[BAND * g:BAND * g + SIDE, :], weight2[SIDE * g:SIDE * (g + 1), HIDDEN, :]).then_inc(s_const2, 16)

            def stage1(i):
                for b in range(2):
                    s = 2 * i + b
                    if in_range(i, b, 4, STEPS):
                        load_x(*shifted(i, b, 4))
                    sp.wait_ge(s_prod, mark(4, s, 3))
                    sp.dma_start(left_w[:, s, :], left_sb[:, b]).then_inc(s_lst[b], 16)
                    sp.wait_ge(s_prod, mark(4, s, 4))
                    sp.dma_start(right_w[:, s, :], right_sb[:, b]).then_inc(s_rst[b], 16)
                    sp.wait_ge(s_sig, mark(6, s, 6))
                    sp.dma_start(gate_w_d[:, s, :], gate_sb[:, b]).then_inc(s_gst[b], 16)

            pairs(sp, STEPS, stage1)
            for b in range(2):
                sp.wait_ge(s_lst[b], 16 * (STEPS // 2))
                sp.wait_ge(s_rst[b], 16 * (STEPS // 2))

            def load_channel(i, b):
                for side in (LEFT, RIGHT):
                    sp.wait_ge(s_lo2[side], mark(1, 2 * i + b - 2, 1))
                sp.dma_start(rch[:, b], right_r[2 * i + b]).then_inc(s_right[b], 16)
                sp.dma_start(lch[:, b], left_r[2 * i + b]).then_inc(s_left[b], 16)

            def stage2(i):
                for b in range(2):
                    if in_range(i, b, 2, DIM):
                        load_channel(*shifted(i, b, 2))
                    sp.wait_ge(s_ev, mark(NT, 2 * i + b, NT))
                    sp.dma_start(mixed_w[2 * i + b], mix[:, b]).then_inc(s_mst[b], 16)

            load_channel(0, 0)
            load_channel(0, 1)
            pairs(sp, DIM, stage2)
            for b in range(2):
                sp.wait_ge(s_mst[b], 16 * (DIM // 2))
                sp.wait_ge(s_gst[b], 16 * (STEPS // 2))

            def load_mixed(i, b):
                s = 2 * i + b
                sp.wait_ge(s_g3, mark(2, s - 2, 2))
                sp.dma_start(ot[:, b], mixed_r[s]).then_inc(s_oin[b], 16)
                sp.dma_start(gt[:, b], gate_r[s]).then_inc(s_oin[b], 16)

            def load_parts(i, b):
                s = 2 * i + b
                sp.wait_ge(s_z3, mark(2, s - 2, 2))
                settle(sp, s_tick_sp)
                sp.dma_start(statrow[0:KR, b], stat_r[s].broadcast_to([PARTS, 2 * PARTS, 2 * CHUNK])).then_inc(s_sin[b], 16)

            def load_x3(i, b):
                sp.dma_start(wv[:, 2, b].rearrange("p h (c d) -> p (h c) d", c=TILES), x_step[2 * i + b]).then_inc(s_x3[b], 16)

            def store_result(i, b):
                s = 2 * i + b
                sp.wait_ge(s_r3, mark(1, s, 1))
                sp.wait_ge(s_ra, mark(1, s, 1))
                settle(sp, s_tick_sp)
                sp.dma_start(out_step[s], late_arena[:, 1, b].rearrange("p h (c d) -> p (h c) d", c=TILES)).then_inc(s_ost[b], 16)

            def stage3(i):
                for b in range(2):
                    if in_range(i, b, 2, STEPS):
                        load_mixed(*shifted(i, b, 2))
                    if in_range(i, b, -1, STEPS):
                        store_result(*shifted(i, b, -1))
                    if in_range(i, b, 1, STEPS):
                        load_x3(*shifted(i, b, 1))
                    if in_range(i, b, 2, STEPS):
                        load_parts(*shifted(i, b, 2))

            load_mixed(0, 0)
            load_mixed(0, 1)
            load_x3(0, 0)
            for half in range(2):
                sp.wait_ge(s_split, half + 1)
                for q in range(PARTS * half, PARTS * (half + 1)):
                    sp.dma_start(stat_w[q], split[:, q]).then_inc(s_stst, 16)
            sp.wait_ge(s_stst, 16 * 2 * PARTS)
            load_parts(0, 0)
            load_parts(0, 1)
            pairs(sp, STEPS, stage3, drain=1)

            w2_view = weight2[:, 0:HIDDEN, :].rearrange("(g j) (p c) n -> j p g (c n)", g=BANDS, c=HC)

            def load_w2(n):
                for j in range(2):
                    dst = w2_in_work[:, j] if n < 1 else w2_in_w1[:, 2 * n - 2 + j]
                    sp.dma_start(dst.rearrange("p g c n -> p g (c n)"), w2_view[2 * n + j]).then_inc(s_w2[n], 16)

            for b in range(2):
                sp.wait_ge(s_ost[b], 16 * (STEPS // 2))
            sp.wait_ge(s_t3, mark(2, STEPS - 1, 2))
            sp.wait_ge(s_clear, 1)
            for g in range(BANDS):
                sp.dma_start(b1_row[BAND * g:BAND * g + SIDE, :], weight1[SIDE * g:SIDE * (g + 1), DIM, :]).then_inc(s_b1, 16)
            load_w2(0)
            sp.wait_ge(s_pack, 1)
            sp.dma_start(pack_hi[:, :], pack[EXPERTS:2 * EXPERTS, :]).then_inc(s_hi, 16)
            sp.wait_ge(s_pick, 1)
            for hh in range(2):
                for kind in range(2):
                    sp.dma_start(rowpick[EXPERTS * hh:EXPERTS * (hh + 1), kind, :],
                                 pick[:, kind, hh:TOP:2],
                                 allow_slow_non_contiguous=True).then_inc(s_rows, 16)
            sp.dma_start(picks_d.rearrange("k e -> e k"), pick[:, 0, :],
                         allow_slow_non_contiguous=True).then_inc(s_pst, 16)
            sp.wait_ge(s_pst, 16)
            sp.dma_start(allpick[:, :], picks_d.rearrange("(o k) e -> o (k e)", o=1).broadcast_to([P, PICKS])).then_inc(s_all, 16)
            for g in range(BANDS):
                sp.dma_start(pick_row[BAND * g:BAND * g + SIDE, :, :], pick[SIDE * g:SIDE * (g + 1), :, :]).then_inc(s_prow, 16)
            for n in range(1, WLOADS):
                sp.wait_ge(s_h1, n + 1)
                load_w2(n)

        @block.gpsimd
        def _(pool):
            made = [0]

            def alone(instruction):
                made[0] += 1
                instruction.then_inc(s_pool0, 1)
                pool.wait_ge(s_pool0, made[0])

            alone(nc.gpsimd.memset(ident[:, :], 0.0))
            alone(nc.gpsimd.memset(sel[:, :], 0.0))
            alone(nc.gpsimd.memset(mhalf[:, :], -0.5))
            alone(nc.gpsimd.memset(half_off[0:EXPERTS, :], 0.0))
            alone(nc.gpsimd.memset(half_off[EXPERTS:P, :], float(CHUNK)))
            alone(nc.gpsimd.memset(exact[:, 1, :], 0.0))
            alone(nc.gpsimd.memset(rowsign[:, :], 1.0))
            alone(nc.gpsimd.memset(b2_row[:, :], 0.0))
            alone(nc.gpsimd.memset(pick_row[:, :, :], -1.0))
            alone(nc.gpsimd.memset(statrow[:, :, :, :], 0.0))
            alone(nc.gpsimd.memset(coef[:, :, :], 0.0))
            alone(nc.gpsimd.affine_select(out=ident[:, :], in_=ident[:, :], compare_op=ALU.not_equal, fill=1.0,
                                          base=0, pattern=[[-1, P]], channel_multiplier=1))
            for shift in (0, EXPERTS):
                alone(nc.gpsimd.affine_select(out=sel[:, :], in_=sel[:, :], compare_op=ALU.not_equal, fill=1.0,
                                              base=-shift, pattern=[[-1, EXPERTS]], channel_multiplier=1))
            alone(nc.gpsimd.affine_select(out=rowsign[:, 0:1], in_=rowsign[:, 0:1], compare_op=ALU.is_ge, fill=-1.0,
                                          base=-PARTS, pattern=[[0, 1]], channel_multiplier=1))
            alone(nc.gpsimd.iota(place[:, :], pattern=[[1, STEPS * TOP]], base=0, channel_multiplier=0,
                                 allow_small_or_imprecise_dtypes=True))
            alone(nc.gpsimd.iota(base[:, :, :], pattern=[[2 * CHUNK, STEPS], [0, TOP]], base=0, channel_multiplier=0,
                                 allow_small_or_imprecise_dtypes=True))

            def rstd(i, b):
                pool.wait_ge(s_var, mark(1, 2 * i + b, 1))
                nc.gpsimd.tensor_tensor(rs[:, b], vv[:, b], mhalf[:, 0:2 * TILES], ALU.pow).then_inc(s_rstd, 1)

            def centre_rest(i, b):
                pool.wait_ge(s_rstd, mark(1, 2 * i + b, 1))
                pool.wait_ge(s_xt, mark(2, 2 * i + b - 2, 2))
                settle(pool, s_tick_pool)
                for t in range(CENTRED, 2 * TILES):
                    last = nc.gpsimd.tensor_scalar(xhat[:, b, t], xin[:, b, t], mv[:, b, t, 0:1],
                                                   rs[:, b, t:t + 1], ALU.subtract, ALU.mult)
                last.then_inc(s_xhp, 1)

            def low_half(i, b, c):
                pool.wait_ge(s_xn, chunk_mark(1, 2 * (2 * i + b) + c, 1))
                nc.gpsimd.tensor_tensor(x_parts[:, LO, b, c], xn[:, b, c], x_parts[:, HI, b, c], ALU.subtract).then_inc(s_lo, 1)

            def stage1(i):
                for b in range(2):
                    if in_range(i, b, 2, STEPS):
                        centre_rest(*shifted(i, b, 2))
                    if in_range(i, b, 1, STEPS):
                        low_half(*shifted(i, b, 1), 0)
                    if in_range(i, b, 3, STEPS):
                        rstd(*shifted(i, b, 3))
                    if in_range(i, b, 1, STEPS):
                        low_half(*shifted(i, b, 1), 1)

            rstd(0, 0)
            centre_rest(0, 0)
            rstd(0, 1)
            centre_rest(0, 1)
            rstd(1, 0)
            low_half(0, 0, 0)
            low_half(0, 0, 1)
            pairs(pool, STEPS, stage1)

            pool.wait_ge(s_setup, 3)
            for a in range(PARTS):
                pool.dma_start(coef[2 * PARTS * a:2 * PARTS * (a + 1), :, :], exact_p[:, a]).then_inc(s_coef, 16)

            def stage2(i):
                for b in range(2):
                    pool.wait_ge(s_hi2, mark(2, 2 * i + b, 1))
                    parts = lr_parts[RIGHT]
                    nc.gpsimd.tensor_tensor(parts[:, LO, b], rch[:, b], parts[:, HI, b], ALU.subtract).then_inc(s_lo2[RIGHT], 1)

            pairs(pool, DIM, stage2)

            def columns(i, b):
                s = 2 * i + b
                pool.wait_ge(s_r3, mark(1, s - 2, 1))
                pool.wait_ge(s_zr, mark(1, s - 2, 1))
                nc.gpsimd.tensor_copy(rcol[:, b], rstd_tok[:, bass.ds(s * 2 * TILES, 2 * TILES)]).then_inc(s_rc, 1)

            def gate(i, b):
                for h in range(2):
                    pool.wait_ge(s_w3, mark(2, 2 * i + b, h + 1))
                    nc.gpsimd.tensor_tensor(gated[:, b, h], gated[:, b, h], gt[:, b, h], ALU.mult).then_inc(s_g3, 1)

            def residual_rest(i, b):
                pool.wait_ge(s_x3[b], 16 * (i + 1))
                pool.wait_ge(s_zr, mark(1, 2 * i + b, 1))
                half = late_arena[:, 1, b, 1]
                nc.gpsimd.tensor_tensor(half, half, wv[:, 2, b, 1], ALU.add).then_inc(s_ra, 1)

            def negate_max(i, b):
                pool.wait_ge(s_e3, mark(1, 2 * i + b - 2, 1))
                pool.wait_ge(s_m3, mark(2, 2 * i + b, 1))
                settle(pool, s_tick_pool)
                nc.gpsimd.tensor_scalar(negmax[:, b], mx[:, b, 0:1], -1.0, 0.0, ALU.mult, ALU.add).then_inc(s_k3, 1)

            def keep(i, b):
                s = 2 * i + b
                pool.wait_ge(s_m3, mark(2, s, 2))
                nc.gpsimd.tensor_copy(cand[:, bass.ds(s, 1), :], mx[:, b:b + 1, :])
                nc.gpsimd.tensor_copy(cidx[:, bass.ds(s, 1), :], ix[:, b:b + 1, :]).then_inc(s_q3, 1)

            def keep_sum(i, b):
                s = 2 * i + b
                pool.wait_ge(s_e3, mark(1, s, 1))
                nc.gpsimd.tensor_copy(csum[:, bass.ds(s, 1)], esum[:, b]).then_inc(s_qs, 1)

            def scales(i, b):
                s = 2 * i + b
                pool.wait_ge(s_v3, mark(1, s, 1))
                pool.wait_ge(s_y3, mark(2, s - 2, 2))
                nc.gpsimd.tensor_tensor(rs[:, b], vv[:, b], mhalf[:, 0:2 * TILES], ALU.pow).then_inc(s_n3, 1)
                pool.wait_ge(s_n3, mark(2, s, 1))
                nc.gpsimd.tensor_tensor(nmr[:, b], minus[:, b], rs[:, b], ALU.mult).then_inc(s_n3, 1)

            def stage3(i):
                for b in range(2):
                    if in_range(i, b, 1, STEPS):
                        columns(*shifted(i, b, 1))
                        gate(*shifted(i, b, 1))
                    if in_range(i, b, -4, STEPS):
                        negate_max(*shifted(i, b, -4))
                        keep(*shifted(i, b, -4))
                    if in_range(i, b, -1, STEPS):
                        scales(*shifted(i, b, -1))
                    if in_range(i, b, 0, STEPS):
                        residual_rest(i, b)
                    if in_range(i, b, -5, STEPS):
                        keep_sum(*shifted(i, b, -5))

            pool.wait_ge(s_rtc, NT * NT)
            columns(0, 0)
            gate(0, 0)
            pairs(pool, STEPS, stage3, drain=3, lead=3)

            for b in range(2):
                pool.wait_ge(s_ost[b], 16 * (STEPS // 2))
            pool.wait_ge(s_t3, mark(2, STEPS - 1, 2))
            nc.gpsimd.memset(b1_row, 0.0).then_inc(s_clear, 1)
            alone(nc.gpsimd.memset(earlier, 1.0))
            alone(nc.gpsimd.affine_select(out=earlier, in_=earlier, compare_op=ALU.is_gt, fill=0.0,
                                          base=PICKS - P, pattern=[[-1, 2 * PICKS - P]], channel_multiplier=1))
            pool.wait_ge(s_l3, mark(2, STEPS - 1, 2))
            nc.gpsimd.memset(yt[:, :, :, :], 0.0).then_inc(s_clear, 1)
            pool.wait_ge(s_ri, 1)
            for g in range(GROUPS):
                pool.indirect_dma_start(xg[:, g, :], None, out_tok, bass.IndirectOffsetOnAxis(rowidx[:, g:g + 1], 0)).then_inc(s_gat, 16)
            nc.gpsimd.memset(win2_words[1], 0.0).then_inc(s_clear, 1)
            pool.wait_ge(s_gvar, 1)
            nc.gpsimd.tensor_tensor(rs[:, 0, 0:GROUPS], vv[:, 0, 0:GROUPS], mhalf[:, 0:GROUPS], ALU.pow).then_inc(s_gr, 1)
            pool.wait_ge(s_h1, 1)
            nc.gpsimd.memset(win2_words[0], 0.0).then_inc(s_clear, 1)
            pool.wait_ge(s_new, GROUPS)
            for g in range(GROUPS):
                pool.indirect_dma_start(out_tok, bass.IndirectOffsetOnAxis(scatidx[:, g:g + 1], 0), yg[:, g, :], None,
                                        bounds_check=TOKENS - 1, oob_is_err=False).then_inc(s_scat, 16)
            pool.wait_ge(s_scat, 16 * GROUPS)

        @block.scalar
        def _(act):
            act.sem_inc(s_xn, 2 * 2)
            act.sem_inc(s_sig, 2 * 6)
            act.sem_inc(s_ev, 2 * NT)
            act.sem_inc(s_hi2, 2 * 2)
            act.sem_inc(s_y3, 2 * 2)
            act.sem_inc(s_zr, 2)
            act.sem_inc(s_p3, 2 * 2)
            act.sem_inc(s_e3, 2)
            act.wait_ge(s_const, 16 * N_CONST)

            def scaled(i, b, c):
                n = 2 * (2 * i + b) + c
                act.wait_ge(s_xt, chunk_mark(1, n, 1))
                act.wait_ge(s_lo, chunk_mark(1, n - 4, 1))
                act.wait_ge(s_proj, chunk_mark(5, n - 4, 5))
                for dst in (xn[:, b, c], x_parts[:, HI, b, c]):
                    last = nc.scalar.activation(dst, ps[c][:, :], ACT.Identity, bias=cols[:, B_COL:B_COL + 1],
                                                scale=cols[:, A_COL:A_COL + 1])
                last.then_inc(s_xn, 1)

            def stage1(i):
                for b in range(2):
                    for c in range(2):
                        s, n = 2 * i + b, 2 * (2 * i + b) + c
                        if in_range(i, b, 1, STEPS):
                            scaled(*shifted(i, b, 1), c)
                        act.wait_ge(s_proj, chunk_mark(5, n, 1))
                        act.wait_ge(s_prod, chunk_mark(2, n - 2, 1))
                        nc.scalar.activation(sig_l[:, c], ps[2][:, :], ACT.Sigmoid, bias=cols[:, BLG:BLG + 1]).then_inc(s_sig, 1)
                        act.wait_ge(s_proj, chunk_mark(5, n, 3))
                        act.wait_ge(s_prod, chunk_mark(2, n - 2, 2))
                        nc.scalar.activation(sig_r[:, c], ps[4][:, :], ACT.Sigmoid, bias=cols[:, BRG:BRG + 1]).then_inc(s_sig, 1)
                        act.wait_ge(s_proj, chunk_mark(5, n, 5))
                        act.wait_ge(s_gst[b], 16 * i)
                        nc.scalar.activation(gate_sb[:, b, CHUNK * c:CHUNK * (c + 1)], ps[6][:, :], ACT.Sigmoid,
                                             bias=cols[:, BOG:BOG + 1]).then_inc(s_sig, 1)

            scaled(0, 0, 0)
            scaled(0, 0, 1)
            pairs(act, STEPS, stage1)

            def high_halves(i, b):
                act.wait_ge(s_right[b], 16 * (i + 1))
                act.wait_ge(s_mix, mark(NT, 2 * i + b - 2, NT))
                nc.scalar.copy(lr_parts[RIGHT][:, HI, b], rch[:, b]).then_inc(s_hi2, 1)
                act.wait_ge(s_left[b], 16 * (i + 1))
                nc.scalar.copy(lr_parts[LEFT][:, HI, b], lch[:, b]).then_inc(s_hi2, 1)

            def stage2(i):
                for b in range(2):
                    d = 2 * i + b
                    if in_range(i, b, 1, DIM):
                        high_halves(*shifted(i, b, 1))
                    act.wait_ge(s_mst[b], 16 * i)
                    act.wait_ge(s_acc, mark(1, d - 2, 1))
                    for t in range(NT):
                        act.wait_ge(s_mix, mark(NT, d, t + 1))
                        nc.scalar.activation(mix[:, b, t], ps[NT * b + t][:, 0:GRID], ACT.Copy, scale=1.0 / GRID)
                        nc.scalar.activation(mixsq[:, b, t], ps[NT * b + t][:, 0:GRID], ACT.Square,
                                             scale=1.0 / GRID).then_inc(s_ev, 1)

            high_halves(0, 0)
            pairs(act, DIM, stage2)

            for t in range(NT):
                act.wait_ge(s_mom, t + 1)
                nc.scalar.activation(rstd_map[:, t], sum2[:, t], ACT.Sqrt).then_inc(s_sq, 1)
            rstd_grid = rstd_tok.rearrange("p (i c) -> p i c", c=NT)
            for t in range(NT):
                for c in range(NT):
                    n = t * NT + c
                    act.wait_ge(s_rtp, n + 1)
                    nc.scalar.copy(rstd_grid[:, t * P:(t + 1) * P, c], ps[n % 2][:, 0:P]).then_inc(s_rtc, 1)

            act.wait_ge(s_mix, mark(NT, DIM - 1, NT))
            act.wait_ge(s_acc, mark(1, DIM - 1, 1))
            act.wait_ge(s_stst, 16 * 2 * PARTS)
            act.wait_ge(s_rtp, NT * NT)
            for b in range(2):
                act.wait_ge(s_mst[b], 16 * (DIM // 2))
                act.wait_ge(s_gst[b], 16 * (STEPS // 2))
                act.wait_ge(s_lst[b], 16 * (STEPS // 2))
                act.wait_ge(s_rst[b], 16 * (STEPS // 2))

            w1_view = weight1[:, 0:DIM, :].rearrange("(g j) p n -> j p g n", g=BANDS)

            def load_w1(n):
                for j in range(2 * n, 2 * n + 2):
                    act.dma_start(w1_sb[:, j], w1_view[j]).then_inc(s_w1, 16)

            def exponentials(i, b):
                s = 2 * i + b
                act.wait_ge(s_m3, mark(2, s, 2))
                act.wait_ge(s_k3, mark(1, s, 1))
                act.wait_ge(s_e3, mark(1, s - 1, 1))
                act.wait_ge(s_qs, mark(1, s - 2, 1))
                nc.scalar.activation(expo[:, :], ps[6 + b][:, :], ACT.Exp, bias=negmax[:, b],
                                     accum_out=esum[:, b]).then_inc(s_e3, 1)

            def scale_rest(i, b):
                s = 2 * i + b
                act.wait_ge(s_rc, mark(1, s, 1))
                act.wait_ge(s_ost[b], 16 * i)
                act.wait_ge(s_y3, mark(2, s - 2, 2))
                act.wait_ge(s_z3, mark(2, s, 2))
                for c in range(TILES):
                    last = nc.scalar.activation(summed[:, b, 1, c], ps[3][:, c * P:(c + 1) * P], ACT.Copy,
                                                scale=rcol[:, b, TILES + c:TILES + c + 1])
                last.then_inc(s_zr, 1)

            def copy_transposed(i, b):
                s = 2 * i + b
                act.wait_ge(s_l3, mark(2, s - 2, 2))
                for h in range(2):
                    act.wait_ge(s_t3, mark(2, s, h + 1))
                    nc.scalar.copy(yt[:, b, h], ps[4 + h][:, :]).then_inc(s_p3, 1)

            def normalise(i, b):
                s = 2 * i + b
                act.wait_ge(s_n3, mark(2, s, 2))
                act.wait_ge(s_t3, mark(2, s - 2, 2))
                for h in range(2):
                    for c in range(TILES):
                        k = TILES * h + c
                        last = nc.scalar.activation(ys[:, b, h, c], summed[:, b, h, c], ACT.Identity,
                                                    bias=nmr[:, b, k:k + 1], scale=rs[:, b, k:k + 1])
                    last.then_inc(s_y3, 1)

            def stage3(i):
                for b in range(2):
                    if in_range(i, b, 0, STEPS):
                        scale_rest(i, b)
                    if in_range(i, b, -1, STEPS):
                        normalise(*shifted(i, b, -1))
                    if in_range(i, b, -2, STEPS):
                        copy_transposed(*shifted(i, b, -2))
                    if in_range(i, b, -4, STEPS):
                        exponentials(*shifted(i, b, -4))

            cuts = [lambda n=n: load_w1(n) for n in range(WLOADS - 1)]
            pairs(act, STEPS, stage3, drain=2, cuts=cuts)

            act.wait_ge(s_z3, mark(2, STEPS - 1, 2))
            for b in range(2):
                act.wait_ge(s_ost[b], 16 * (STEPS // 2))
            load_w1(WLOADS - 1)
            act.wait_ge(s_nm, 1)
            nc.scalar.activation(wexp[:, :], cand[:, :, 0], ACT.Exp, bias=negm[:, :]).then_inc(s_we, 1)
            act.wait_ge(s_nm, 2)
            nc.scalar.activation(zscale[:, :], both[:, 0, 0:2 * TOP:TOP], ACT.Exp, bias=negbest[:, :]).then_inc(s_we, 1)
            nc.scalar.activation(pick[:, 1, :], best[:, :], ACT.Exp, bias=negbest[:, :]).then_inc(s_we, 1)
            act.wait_ge(s_pre, 1)
            nc.scalar.activation(hid, hid, ACT.Gelu).then_inc(s_hid, 1)

        @block.vector
        def _(dve):
            chain = [0]

            def link(instruction):
                chain[0] += 1
                instruction.then_inc(s_dve, 1)
                dve.wait_ge(s_dve, chain[0])

            for s_, n in ((s_bn, 1), (s_ag, 1), (s_var, 1), (s_xhat, 1), (s_prod, 4), (s_acc, 1),
                          (s_w3, 2), (s_r3, 1), (s_v3, 1), (s_m3, 2)):
                dve.sem_inc(s_, 2 * n)
            for s_, n in ((s_lo2[LEFT], 1), (s_lo2[RIGHT], 1), (s_rstd, 1), (s_xhp, 1), (s_lo, 2), (s_rc, 1), (s_g3, 2), (s_ra, 1), (s_n3, 2), (s_k3, 1), (s_q3, 1), (s_qs, 1)):
                dve.sem_inc(s_, 2 * n)

            def statistics(i, b):
                s = 2 * i + b
                dve.wait_ge(s_xin[b], 16 * (i + 1))
                for t in range(2 * TILES):
                    last = nc.vector.bn_stats(bn[:, b, t], xin[:, b, t])
                last.then_inc(s_bn, 1)
                dve.wait_ge(s_bn, mark(1, s, 1))
                dve.wait_ge(s_xhp, mark(1, s - 2, 1))
                settle(dve, s_tick_dve)
                for t in range(2 * TILES):
                    last = nc.vector.bn_aggr(mv[:, b, t], bn[:, b, t])
                last.then_inc(s_ag, 1)
                dve.wait_ge(s_ag, mark(1, s, 1))
                nc.vector.tensor_scalar(vv[:, b], mv[:, b, :, 1], 1.0 + EPS, EPS_CONV_IN * EPS,
                                        ALU.mult, ALU.add).then_inc(s_var, 1)

            def centre(i, b):
                dve.wait_ge(s_rstd, mark(1, 2 * i + b, 1))
                dve.wait_ge(s_xt, mark(2, 2 * i + b - 2, 2))
                for t in range(CENTRED):
                    last = nc.vector.tensor_scalar(xhat[:, b, t], xin[:, b, t], mv[:, b, t, 0:1],
                                                   rs[:, b, t:t + 1], ALU.subtract, ALU.mult)
                last.then_inc(s_xhat, 1)

            def product(i, b, c, side):
                n = 2 * (2 * i + b) + c
                stored, bank, col, sig, dst = ((s_lst, 3, BL, sig_l, left_sb), (s_rst, 5, BR, sig_r, right_sb))[side]
                dve.wait_ge(stored[b], 16 * i)
                dve.wait_ge(s_sig, chunk_mark(3, n, side + 1))
                dve.wait_ge(s_proj, chunk_mark(5, n, 2 * side + 2))
                nc.vector.scalar_tensor_tensor(out=dst[:, b, CHUNK * c:CHUNK * (c + 1)], in0=ps[bank][:, :],
                                               scalar=cols[:, col:col + 1], in1=sig[:, c], op0=ALU.add,
                                               op1=ALU.mult).then_inc(s_prod, 1)

            def stage1(i):
                for b in range(2):
                    if in_range(i, b, 2, STEPS):
                        centre(*shifted(i, b, 2))
                    product(i, b, 0, 0)
                    product(i, b, 0, 1)
                    if in_range(i, b, 3, STEPS):
                        statistics(*shifted(i, b, 3))
                    product(i, b, 1, 0)
                    product(i, b, 1, 1)

            statistics(0, 0)
            centre(0, 0)
            statistics(0, 1)
            centre(0, 1)
            statistics(1, 0)

            dve.wait_ge(s_const, 16 * N_CONST)
            dve.wait_ge(s_gtp, 1)
            nc.vector.tensor_copy(gate_t[:, :], ps[7][:, 0:EXPERTS]).then_inc(s_setup, 1)
            link(nc.vector.tensor_copy(w_parts[:, HI], wcat))
            nc.vector.tensor_tensor(w_parts[:, LO], wcat, w_parts[:, HI], ALU.subtract).then_inc(s_setup, 1)
            nc.vector.memset(sum1[:, :, :], 0.0)
            nc.vector.memset(sum2[:, :, :], 0.0)

            pairs(dve, STEPS, stage1)

            dve.wait_ge(s_const2, 16 * N_CONST2)
            dve.wait_ge(s_pool0, N_POOL0)
            for q in range(2):
                link(nc.vector.tensor_scalar(exact[:, q, :], exact[:, q, :], rowsign[:, q:q + 1], None, ALU.mult))
            link(nc.vector.tensor_copy(exact_p[:, 0], exact[:, :, :]))
            link(nc.vector.tensor_tensor(exact_lo[:, :, :], exact[:, :, :], exact_p[:, 0], ALU.subtract))
            link(nc.vector.tensor_copy(exact_p[:, 1], exact_lo[:, :, :]))
            link(nc.vector.tensor_tensor(exact_lo[:, :, :], exact_lo[:, :, :], exact_p[:, 1], ALU.subtract))
            nc.vector.tensor_copy(exact_p[:, 2], exact_lo[:, :, :]).then_inc(s_setup, 1)

            def low_half_left(i, b):
                dve.wait_ge(s_hi2, mark(2, 2 * i + b, 2))
                parts = lr_parts[LEFT]
                nc.vector.tensor_tensor(parts[:, LO, b], lch[:, b], parts[:, HI, b], ALU.subtract).then_inc(s_lo2[LEFT], 1)

            def stage2(i):
                for b in range(2):
                    d = 2 * i + b
                    if in_range(i, b, 1, DIM):
                        low_half_left(*shifted(i, b, 1))
                    dve.wait_ge(s_ev, mark(NT, d, NT))
                    dve.wait_ge(s_acc, mark(1, d - 1, 1))
                    nc.vector.tensor_tensor(sum1[:, :, :], sum1[:, :, :], mix[:, b], ALU.add)
                    nc.vector.tensor_tensor(sum2[:, :, :], sum2[:, :, :], mixsq[:, b], ALU.add).then_inc(s_acc, 1)

            low_half_left(0, 0)
            pairs(dve, DIM, stage2)

            dve.wait_ge(s_acc, mark(1, DIM - 1, 1))
            link(nc.vector.tensor_scalar(sum1[:, :, :], sum1[:, :, :], 1.0 / DIM, None, ALU.mult))
            link(nc.vector.tensor_tensor(newton, sum1, sum1, ALU.mult))
            link(nc.vector.scalar_tensor_tensor(out=sum2[:, :, :], in0=sum2[:, :, :], scalar=1.0 / DIM,
                                                in1=newton, op0=ALU.mult, op1=ALU.subtract))
            for t in range(NT):
                nc.vector.tensor_scalar(sum2[:, t], sum2[:, t], 0.0, EPS, ALU.max, ALU.add).then_inc(s_mom, 1)

            def split3(value, first):
                link(nc.vector.tensor_copy(split[:, first], value))
                link(nc.vector.tensor_tensor(value, value, split[:, first], ALU.subtract))
                link(nc.vector.tensor_copy(split[:, first + 1], value))
                link(nc.vector.tensor_tensor(value, value, split[:, first + 1], ALU.subtract))
                link(nc.vector.tensor_copy(split[:, first + 2], value))

            split3(sum1, 0)
            nc.vector.engine_nop().then_inc(s_split, 1)
            dve.wait_ge(s_sq, NT)
            link(nc.vector.reciprocal(rstd_map, rstd_map))
            link(nc.vector.tensor_tensor(newton, rstd_map, rstd_map, ALU.mult))
            link(nc.vector.tensor_tensor(newton, newton, sum2, ALU.mult))
            link(nc.vector.tensor_scalar(newton, newton, -0.5, 1.5, ALU.mult, ALU.add))
            nc.vector.tensor_tensor(rstd_map, rstd_map, newton, ALU.mult).then_inc(s_rmap, 1)
            dve.wait_ge(s_rmap, 1)
            link(nc.vector.tensor_tensor(sum2, sum2, rstd_map, ALU.mult))
            split3(sum2, PARTS)
            nc.vector.engine_nop().then_inc(s_split, 1)

            def weighted(i, b):
                for h in range(2):
                    dve.wait_ge(s_oin[b], 32 * (i + 1))
                    dve.wait_ge(s_c3, mark(2, 2 * i + b, h + 1))
                    dve.wait_ge(s_z3, mark(2, 2 * i + b - 2, h + 1))
                    nc.vector.scalar_tensor_tensor(out=gated[:, b, h], in0=ot[:, b, h], scalar=cols[:, ONA:ONA + 1],
                                                   in1=ps[h][:, :], op0=ALU.mult, op1=ALU.add).then_inc(s_w3, 1)

            def residual(i, b):
                s = 2 * i + b
                dve.wait_ge(s_rc, mark(1, s, 1))
                dve.wait_ge(s_x3[b], 16 * (i + 1))
                dve.wait_ge(s_ost[b], 16 * i)
                dve.wait_ge(s_y3, mark(2, s - 2, 2))
                dve.wait_ge(s_z3, mark(2, s, 1))
                for c in range(TILES):
                    last = nc.vector.scalar_tensor_tensor(out=summed[:, b, 0, c], in0=ps[2][:, c * P:(c + 1) * P],
                                                          scalar=rcol[:, b, c:c + 1], in1=xs[:, b, 0, c],
                                                          op0=ALU.mult, op1=ALU.add)
                last.then_inc(s_r3, 1)

            def statistics3(i, b, h):
                summed_by = (s_r3, s_ra)[h]
                dve.wait_ge(summed_by, mark(1, 2 * i + b, 1))
                for c in range(TILES):
                    last = nc.vector.bn_stats(bn[:, b, TILES * h + c], summed[:, b, h, c])
                if h:
                    last.then_inc(s_bn, 1)

            def aggregate3(i, b):
                s = 2 * i + b
                dve.wait_ge(s_bn, mark(1, STEPS + s, 1))
                dve.wait_ge(s_n3, mark(2, s - 2, 2))
                settle(dve, s_tick_dve)
                for t in range(2 * TILES):
                    last = nc.vector.bn_aggr(mv[:, b, t], bn[:, b, t])
                last.then_inc(s_ag, 1)

            def moments3(i, b):
                s = 2 * i + b
                dve.wait_ge(s_ag, mark(1, STEPS + s, 1))
                nc.vector.tensor_scalar(minus[:, b], mv[:, b, :, 0], -1.0, None, ALU.mult)
                nc.vector.tensor_scalar(vv[:, b], mv[:, b, :, 1], 1.0, EPS, ALU.mult, ALU.add).then_inc(s_v3, 1)

            def best_values(i, b):
                s = 2 * i + b
                dve.wait_ge(s_l3, mark(2, s, 2))
                dve.wait_ge(s_q3, mark(1, s - 2, 1))
                dve.wait_ge(s_k3, mark(1, s - 2, 1))
                settle(dve, s_tick_dve)
                nc.vector.max(mx[:, b], ps[6 + b][:, :]).then_inc(s_m3, 1)

            def best_places(i, b):
                s = 2 * i + b
                dve.wait_ge(s_m3, mark(2, s, 1))
                settle(dve, s_tick_dve)
                nc.vector.max_index(ix[:, b], mx[:, b], ps[6 + b][:, :]).then_inc(s_m3, 1)

            def stage3(i):
                for b in range(2):
                    if in_range(i, b, 1, STEPS):
                        weighted(*shifted(i, b, 1))
                    if in_range(i, b, -1, STEPS):
                        statistics3(*shifted(i, b, -1), 0)
                        statistics3(*shifted(i, b, -1), 1)
                        aggregate3(*shifted(i, b, -1))
                        moments3(*shifted(i, b, -1))
                    if in_range(i, b, 0, STEPS):
                        residual(i, b)
                    if in_range(i, b, -3, STEPS):
                        best_values(*shifted(i, b, -3))
                        best_places(*shifted(i, b, -3))

            weighted(0, 0)
            pairs(dve, STEPS, stage3, drain=2)

            dve.wait_ge(s_q3, mark(1, STEPS - 1, 1))
            dve.wait_ge(s_qs, mark(1, STEPS - 1, 1))
            flat = "p s k -> p (s k)"
            link(nc.vector.scalar_tensor_tensor(out=cidx[:, :, :], in0=cidx[:, :, :], scalar=half_off[:, :],
                                                in1=base[:, :, :], op0=ALU.add, op1=ALU.add))
            link(nc.vector.tensor_scalar(cand[:, :, :], cand[:, :, :], gb_col[:, :], None, ALU.add))
            link(nc.vector.max(pack[:, 0:TOP], cand[:, :, :].rearrange(flat)))
            nc.vector.tensor_scalar(negm[:, :], pack[:, 0:1], -1.0, None, ALU.mult).then_inc(s_nm, 1)
            link(nc.vector.max_index(posu[:, :], pack[:, 0:TOP], cand[:, :, :].rearrange(flat)))
            link(nc.vector.tensor_copy(posf[:, :], posu[:, :]))
            for k in range(TOP):
                link(nc.vector.scalar_tensor_tensor(out=junk[:, 0:STEPS * TOP], in0=place[:, :], scalar=posf[:, k:k + 1],
                                                      in1=cidx[:, :, :].rearrange(flat), op0=ALU.is_equal, op1=ALU.mult,
                                                      accum_out=pack[:, TOP + k:TOP + k + 1]))
            dve.wait_ge(s_we, 1)
            nc.vector.scalar_tensor_tensor(out=junk[:, 0:STEPS], in0=wexp[:, :], scalar=1.0, in1=csum[:, :],
                                           op0=ALU.mult, op1=ALU.mult,
                                           accum_out=pack[:, 2 * TOP:2 * TOP + 1]).then_inc(s_pack, 1)
            dve.wait_ge(s_pack, 1)
            nc.vector.tensor_copy(both[:, :, 0:TOP], pack[0:EXPERTS, 0:2 * TOP].rearrange("p (q k) -> p q k", q=2))
            nc.vector.tensor_copy(zsum[:, 0:1], pack[0:EXPERTS, 2 * TOP:2 * TOP + 1])
            dve.wait_ge(s_hi, 16)
            nc.vector.tensor_copy(both[:, :, TOP:2 * TOP], pack_hi[:, 0:2 * TOP].rearrange("p (q k) -> p q k", q=2))
            link(nc.vector.tensor_copy(zsum[:, 1:2], pack_hi[:, 2 * TOP:2 * TOP + 1]))
            def each(v):
                return v.rearrange("p (o k) -> p o k", o=1)

            def of(v):
                return v.rearrange("p (k o) -> p k o", o=1)

            square, eight = [EXPERTS, 2 * TOP, 2 * TOP], [EXPERTS, TOP, 2 * TOP]
            for q, (dst, op) in enumerate(((ahead, ALU.is_gt), (same, ALU.is_equal), (sooner, ALU.is_lt))):
                v = both[:, q // 2]
                last = nc.vector.tensor_tensor(dst, each(v).broadcast_to(square), of(v).broadcast_to(square), op)
            link(last)
            link(nc.vector.tensor_tensor(same, same, sooner, ALU.mult))
            link(nc.vector.tensor_tensor(ahead, ahead, same, ALU.add))
            link(nc.vector.tensor_reduce(rank[:, :], ahead, AXX, ALU.add))
            link(nc.vector.tensor_tensor(chosen, each(rank[:, :]).broadcast_to(eight),
                                         of(place[0:EXPERTS, 0:TOP]).broadcast_to(eight), ALU.is_equal))
            nc.vector.tensor_tensor(same[:, 0:TOP], chosen, each(both[:, 0]).broadcast_to(eight), ALU.mult)
            link(nc.vector.tensor_tensor(sooner[:, 0:TOP], chosen, each(both[:, 1]).broadcast_to(eight), ALU.mult))
            nc.vector.tensor_reduce(best[:, :], same[:, 0:TOP], AXX, ALU.add)
            link(nc.vector.tensor_reduce(pick[:, 0, :], sooner[:, 0:TOP], AXX, ALU.add))
            nc.vector.tensor_scalar(negbest[:, :], best[:, 0:1], -1.0, None, ALU.mult).then_inc(s_nm, 1)
            dve.wait_ge(s_we, 3)
            link(nc.vector.scalar_tensor_tensor(out=ztot[:, :], in0=zscale[:, :], scalar=1.0, in1=zsum[:, :],
                                                op0=ALU.mult, op1=ALU.mult, accum_out=negbest[:, :]))
            link(nc.vector.reciprocal(ztot[:, 0:1], negbest[:, :]))
            nc.vector.tensor_scalar(pick[:, 1, :], pick[:, 1, :], ztot[:, 0:1], None, ALU.mult).then_inc(s_pick, 1)
            dve.wait_ge(s_rows, 64)
            nc.vector.tensor_copy(rowidx[:, :], rowpick[:, 0, :]).then_inc(s_ri, 1)
            dve.wait_ge(s_gat, 16 * GROUPS)
            for g in range(GROUPS):
                last = nc.vector.bn_stats(bn[:, 0, g], xg[:, g])
            link(last)
            for g in range(GROUPS):
                last = nc.vector.bn_aggr(mv[:, 0, g], bn[:, 0, g])
            link(last)
            nc.vector.tensor_scalar(vv[:, 0, 0:GROUPS], mv[:, 0, 0:GROUPS, 1], 1.0, EPS, ALU.mult, ALU.add).then_inc(s_gvar, 1)
            dve.wait_ge(s_gr, 1)
            link(nc.vector.tensor_tensor(rw[:, :], rs[:, 0, 0:GROUPS], rowpick[:, 1, :], ALU.mult))
            for g in range(GROUPS):
                last = nc.vector.tensor_scalar(yg[:, g], xg[:, g], mv[:, 0, g, 0:1], rw[:, g:g + 1], ALU.subtract, ALU.mult)
            last.then_inc(s_yg, 1)
            dve.wait_ge(s_pool, 1)
            dve.wait_ge(s_clear, 2)
            nc.vector.tensor_copy(diagonal(win1), ps[0][:, 0:EXPERTS].rearrange("p (g j) -> p g j", g=BANDS)).then_inc(s_pl, 1)
            dve.wait_ge(s_all, 16)
            dve.wait_ge(s_pool0, N_POOL0 + 2)
            for g in range(GROUPS):
                at = PICKS - P - g * P
                link(nc.vector.scalar_tensor_tensor(out=junk[:, 0:PICKS], in0=allpick[:, :], scalar=rowpick[:, 0, g:g + 1],
                                                      in1=earlier[:, at:at + PICKS], op0=ALU.is_equal, op1=ALU.mult,
                                                      accum_out=seen[:, g:g + 1]))
            link(nc.vector.scalar_tensor_tensor(out=scatf[:, :], in0=seen[:, :], scalar=float(TOKENS),
                                                in1=rowpick[:, 0, :], op0=ALU.mult, op1=ALU.add))
            nc.vector.tensor_copy(scatidx[:, :], scatf[:, :])
            dve.wait_ge(s_prow, 16 * BANDS)
            for k in range(TOP):
                dst = wt if k == 0 else wtk
                link(nc.vector.tensor_scalar(dst[:, :], allpick[:, :], pick_row[:, 0, k:k + 1], pick_row[:, 1, k:k + 1],
                                             ALU.is_equal, ALU.mult))
                if k:
                    link(nc.vector.tensor_tensor(wt[:, :], wt[:, :], wtk[:, :], ALU.add))
            dve.wait_ge(s_b1, 16 * BANDS)
            dve.wait_ge(s_h1, WLOADS)
            nc.vector.tensor_tensor(hid, b1_row, ps[2][:, :], ALU.add).then_inc(s_pre, 1)
            dve.wait_ge(s_clear, 4)
            for c in range(HC):
                dve.wait_ge(s_ht, c + 1)
                nc.vector.tensor_copy(diagonal(win2[c]), ps[HT_BANK[c]][:, 0:P].rearrange(
                    "p (g w) -> p g w", g=BANDS)[:, :, 0:SIDE]).then_inc(s_win, 1)
            dve.wait_ge(s_h2, 1)
            nc.vector.tensor_tensor(eo[:, :], b2_row[:, :], ps[1][:, 0:DIM], ALU.add).then_inc(s_eo, 1)
            dve.wait_ge(s_del, 1)
            for g in range(GROUPS):
                nc.vector.tensor_tensor(yg[:, g], xg[:, g], ps[5][:, g * DIM:(g + 1) * DIM], ALU.add).then_inc(s_new, 1)

        @block.tensor
        def _(pe):
            for s_, n in ((s_xt, 2), (s_proj, 10), (s_mix, NT), (s_c3, 2), (s_z3, 2), (s_t3, 2), (s_l3, 2)):
                pe.sem_inc(s_, 2 * n)
            TERMS = ((LO, HI), (HI, LO), (HI, HI))
            def transposes(i, b, c):
                s, n = 2 * i + b, 2 * (2 * i + b) + c
                pe.wait_ge(s_xhat, mark(1, s, 1))
                if c:
                    pe.wait_ge(s_xhp, mark(1, s, 1))
                pe.wait_ge(s_xn, chunk_mark(1, n - 2, 1))
                for t in range(TILES):
                    last = nc.tensor.transpose(ps[c][:, t * P:(t + 1) * P], xhat[:, b, TILES * c + t], ident[:, :])
                last.then_inc(s_xt, 1)

            def projections(i, b, c):
                n = 2 * (2 * i + b) + c
                pe.wait_ge(s_lo, chunk_mark(1, n, 1))
                free = ((s_sig, 3, 1), (s_prod, 2, 1), (s_sig, 3, 2), (s_prod, 2, 2), (s_sig, 3, 3))
                for k, (reader, per, at) in enumerate(free):
                    pe.wait_ge(reader, chunk_mark(per, n - 1, at))
                    for wq, xq in TERMS:
                        last = nc.tensor.matmul(ps[2 + k][:, :], w_parts[:, wq, k], x_parts[:, xq, b, c],
                                                start=((wq, xq) == TERMS[0]), stop=((wq, xq) == TERMS[-1]))
                    last.then_inc(s_proj, 1)

            def stage1(i):
                for b in range(2):
                    for c in range(2):
                        if in_range(i, b, 1, STEPS):
                            transposes(*shifted(i, b, 1), c)
                        projections(i, b, c)

            pe.wait_ge(s_pool0, N_POOL0)
            transposes(0, 0, 0)
            transposes(0, 0, 1)
            pe.wait_ge(s_const, 16 * N_CONST)
            nc.tensor.transpose(ps[7][:, 0:EXPERTS], gate_nat[:, :], ident[0:EXPERTS, 0:EXPERTS]).then_inc(s_gtp, 1)
            pe.wait_ge(s_setup, 2)
            pairs(pe, STEPS, stage1)

            pe.wait_ge(s_xn, mark(2, STEPS - 1, 2))
            pe.wait_ge(s_sig, mark(6, STEPS - 1, 6))
            pe.wait_ge(s_prod, mark(4, STEPS - 1, 4))

            def stage2(i):
                for b in range(2):
                    d = 2 * i + b
                    terms = ((HI, HI), (HI, LO), (LO, HI))
                    for t in range(NT):
                        pe.wait_ge(s_ev, mark(NT, d - 2, t + 1))
                        for rq, lq in terms:
                            if t == 0:
                                ready = {(HI, HI): (s_hi2, 2, 2), (HI, LO): (s_lo2[LEFT], 1, 1),
                                         (LO, HI): (s_lo2[RIGHT], 1, 1)}[rq, lq]
                                pe.wait_ge(ready[0], mark(ready[1], d, ready[2]))
                            for k in range(NT):
                                last = nc.tensor.matmul(
                                    ps[NT * b + t][:, 0:GRID], lr_parts[RIGHT][:, rq, b, k, t * P:(t + 1) * P],
                                    lr_parts[LEFT][:, lq, b, k], start=((rq, lq) == terms[0] and k == 0),
                                    stop=((rq, lq) == terms[-1] and k == NT - 1))
                        last.then_inc(s_mix, 1)

            pairs(pe, DIM, stage2)

            pe.wait_ge(s_ev, mark(NT, DIM - 1, NT))
            pe.wait_ge(s_rmap, 1)
            for t in range(NT):
                for c in range(NT):
                    n = t * NT + c
                    if n >= 2:
                        pe.wait_ge(s_rtc, n - 1)
                    nc.tensor.transpose(ps[n % 2][:, 0:P], rstd_map[:, t, c * P:(c + 1) * P], ident[:, :]).then_inc(s_rtp, 1)

            def outer(i, b):
                s = 2 * i + b
                pe.wait_ge(s_sin[b], 16 * (i + 1))
                for h in range(2):
                    pe.wait_ge(s_w3, mark(2, s - 1, h + 1))
                    nc.tensor.matmul(ps[h][:, :], coef[:, 0, :], statrow[:, b, h, :], start=True, stop=True).then_inc(s_c3, 1)

            def project(i, b):
                s = 2 * i + b
                for h in range(2):
                    pe.wait_ge(s_g3, mark(2, s, h + 1))
                    pe.wait_ge((s_r3, s_zr)[h], mark(1, s - 1, 1))
                    for c in range(TILES):
                        tok = slice(c * P, (c + 1) * P)
                        nc.tensor.matmul(ps[2 + h][:, tok], gated[:, b, h, tok], wo_sb[:, :], start=True, stop=False)
                        last = nc.tensor.matmul(ps[2 + h][:, tok], statrow[:, b, h, tok], coef[:, 1, :], start=False, stop=True)
                    last.then_inc(s_z3, 1)

            def transposes3(i, b):
                s = 2 * i + b
                for h in range(2):
                    pe.wait_ge(s_y3, mark(2, s, h + 1))
                    pe.wait_ge(s_p3, mark(2, s - 1, h + 1))
                    for c in range(TILES):
                        last = nc.tensor.transpose(ps[4 + h][:, c * P:(c + 1) * P], ys[:, b, h, c], ident[:, :])
                    last.then_inc(s_t3, 1)

            def logits(i, b):
                s = 2 * i + b
                pe.wait_ge(s_e3, mark(1, s - 2, 1))
                for h in range(2):
                    pe.wait_ge(s_p3, mark(2, s, h + 1))
                    nc.tensor.matmul(ps[6 + b][EXPERTS * h:EXPERTS * (h + 1), :], gate_t[:, :], yt[:, b, h],
                                     start=True, stop=True).then_inc(s_l3, 1)

            def stage3(i):
                for b in range(2):
                    if in_range(i, b, 1, STEPS):
                        outer(*shifted(i, b, 1))
                    if in_range(i, b, 0, STEPS):
                        project(i, b)
                    if in_range(i, b, -3, STEPS):
                        logits(*shifted(i, b, -3))
                    if in_range(i, b, -2, STEPS):
                        transposes3(*shifted(i, b, -2))

            pe.wait_ge(s_rtc, NT * NT)
            pe.wait_ge(s_coef, 16 * PARTS)
            pe.wait_ge(s_setup, 3)
            outer(0, 0)
            pairs(pe, STEPS, stage3, drain=2)

            pe.wait_ge(s_r3, mark(1, STEPS - 1, 1))
            pe.wait_ge(s_zr, mark(1, STEPS - 1, 1))
            pe.wait_ge(s_p3, mark(2, STEPS - 1, 2))
            pe.wait_ge(s_e3, mark(1, STEPS - 1, 1))
            pe.wait_ge(s_yg, 1)
            for g in range(GROUPS):
                last = nc.tensor.matmul(ps[0][:, 0:EXPERTS], yg[:, g], sel[:, :], start=(g == 0), stop=(g == GROUPS - 1))
            last.then_inc(s_pool, 1)
            pe.wait_ge(s_pl, 1)
            pe.wait_ge(s_w1, 16 * SIDE)
            order = (WLOADS - 1,) + tuple(range(WLOADS - 1))
            for n in order:
                for j in (2 * n, 2 * n + 1):
                    for g in range(BANDS):
                        last = nc.tensor.matmul(ps[2][BAND * g:BAND * (g + 1), :], win1[:, g, BAND * j:BAND * (j + 1)],
                                                w1_sb[:, j, g], start=(j == 2 * order[0]), stop=(j == 2 * order[-1] + 1))
                last.then_inc(s_h1, 1)
            pe.wait_ge(s_hid, 1)
            for c in range(HC):
                nc.tensor.transpose(ps[HT_BANK[c]][:, 0:P], hid[:, c::HC], ident[:, :]).then_inc(s_ht, 1)
            pe.wait_ge(s_win, HC)
            for n in range(WLOADS):
                pe.wait_ge(s_w2[n], 32)
                for j in (2 * n, 2 * n + 1):
                    w2 = w2_in_work[:, j] if n == 0 else w2_in_w1[:, j - 2]
                    for c in range(HC):
                        for g in range(BANDS):
                            last = nc.tensor.matmul(ps[1][BAND * g:BAND * (g + 1), 0:DIM], win2[c][:, g, BAND * j:BAND * (j + 1)],
                                                    w2[:, g, c], start=(j == 0 and c == 0), stop=(j == SIDE - 1 and c == HC - 1))
            last.then_inc(s_h2, 1)
            pe.wait_ge(s_eo, 1)
            for g in range(GROUPS):
                last = nc.tensor.matmul(ps[5][:, g * DIM:(g + 1) * DIM], wt[:, g * P:(g + 1) * P], eo[:, :], start=True, stop=True)
            last.then_inc(s_del, 1)


_INS = ["x", "L0_conv_norm_a", "L0_conv_norm_b", "L0_conv_Wl", "L0_conv_bl", "L0_conv_Wr", "L0_conv_br",
        "L0_conv_Wlg", "L0_conv_blg", "L0_conv_Wrg", "L0_conv_brg", "L0_conv_Wog", "L0_conv_bog",
        "L0_conv_on_a", "L0_conv_on_b", "L0_conv_Wo", "L0_conv_bo", "L0_ffn_gate_w", "L0_ffn_gate_b",
        "L0_ffn_weight1", "L0_ffn_weight2"]


def kernel(**inputs):
    import concourse.bacc as bacc
    from concourse.bass_utils import run_bass_kernel_spmd

    nc = bacc.Bacc("TRN2", target_bir_lowering=False, num_devices=1)
    arrays, args = {}, []
    for name in _INS:
        a = np.ascontiguousarray(inputs[name])
        arrays[f"in_{name}_dram"] = a
        args.append(nc.dram_tensor(f"in_{name}_dram", a.shape, mybir.dt.from_np(a.dtype), kind="ExternalInput").ap())
    result = nc.dram_tensor("out_0_dram", arrays["in_x_dram"].shape, FP32, kind="ExternalOutput").ap()
    build(nc, *args, result)
    r = run_bass_kernel_spmd(nc, [arrays], core_ids=[0])
    return r.results[0]["out_0_dram"]
```
